# Optimizing a Trainium2 kernel written in Bass

```python
import numpy as np
import jax
import jax.numpy as jnp

def _softmax(x, axis=-1):
    return jax.nn.softmax(x, axis=axis)

def _gelu(x):
    return jax.nn.gelu(x, approximate=True)

def _silu(x):
    return jax.nn.silu(x)

def _sigmoid(x):
    return jax.nn.sigmoid(x)

def _layernorm(x, axis=-1, eps=1e-05):
    m = jnp.mean(x, axis=axis, keepdims=True)
    v = jnp.var(x, axis=axis, keepdims=True)
    return (x - m) / jnp.sqrt(v + eps)

def _scatter_add(tgt, idx, src, axis=0):
    return tgt.at[idx].add(src)

def _segment_sum(src, seg, n):
    return jax.ops.segment_sum(src, seg, n)
kernel_name = 'mk_seq_preln_d2_jaxref_r8_ed0e21'

def setup_inputs(seed: int=0):
    np.random.seed(seed)
    _w = jnp.asarray

    def _L0_attn_setup():
        import jax, jax.numpy as jnp
        import numpy as np
        HEAD = 64

        def wkv6(r, k, v, w, u):
            B, T, C = r.shape
            N = C // HEAD
            shp = lambda a: a.reshape(B, T, N, HEAD).transpose(1, 0, 2, 3)
            rT, kT, vT = (shp(r), shp(k), shp(v))
            dT = jnp.exp(shp(w))
            uu = u[None]

            def step(S, inp):
                rt, kt, vt, dt = inp
                kv = vt[..., :, None] * kt[..., None, :]
                yt = jnp.einsum('bnj,bnij->bni', rt, S + uu[..., None, :] * kv)
                S = S * dt[..., None, :] + kv
                return (S, yt)
            S0 = jnp.zeros((B, N, HEAD, HEAD), r.dtype)
            _, ys = jax.lax.scan(step, S0, (rT, kT, vT, dT))
            return ys.transpose(1, 0, 2, 3).reshape(B, T, C)
        key = jax.random.key(seed)
        B, T, C = (2, 128, 128)
        N = C // HEAD
        depth, layer_id = (24, 12)
        r01 = layer_id / (depth - 1)
        r1a0 = 1.0 - layer_id / depth
        ddd = np.arange(C, dtype=np.float64) / C
        miu_x = (1.0 - ddd ** (0.6 * r1a0 ** 0.9)).reshape(1, 1, C).astype(np.float32)
        lam = np.stack([1.0 - ddd ** (0.9 * r1a0), 1.0 - ddd ** (0.9 * r1a0) - 0.4 * r01, 1.0 - ddd ** (0.4 * r1a0) - 0.6 * r01, 1.0 - ddd ** (0.2 * r1a0), 1.0 - ddd ** (0.2 * r1a0)]).reshape(5, 1, 1, C).astype(np.float32)
        n = np.arange(C, dtype=np.float64)
        td_miu = (-6.0 + 5.5 * (n / (C - 1)) ** (0.85 + 1.0 * r01 ** 0.5)).reshape(1, 1, C).astype(np.float32)
        zigzag = ((n + 1) % 3 - 1) * 0.1
        u = (r01 * (2.5 - n / (C - 1)) + zigzag).reshape(N, HEAD).astype(np.float32)
        ks = jax.random.split(key, 12)
        unif = lambda k, shape, s: jax.random.uniform(k, shape, jnp.float32, -s, s)
        x = jax.random.normal(ks[0], (B, T, C), jnp.float32)
        return {'x': x, 'miu_x': jnp.asarray(miu_x), 'lam': jnp.asarray(lam), 'A': unif(ks[1], (C, 160), 0.01), 'Bp': unif(ks[2], (5, 32, C), 0.01), 'td_miu': jnp.asarray(td_miu), 'tdA': unif(ks[3], (C, 64), 0.01), 'tdB': unif(ks[4], (64, C), 0.01), 'u': jnp.asarray(u), 'Wk': unif(ks[5], (C, C), 0.05 / C ** 0.5), 'Wv': unif(ks[6], (C, C), 0.5 / C ** 0.5), 'Wr': unif(ks[7], (C, C), 0.5 / C ** 0.5), 'Wo': unif(ks[8], (C, C), 0.5 / C ** 0.5), 'Wg1': unif(ks[9], (C, 160), 0.01), 'Wg2': unif(ks[10], (160, C), 0.01), 'gamma': jnp.ones((C,), jnp.float32), 'beta': jnp.zeros((C,), jnp.float32)}
    _L0_attn_in = _L0_attn_setup()

    def _L0_ffn_setup():
        import jax, jax.numpy as jnp
        import numpy as np
        D, H, O, E, K = (128, 256, 128, 8, 2)
        B, S = (4, 128)
        key = jax.random.key(seed)
        ks = jax.random.split(key, 8)
        scale = 0.02
        return {'hidden_states': jax.random.normal(ks[0], (B, S, D), jnp.float32), 'router_w': jax.random.normal(ks[1], (E, D), jnp.float32) * scale, 'sg': jax.random.normal(ks[2], (H, D), jnp.float32) * scale, 'su': jax.random.normal(ks[3], (H, D), jnp.float32) * scale, 'sd': jax.random.normal(ks[4], (O, H), jnp.float32) * scale, 'eg': jax.random.normal(ks[5], (E, H, D), jnp.float32) * scale, 'eu': jax.random.normal(ks[6], (E, H, D), jnp.float32) * scale, 'ed': jax.random.normal(ks[7], (E, O, H), jnp.float32) * scale}
    _L0_ffn_in = _L0_ffn_setup()

    def _L1_attn_setup():
        import jax, jax.numpy as jnp
        import numpy as np
        from jax import lax
        B, T, H = (4, 256, 128)
        HU = 4 * H
        LAYERS, INDEX = (12, 0)
        K_CLAMP, K_EPS = (60.0, 1e-08)
        LN_EPS = 1e-05

        def _ln(x, g, b):
            m = jnp.mean(x, -1, keepdims=True)
            v = jnp.mean((x - m) ** 2, -1, keepdims=True)
            return (x - m) / jnp.sqrt(v + LN_EPS) * g + b

        def _shift(x):
            return jnp.pad(x[:, :-1], ((0, 0), (1, 0), (0, 0)))

        def _wkv(k, kv, decay, first):

            def step(carry, inp):
                sk, skv = carry
                kt, kvt = inp
                out = (first * kt + sk, first * kvt + skv)
                return ((kt + decay * sk, kvt + decay * skv), out)
            b = k.shape[0]
            init = (jnp.zeros((b, k.shape[2]), k.dtype), jnp.zeros((b, k.shape[2]), k.dtype))
            _, (wk, wkv) = lax.scan(step, init, (jnp.swapaxes(k, 0, 1), jnp.swapaxes(kv, 0, 1)))
            return (jnp.swapaxes(wk, 0, 1), jnp.swapaxes(wkv, 0, 1))
        key = jax.random.key(seed)
        ks = jax.random.split(key, 9)
        s = 0.02
        tr01 = INDEX / (LAYERS - 1)
        tr1pz = 1.0 - INDEX / LAYERS
        i_h = np.arange(H, dtype=np.float64) / H
        i_hu = np.arange(HU, dtype=np.float64)
        decay_speed = -5.0 + 8.0 * (i_hu / (HU - 1)) ** (0.7 + 1.3 * tr01)
        zigzag = ((np.arange(HU) + 1) % 3 - 1) * 0.5
        time_first = np.log(0.3) + zigzag
        f32 = lambda a: jnp.asarray(a, jnp.float32)
        return {'x': jax.random.normal(ks[0], (B, T, H), jnp.float32), 'ln0_g': jnp.ones((H,), jnp.float32), 'ln0_b': jnp.zeros((H,), jnp.float32), 'pre_g': jnp.ones((H,), jnp.float32), 'pre_b': jnp.zeros((H,), jnp.float32), 'post_g': jnp.ones((H,), jnp.float32), 'post_b': jnp.zeros((H,), jnp.float32), 'tm_decay': f32(decay_speed), 'tm_first': f32(time_first), 'tm_mix_k': f32(i_h ** tr1pz), 'tm_mix_v': f32(i_h ** tr1pz + 0.3 * tr01), 'tm_mix_r': f32(i_h ** (0.5 * tr1pz)), 'tm_Wk': jax.random.normal(ks[1], (H, HU), jnp.float32) * s, 'tm_Wv': jax.random.normal(ks[2], (H, HU), jnp.float32) * s, 'tm_Wr': jax.random.normal(ks[3], (H, HU), jnp.float32) * s, 'tm_Wo': jax.random.normal(ks[4], (HU, H), jnp.float32) * s, 'cm_mix_k': f32(i_h ** tr1pz), 'cm_mix_r': f32(i_h ** tr1pz), 'cm_Wk': jax.random.normal(ks[5], (H, HU), jnp.float32) * s, 'cm_Wv': jax.random.normal(ks[6], (HU, H), jnp.float32) * s, 'cm_Wr': jax.random.normal(ks[7], (H, H), jnp.float32) * s}
    _L1_attn_in = _L1_attn_setup()

    def _L1_ffn_setup():
        import jax, jax.numpy as jnp
        import numpy as np
        B, C, D = (2, 256, 128)
        I = 256
        E, K = (8, 2)
        CF = 1.25
        key = jax.random.key(seed)
        k1, k2, k3, k4 = jax.random.split(key, 4)
        scale = 0.02
        return {'hidden_states': jax.random.normal(k1, (B, C, D), jnp.float32), 'Wg': jax.random.normal(k2, (E, D), jnp.float32) * scale, 'W1': jax.random.normal(k3, (E, D, 2 * I), jnp.float32) * scale, 'W2': jax.random.normal(k4, (E, I, D), jnp.float32) * scale}
    _L1_ffn_in = _L1_ffn_setup()
    _d = {'L0_attn_x': _L0_attn_in['x'], 'L0_attn_miu_x': _L0_attn_in['miu_x'], 'L0_attn_lam': _L0_attn_in['lam'], 'L0_attn_A': _L0_attn_in['A'], 'L0_attn_Bp': _L0_attn_in['Bp'], 'L0_attn_td_miu': _L0_attn_in['td_miu'], 'L0_attn_tdA': _L0_attn_in['tdA'], 'L0_attn_tdB': _L0_attn_in['tdB'], 'L0_attn_u': _L0_attn_in['u'], 'L0_attn_Wk': _L0_attn_in['Wk'], 'L0_attn_Wv': _L0_attn_in['Wv'], 'L0_attn_Wr': _L0_attn_in['Wr'], 'L0_attn_Wo': _L0_attn_in['Wo'], 'L0_attn_Wg1': _L0_attn_in['Wg1'], 'L0_attn_Wg2': _L0_attn_in['Wg2'], 'L0_attn_gamma': _L0_attn_in['gamma'], 'L0_attn_beta': _L0_attn_in['beta'], 'L0_ffn_router_w': _L0_ffn_in['router_w'], 'L0_ffn_sg': _L0_ffn_in['sg'], 'L0_ffn_su': _L0_ffn_in['su'], 'L0_ffn_sd': _L0_ffn_in['sd'], 'L0_ffn_eg': _L0_ffn_in['eg'], 'L0_ffn_eu': _L0_ffn_in['eu'], 'L0_ffn_ed': _L0_ffn_in['ed'], 'L1_attn_ln0_g': _L1_attn_in['ln0_g'], 'L1_attn_ln0_b': _L1_attn_in['ln0_b'], 'L1_attn_pre_g': _L1_attn_in['pre_g'], 'L1_attn_pre_b': _L1_attn_in['pre_b'], 'L1_attn_post_g': _L1_attn_in['post_g'], 'L1_attn_post_b': _L1_attn_in['post_b'], 'L1_attn_tm_decay': _L1_attn_in['tm_decay'], 'L1_attn_tm_first': _L1_attn_in['tm_first'], 'L1_attn_tm_mix_k': _L1_attn_in['tm_mix_k'], 'L1_attn_tm_mix_v': _L1_attn_in['tm_mix_v'], 'L1_attn_tm_mix_r': _L1_attn_in['tm_mix_r'], 'L1_attn_tm_Wk': _L1_attn_in['tm_Wk'], 'L1_attn_tm_Wv': _L1_attn_in['tm_Wv'], 'L1_attn_tm_Wr': _L1_attn_in['tm_Wr'], 'L1_attn_tm_Wo': _L1_attn_in['tm_Wo'], 'L1_attn_cm_mix_k': _L1_attn_in['cm_mix_k'], 'L1_attn_cm_mix_r': _L1_attn_in['cm_mix_r'], 'L1_attn_cm_Wk': _L1_attn_in['cm_Wk'], 'L1_attn_cm_Wv': _L1_attn_in['cm_Wv'], 'L1_attn_cm_Wr': _L1_attn_in['cm_Wr'], 'L1_ffn_Wg': _L1_ffn_in['Wg'], 'L1_ffn_W1': _L1_ffn_in['W1'], 'L1_ffn_W2': _L1_ffn_in['W2']}
    _x0 = _d['L0_attn_x']
    _d['L0_attn_x'] = jax.random.normal(jax.random.fold_in(jax.random.key(seed), 1), (8, 512, 128), dtype=_x0.dtype)
    del _x0
    return _d

def reference(L0_attn_x, L0_attn_miu_x, L0_attn_lam, L0_attn_A, L0_attn_Bp, L0_attn_td_miu, L0_attn_tdA, L0_attn_tdB, L0_attn_u, L0_attn_Wk, L0_attn_Wv, L0_attn_Wr, L0_attn_Wo, L0_attn_Wg1, L0_attn_Wg2, L0_attn_gamma, L0_attn_beta, L0_ffn_router_w, L0_ffn_sg, L0_ffn_su, L0_ffn_sd, L0_ffn_eg, L0_ffn_eu, L0_ffn_ed, L1_attn_ln0_g, L1_attn_ln0_b, L1_attn_pre_g, L1_attn_pre_b, L1_attn_post_g, L1_attn_post_b, L1_attn_tm_decay, L1_attn_tm_first, L1_attn_tm_mix_k, L1_attn_tm_mix_v, L1_attn_tm_mix_r, L1_attn_tm_Wk, L1_attn_tm_Wv, L1_attn_tm_Wr, L1_attn_tm_Wo, L1_attn_cm_mix_k, L1_attn_cm_mix_r, L1_attn_cm_Wk, L1_attn_cm_Wv, L1_attn_cm_Wr, L1_ffn_Wg, L1_ffn_W1, L1_ffn_W2):

    def _L0_attn_ref(x, miu_x, lam, A, Bp, td_miu, tdA, tdB, u, Wk, Wv, Wr, Wo, Wg1, Wg2, gamma, beta):
        import jax, jax.numpy as jnp
        import numpy as np
        HEAD = 64

        def wkv6(r, k, v, w, u):
            B, T, C = r.shape
            N = C // HEAD
            shp = lambda a: a.reshape(B, T, N, HEAD).transpose(1, 0, 2, 3)
            rT, kT, vT = (shp(r), shp(k), shp(v))
            dT = jnp.exp(shp(w))
            uu = u[None]

            def step(S, inp):
                rt, kt, vt, dt = inp
                kv = vt[..., :, None] * kt[..., None, :]
                yt = jnp.einsum('bnj,bnij->bni', rt, S + uu[..., None, :] * kv)
                S = S * dt[..., None, :] + kv
                return (S, yt)
            S0 = jnp.zeros((B, N, HEAD, HEAD), r.dtype)
            _, ys = jax.lax.scan(step, S0, (rT, kT, vT, dT))
            return ys.transpose(1, 0, 2, 3).reshape(B, T, C)
        B, T, C = x.shape
        N = C // HEAD
        x_last = jnp.concatenate([jnp.zeros_like(x[:, :1]), x[:, :-1]], axis=1)
        b_a = x_last - x
        xx = x + b_a * miu_x
        h = jnp.tanh(xx @ A).reshape(5, B * T, 32)
        miu = jnp.einsum('smk,skc->smc', h, Bp).reshape(5, B, T, C) + lam
        x5 = x[None] + b_a[None] * miu
        w_in, k_in, v_in, r_in, g_in = (x5[0], x5[1], x5[2], x5[3], x5[4])
        w = td_miu + jnp.tanh(w_in @ tdA) @ tdB
        k = k_in @ Wk.T * jnp.exp(jnp.minimum(w, 0.0))
        v = v_in @ Wv.T
        r = r_in @ Wr.T
        g = jnp.tanh(g_in @ Wg1) @ Wg2
        y = wkv6(r, k, v, w, u)
        yh = y.reshape(B, T, N, HEAD)
        mean = yh.mean(-1, keepdims=True)
        var = yh.var(-1, keepdims=True)
        yn = (yh - mean) / jnp.sqrt(var + 1e-05 * N)
        yn = yn.reshape(B, T, C) * gamma + beta
        return yn * g @ Wo.T

    def _L0_ffn_ref(hidden_states, router_w, sg, su, sd, eg, eu, ed):
        import jax, jax.numpy as jnp
        import numpy as np
        D, H, O, E, K = (128, 256, 128, 8, 2)
        B, S = (4, 128)
        b, s, d = hidden_states.shape
        shared_out = jnp.einsum('bsh,oh->bso', jax.nn.silu(jnp.einsum('bsd,hd->bsh', hidden_states, sg)) * jnp.einsum('bsd,hd->bsh', hidden_states, su), sd)
        flat = hidden_states.reshape(-1, d)
        T = flat.shape[0]
        logits = flat @ router_w.T
        probs = jax.nn.softmax(logits.astype(jnp.float32), axis=-1)
        topk_w, topk_idx = jax.lax.top_k(probs, K)
        topk_w = topk_w / jnp.sum(topk_w, axis=-1, keepdims=True)
        topk_w = topk_w.astype(hidden_states.dtype)
        combine = jnp.zeros((T, probs.shape[-1]), hidden_states.dtype)
        combine = combine.at[jnp.arange(T)[:, None], topk_idx].add(topk_w)
        gate = jnp.einsum('td,ehd->teh', flat, eg)
        up = jnp.einsum('td,ehd->teh', flat, eu)
        eout = jnp.einsum('teh,eoh->teo', jax.nn.silu(gate) * up, ed)
        routed = jnp.einsum('teo,te->to', eout, combine)
        return shared_out + routed.reshape(b, s, -1)

    def _L1_attn_ref(x, ln0_g, ln0_b, pre_g, pre_b, post_g, post_b, tm_decay, tm_first, tm_mix_k, tm_mix_v, tm_mix_r, tm_Wk, tm_Wv, tm_Wr, tm_Wo, cm_mix_k, cm_mix_r, cm_Wk, cm_Wv, cm_Wr):
        import jax, jax.numpy as jnp
        import numpy as np
        from jax import lax
        B, T, H = (4, 256, 128)
        HU = 4 * H
        LAYERS, INDEX = (12, 0)
        K_CLAMP, K_EPS = (60.0, 1e-08)
        LN_EPS = 1e-05

        def _ln(x, g, b):
            m = jnp.mean(x, -1, keepdims=True)
            v = jnp.mean((x - m) ** 2, -1, keepdims=True)
            return (x - m) / jnp.sqrt(v + LN_EPS) * g + b

        def _shift(x):
            return jnp.pad(x[:, :-1], ((0, 0), (1, 0), (0, 0)))

        def _wkv(k, kv, decay, first):

            def step(carry, inp):
                sk, skv = carry
                kt, kvt = inp
                out = (first * kt + sk, first * kvt + skv)
                return ((kt + decay * sk, kvt + decay * skv), out)
            b = k.shape[0]
            init = (jnp.zeros((b, k.shape[2]), k.dtype), jnp.zeros((b, k.shape[2]), k.dtype))
            _, (wk, wkv) = lax.scan(step, init, (jnp.swapaxes(k, 0, 1), jnp.swapaxes(kv, 0, 1)))
            return (jnp.swapaxes(wk, 0, 1), jnp.swapaxes(wkv, 0, 1))
        if INDEX == 0:
            x = _ln(x, ln0_g, ln0_b)
        xn = _ln(x, pre_g, pre_b)
        xx = _shift(xn)
        xk = xn * tm_mix_k + xx * (1.0 - tm_mix_k)
        xv = xn * tm_mix_v + xx * (1.0 - tm_mix_v)
        xr = xn * tm_mix_r + xx * (1.0 - tm_mix_r)
        k = jnp.exp(jnp.minimum(xk @ tm_Wk, K_CLAMP))
        v = xv @ tm_Wv
        r = xr @ tm_Wr
        kv = k * v
        decay = jnp.exp(-jnp.exp(tm_decay))
        first = jnp.exp(tm_first)
        wk, wkv = _wkv(k, kv, decay, first)
        rwkv = jax.nn.sigmoid(r) * (wkv / (wk + K_EPS))
        x = x + rwkv @ tm_Wo
        xn = _ln(x, post_g, post_b)
        xx = _shift(xn)
        xk = xn * cm_mix_k + xx * (1.0 - cm_mix_k)
        xr = xn * cm_mix_r + xx * (1.0 - cm_mix_r)
        kv = jax.nn.silu(xk @ cm_Wk) @ cm_Wv
        x = x + (jax.nn.sigmoid(xr @ cm_Wr) + kv)
        return x

    def _L1_ffn_ref(hidden_states, Wg, W1, W2):
        import jax, jax.numpy as jnp
        import numpy as np
        B, C, D = (2, 256, 128)
        I = 256
        E, K = (8, 2)
        CF = 1.25
        Bx, Cx, d = hidden_states.shape
        N = Bx * Cx
        cap = int(N * K * CF / E)
        x = hidden_states.reshape(N, d)
        logits = x @ Wg.T
        top_v, top_i = jax.lax.top_k(logits, K)
        gates = jax.nn.softmax(top_v, axis=-1)
        flat_e = top_i.reshape(N * K)
        gates_f = gates.reshape(N * K)
        tok = jnp.repeat(jnp.arange(N), K)
        onehot = jax.nn.one_hot(flat_e, E, dtype=jnp.int32)
        pos = jnp.cumsum(onehot, axis=0) - 1
        pos_f = jnp.take_along_axis(pos, flat_e[:, None], axis=1)[:, 0]
        keep = pos_f < cap
        pos_safe = jnp.where(keep, pos_f, cap)
        exp_batches = jnp.zeros((E, cap, d), x.dtype).at[flat_e, pos_safe].set(x[tok], mode='drop')
        h = jnp.einsum('ecd,edf->ecf', exp_batches, W1)
        inp, gate = jnp.split(h, 2, axis=-1)
        h = jax.nn.gelu(inp, approximate=False) * gate
        exp_out = jnp.einsum('eci,eid->ecd', h, W2)
        gathered = exp_out[flat_e, jnp.minimum(pos_safe, cap - 1)]
        contrib = jnp.where(keep, gates_f, 0.0)[:, None] * gathered
        out = jax.ops.segment_sum(contrib, tok, num_segments=N)
        return out.reshape(Bx, Cx, d)
    x = L0_attn_x
    x = x + _L0_attn_ref(_layernorm(x, axis=-1), L0_attn_miu_x, L0_attn_lam, L0_attn_A, L0_attn_Bp, L0_attn_td_miu, L0_attn_tdA, L0_attn_tdB, L0_attn_u, L0_attn_Wk, L0_attn_Wv, L0_attn_Wr, L0_attn_Wo, L0_attn_Wg1, L0_attn_Wg2, L0_attn_gamma, L0_attn_beta)
    x = x + _L0_ffn_ref(_layernorm(x, axis=-1), L0_ffn_router_w, L0_ffn_sg, L0_ffn_su, L0_ffn_sd, L0_ffn_eg, L0_ffn_eu, L0_ffn_ed)
    x = x + _L1_attn_ref(_layernorm(x, axis=-1), L1_attn_ln0_g, L1_attn_ln0_b, L1_attn_pre_g, L1_attn_pre_b, L1_attn_post_g, L1_attn_post_b, L1_attn_tm_decay, L1_attn_tm_first, L1_attn_tm_mix_k, L1_attn_tm_mix_v, L1_attn_tm_mix_r, L1_attn_tm_Wk, L1_attn_tm_Wv, L1_attn_tm_Wr, L1_attn_tm_Wo, L1_attn_cm_mix_k, L1_attn_cm_mix_r, L1_attn_cm_Wk, L1_attn_cm_Wv, L1_attn_cm_Wr)
    x = x + _L1_ffn_ref(_layernorm(x, axis=-1), L1_ffn_Wg, L1_ffn_W1, L1_ffn_W2)
    return x

_drawn_inputs = setup_inputs


def setup_inputs(seed=0):
    import zlib

    import numpy as np

    out = dict(_drawn_inputs(seed))
    spreads = {'L0_attn_gamma': (1.0, 0.6),
     'L0_attn_beta': (0.0, 0.8),
     'L1_attn_ln0_g': (1.0, 0.2),
     'L1_attn_ln0_b': (0.0, 0.1),
     'L1_attn_pre_g': (1.0, 0.6),
     'L1_attn_pre_b': (0.0, 0.8),
     'L1_attn_post_g': (1.0, 0.6),
     'L1_attn_post_b': (0.0, 0.8)}
    factors = {'L0_attn_miu_x': 8.0,
     'L0_attn_lam': 8.0,
     'L0_attn_A': 8.0,
     'L0_attn_Bp': 8.0,
     'L0_attn_td_miu': 8.0,
     'L0_attn_tdA': 8.0,
     'L0_attn_tdB': 8.0,
     'L0_attn_u': 8.0,
     'L0_attn_Wk': 8.0,
     'L0_attn_Wv': 8.0,
     'L0_attn_Wr': 8.0,
     'L0_attn_Wo': 8.0,
     'L0_attn_Wg1': 8.0,
     'L0_attn_Wg2': 8.0,
     'L0_ffn_router_w': 8.0,
     'L0_ffn_sg': 6.957,
     'L0_ffn_su': 6.907,
     'L0_ffn_sd': 6.954,
     'L0_ffn_eg': 8.0,
     'L0_ffn_eu': 8.0,
     'L0_ffn_ed': 8.0,
     'L1_attn_tm_decay': 6.335,
     'L1_attn_tm_first': 8.0,
     'L1_attn_tm_mix_k': 8.0,
     'L1_attn_tm_mix_v': 8.0,
     'L1_attn_tm_mix_r': 8.0,
     'L1_attn_tm_Wk': 8.0,
     'L1_attn_tm_Wv': 4.08,
     'L1_attn_tm_Wr': 8.0,
     'L1_attn_tm_Wo': 4.074,
     'L1_attn_cm_mix_k': 4.657,
     'L1_attn_cm_mix_r': 4.361,
     'L1_attn_cm_Wk': 2.716,
     'L1_attn_cm_Wv': 2.69,
     'L1_ffn_Wg': 8.0,
     'L1_ffn_W1': 8.0,
     'L1_ffn_W2': 8.0}
    for name, (base, spread) in spreads.items():
        noise = np.random.default_rng([zlib.crc32(name.encode()), seed]).standard_normal(out[name].shape)
        drawn = base * np.exp(spread * noise) if base else spread * noise
        out[name] = jnp.asarray(drawn.astype(out[name].dtype))
    for name, factor in factors.items():
        out[name] = (out[name] * factor).astype(out[name].dtype)
    return out
```

```python
from contextlib import ExitStack

import concourse.bass as bass
from concourse import mybir

P = 128
B = 8
T = 512
TB = T // P
C = 128
HEAD = 64
NH = C // HEAD
NE = 8
HID = 256
HC = HID // P
HU = 512
UC = HU // P
NS = 5
LR = 32
CAP = int(B * T * 2 * 1.25 / NE)
EPS = 1e-5
K_CLAMP = 60.0
K_EPS = 1e-8
E_CLAMP = 1.1420073898156842e26

F32 = mybir.dt.float32
U32 = mybir.dt.uint32
I32 = mybir.dt.int32
ALU = mybir.AluOpType
ACT = mybir.ActivationFunctionType
AX = mybir.AxisListType

ATTN0 = [("A", NS * LR), ("Bp", C), ("tdA", HEAD), ("WkT", C), ("WvT", C), ("WrT", C), ("WoT", C),
         ("Wg1", 160), ("Wg2a", C)]
MOE0 = [("g", 9 * HID), ("u", 9 * HID), ("d", 9 * HC * C), ("router", NE)]
ATTN1 = [("Wk", HU), ("Wv", HU), ("Wr", HU), ("Wo", UC * C), ("cWk", HU), ("cWv", UC * C), ("cWr", C)]
MOE1 = [("in", NE * HID), ("gate", NE * HID), ("d", NE * HC * C), ("router", NE)]
VECS = ["miu_x", "lam0", "lam1", "lam2", "lam3", "lam4", "td_miu", "u", "gamma", "beta",
        "pre_g", "pre_b", "post_g", "post_b", "mix_k", "mix_v", "mix_r", "cmix_k", "cmix_r"]
NV = len(VECS)
NORMS = ("attn0", "heads", "ffn0", "attn1", "ln0", "pre", "post", "ffn1")
LEVELS = 7


def columns(parts):
    at, out = 0, {}
    for name, n in parts:
        out[name] = at
        at += n
    return out, at


class Sem:

    def __init__(self, handle, per):
        self.handle, self.per = handle, per

    def at(self, b, k=None):
        return b * self.per + (self.per if k is None else k)

    def before(self, b, k=None):
        return (b - 1) * self.per + (self.per if k is None else k)


class Chain:

    def __init__(self, eng, handle):
        self.eng, self.handle, self.per, self.b, self.k = eng, handle, 0, 0, 0

    def start(self, b, first):
        self.per = self.per if first else max(self.per, self.k)
        self.b, self.k = b, 0

    def step(self, ins):
        ins.then_inc(self.handle, 1)
        self.k += 1
        self.eng.wait_ge(self.handle, self.b * self.per + self.k)


def build(nc, x, attn0, tdB, bp4, wg2b, moe0, attn1, lnrow, dfvec, vecs, moe1, ident, levels, tri, iota, out):
    a0, na0 = columns(ATTN0)
    m0, nm0 = columns(MOE0)
    a1, na1 = columns(ATTN1)
    m1, nm1 = columns(MOE1)
    with ExitStack() as ctx:
        def sb(name, shape, dt=F32):
            return ctx.enter_context(nc.sbuf_tensor(name, shape, dt))

        def sem(name, per=1):
            return Sem(ctx.enter_context(nc.semaphore(name)), per)

        W0 = sb("W0", [P, na0])
        TDB = sb("TDB", [HEAD, C])
        BP4 = sb("BP4", [LR, C])
        WG2B = sb("WG2B", [LR, C])
        WM0 = sb("WM0", [P, nm0])
        W1 = sb("W1", [P, na1])
        WM1 = sb("WM1", [P, nm1])
        LNR = sb("LNR", [P, 2, C])
        DF = sb("DF", [P, 2, UC])
        V = sb("V", [P, NV])
        ID = sb("ID", [P, P])
        MASK = sb("MASK", [P, LEVELS, P], I32)
        TRI = sb("TRI", [P, P])
        IOTA = sb("IOTA", [P, 1, NE])
        ONES = sb("ONES", [P, P])
        CON = sb("CON", [P, 3, NE])
        DEC = sb("DEC", [P, 2, UC])
        DTMP = sb("DTMP", [P, UC])

        X = sb("X", [P, B, TB, C])
        XN = sb("XN", [P, B, T + 1])
        XF = XN[:, :, 1:T + 1]
        CW = sb("CW", [P, B, TB, NE])

        ST = sb("ST", [P, TB * NH, 6])
        MV = sb("MV", [P, TB * NH, 2])
        VE = sb("VE", [P, TB * NH])
        RS = sb("RS", [P, TB * NH])
        tile = [sb(f"tile{n}", [P, T]) for n in range(22)]
        XP = [sb(f"XP{n}", [P, T + 1]) for n in range(2)]
        SKP = [sb(f"SKP{n}", [P, T + 1]) for n in range(2)]
        AT = [sb(f"AT{n}", [P, TB, P]) for n in range(NH)]
        D = [sb(f"D{n}", [P, T >> n]) for n in range(1, LEVELS + 1)]
        S4 = sb("S4", [P, TB, C])
        HS = sb("HS", [P, TB, NS * LR])
        R = [sb(f"R{n}", [P, TB, NE]) for n in range(6)]
        M8 = sb("M8", [P, TB, NE])
        I8 = sb("I8", [P, TB, NE], U32)
        IF = sb("IF", [P, TB, 2])
        R4 = [sb(f"R4{n}", [P, TB, 1]) for n in range(4)]
        W2 = sb("W2", [P, TB, 2])
        CARRY = sb("CARRY", [P, 1, NE])

        ps = [ctx.enter_context(nc.psum_tensor(f"bank{n}", [P, T], F32)) for n in range(8)]
        h_dram = nc.dram_tensor("h_scratch", [B * T * NS, LR], F32, kind="Internal").ap()

        def v(name):
            return V[:, VECS.index(name):VECS.index(name) + 1]

        def blk(ap):
            return ap.rearrange("p (a c) -> p a c", c=P)

        def col(j, n=P):
            return slice(n * j, n * (j + 1))

        def w0(name, n, at=0):
            return W0[:, a0[name] + at:a0[name] + at + n]

        def w1(name, n, at=0):
            return W1[:, a1[name] + at:a1[name] + at + n]

        x_in, w_in, const, dec, fences = (sem(n) for n in ("x_in", "w_in", "const", "dec", "fences"))
        dve_chain, dve_chain_a, dve_chain_b = sem("dve_chain"), sem("dve_chain_a"), sem("dve_chain_b")
        norm_rstd = {n: sem(f"{n}_rstd") for n in NORMS}
        norm_moments = {n: sem(f"{n}_moments") for n in NORMS}
        norm_var_eps = {n: sem(f"{n}_var_eps") for n in NORMS}
        norm_out = {n: sem(f"{n}_out") for n in NORMS}
        a_xT, a_xn, a_xx, a_store = sem("a_xT"), sem("a_xn"), sem("a_xx"), sem("a_store", 16)
        a_h, a_tanh = sem("a_h", 2), sem("a_tanh", 2)
        b_load = sem("b_load", 16 * TB)
        b_hT, b_hTs, b_miu, b_mixed, b_x5 = sem("b_hT"), sem("b_hTs", 2), sem("b_miu", NS), sem("b_mixed", NS), sem("b_x5", NS)
        b_td, b_tdt, b_w, b_d, b_k, b_kd = (sem(n) for n in ("b_td", "b_tdt", "b_w", "b_d", "b_k", "b_kd"))
        b_v, b_vs, b_r, b_rs, b_ru = (sem(n) for n in ("b_v", "b_vs", "b_r", "b_rs", "b_ru"))
        b_g1, b_g1t, b_g2, b_gs = sem("b_g1"), sem("b_g1t", 2), sem("b_g2"), sem("b_gs")
        b_level, b_scaled, b_put = sem("b_level", LEVELS + 1), sem("b_scaled", 3 * LEVELS), sem("b_put", LEVELS + 1)
        b_kT, b_kTs, b_u, b_state, b_y = sem("b_kT"), sem("b_kTs"), sem("b_u"), sem("b_state", TB - 1), sem("b_y")
        b_ynT, b_yg, b_z, b_o, b_res = sem("b_ynT"), sem("b_yg"), sem("b_z"), sem("b_o"), sem("b_res")
        b_xT, b_xf, b_logits, b_shift, b_exp, b_cw = (sem(n) for n in ("b_xT", "b_xf", "b_logits", "b_shift", "b_exp", "b_cw"))
        moe_sems = {k: [sem(f"{k}_gu", 4 * n), sem(f"{k}_act", HC * n), sem(f"{k}_hid", HC * n),
                        sem(f"{k}_down", n), sem(f"{k}_sum", n)] for k, n in (("c", NE + 1), ("e", NE))}
        d_aff, d_xT, d_xn, d_mix = sem("d_aff"), sem("d_xT"), sem("d_xn"), sem("d_mix", 3)
        d_kvr, d_act, d_kv, d_rw, d_o, d_x1 = sem("d_kvr", 3 * UC), sem("d_act", 2 * UC), sem("d_kv", UC), sem("d_rw", UC), sem("d_o"), sem("d_x1")
        d_x2T, d_xn2, d_mix2, d_kk, d_silu = sem("d_x2T"), sem("d_xn2"), sem("d_mix2", 2), sem("d_kk", UC), sem("d_silu", UC)
        d_o2, d_sig, d_res = sem("d_o2"), sem("d_sig"), sem("d_res")
        d_x3T, d_xf, d_logits, d_gap, d_exp, d_sel, d_pos, d_cw = (
            sem(n) for n in ("d_x3T", "d_xf", "d_logits", "d_gap", "d_exp", "d_sel", "d_pos", "d_cw"))
        stored = sem("stored", 16)

        block = ctx.enter_context(nc.Block())

        def over_batches(eng, body):
            body(0, True)
            with eng.Fori(1, B) as b:
                body(b, False)

        def fence(eng):
            eng.sem_inc(fences.handle, 1)

        WEIGHTS = ((W0, attn0), (TDB, tdB), (BP4, bp4), (WG2B, wg2b), (V, vecs), (ID, ident), (MASK, levels),
                   (IOTA, iota), (WM0, moe0), (W1, attn1), (LNR, lnrow), (DF, dfvec), (TRI, tri), (WM1, moe1))
        N_CONST = 8 + len(XP) + len(SKP)
        ALL_W = 16 * len(WEIGHTS)

        @block.sync
        def _(sp):
            sp.dma_start(X[:], x).then_inc(x_in.handle, 16)
            for dst, src in WEIGHTS:
                sp.dma_start(dst[:], src).then_inc(w_in.handle, 16)

            def store_h(b, first):
                sp.wait_ge(a_tanh.handle, a_tanh.at(b))
                sp.dma_start(h_dram.rearrange("(b j p s) k -> b p j (s k)", p=P, j=TB, s=NS)[b], HS[:])\
                    .then_inc(a_store.handle, 16)

            over_batches(sp, store_h)
            sp.wait_ge(a_store.handle, a_store.at(B - 1))

            def load_h(b, first):
                if not first:
                    sp.wait_ge(b_hT.handle, b_hT.before(b))
                src = h_dram.rearrange("(s b j p) k -> b j p s k", p=P, j=TB, s=NS)[b]
                for j in range(TB):
                    sp.dma_start(HS[:, j].rearrange("p (s k) -> p s k", s=NS), src[j]).then_inc(b_load.handle, 16)

            over_batches(sp, load_h)
            done = moe_sems["e"][4]

            def store_out(b, first):
                sp.wait_ge(done.handle, done.at(b))
                sp.dma_start(out[b], X[:, b]).then_inc(stored.handle, 16)

            over_batches(sp, store_out)
            sp.wait_ge(stored.handle, stored.at(B - 1))

        @block.gpsimd
        def _(pool):
            pool.memset(ONES[:], 1.0).then_inc(const.handle, 1)
            pool.memset(CON[:, 0], EPS).then_inc(const.handle, 1)
            pool.memset(CON[:, 1], EPS * NH).then_inc(const.handle, 1)
            pool.memset(CON[:, 2], -0.5).then_inc(const.handle, 1)
            pool.memset(XN[:, :, 0:1], 0.0).then_inc(const.handle, 1)
            for z in (*XP, *SKP):
                pool.memset(z[:, 0:1], 0.0).then_inc(const.handle, 1)
            pool.memset(S4[:], 0.0).then_inc(const.handle, 1)
            pool.memset(CARRY[:], 0.0).then_inc(const.handle, 1)
            pool.memset(R4[3][:], 0.0).then_inc(const.handle, 1)
            pool.wait_ge(const.handle, N_CONST)

            def rstd(b, name, n=TB, eps=0):
                pool.wait_ge(norm_moments[name].handle, norm_moments[name].at(b))
                pool.tensor_tensor(VE[:, 0:n], MV[:, 0:n, 1], CON[:, eps, 0:n], ALU.add).then_inc(norm_var_eps[name].handle, 1)
                pool.wait_ge(norm_var_eps[name].handle, norm_var_eps[name].at(b))
                pool.tensor_tensor(RS[:, 0:n], VE[:, 0:n], CON[:, 2, 0:n], ALU.pow).then_inc(norm_rstd[name].handle, 1)

            over_batches(pool, lambda b, first: rstd(b, "attn0"))

            def pool_b(b, first):
                for s in range(NS):
                    pool.wait_ge(b_mixed.handle, b_mixed.at(b, s + 1))
                    fence(pool)
                    pool.tensor_tensor(tile[2 + s][:], tile[2 + s][:], XN[:, b, 1:T + 1], ALU.add).then_inc(b_x5.handle, 1)
                rstd(b, "heads", TB * NH, 1)
                pool.wait_ge(b_yg.handle, b_yg.at(b))
                pool.wait_ge(b_gs.handle, b_gs.at(b))
                pool.tensor_tensor(tile[16][:], tile[16][:], tile[15][:], ALU.mult).then_inc(b_z.handle, 1)
                rstd(b, "ffn0")

            over_batches(pool, pool_b)

            def pool_d(b, first):
                for name in NORMS[3:]:
                    rstd(b, name)

            over_batches(pool, pool_d)

        @block.vector
        def _(dve):
            chain_a, chain_b, chain_d = (Chain(dve, s.handle) for s in (dve_chain_a, dve_chain_b, dve_chain))

            def norm(b, name, chain, src, dst, n=TB):
                for j in range(n):
                    ins = dve.bn_stats(ST[:, j], src(j))
                chain.step(ins)
                fence(dve)
                for j in range(n):
                    ins = dve.bn_aggr(MV[:, j], ST[:, j])
                ins.then_inc(norm_moments[name].handle, 1)
                dve.wait_ge(norm_rstd[name].handle, norm_rstd[name].at(b))
                for j in range(n):
                    ins = dve.tensor_scalar(dst(j), src(j), MV[:, j, 0:1], RS[:, j:j + 1], ALU.subtract, ALU.mult)
                ins.then_inc(norm_out[name].handle, 1)

            def top_two(chain, probs):
                fence(dve)
                for j in range(TB):
                    ins = dve.max(M8[:, j], probs[:, j])
                chain.step(ins)
                fence(dve)
                for j in range(TB):
                    ins = dve.max_index(I8[:, j], M8[:, j], probs[:, j])
                chain.step(ins)
                chain.step(dve.tensor_copy(IF[:], I8[:, :, 0:2]))
                for k in range(2):
                    ins = dve.tensor_tensor(R[3 + k][:], IOTA[:].to_broadcast([P, TB, NE]),
                                            IF[:, :, k:k + 1].to_broadcast([P, TB, NE]), ALU.is_equal)
                chain.step(ins)

            dve.wait_ge(x_in.handle, 16)
            dve.wait_ge(w_in.handle, ALL_W)
            dve.wait_ge(const.handle, N_CONST)

            def dve_a(b, first):
                chain_a.start(b, first)
                if not first:
                    dve.wait_ge(a_xT.handle, a_xT.before(b))
                    fence(dve)
                norm(b, "attn0", chain_a, lambda j: X[:, b, j], lambda j: tile[0][:, col(j)])
                dve.wait_ge(a_xn.handle, a_xn.at(b))
                if not first:
                    dve.wait_ge(a_h.handle, a_h.before(b))
                chain_a.step(dve.tensor_tensor(tile[1][:], XN[:, b, 0:T], XN[:, b, 1:T + 1], ALU.subtract))
                dve.scalar_tensor_tensor(out=tile[2][:], in0=tile[1][:], scalar=v("miu_x"), in1=XN[:, b, 1:T + 1],
                                         op0=ALU.mult, op1=ALU.add).then_inc(a_xx.handle, 1)

            over_batches(dve, dve_a)

            def dve_b(b, first):
                chain_b.start(b, first)
                if first:
                    dve.wait_ge(a_h.handle, a_h.at(B - 1))
                chain_b.step(dve.tensor_tensor(tile[1][:], XN[:, b, 0:T], XN[:, b, 1:T + 1], ALU.subtract))
                if not first:
                    dve.wait_ge(b_g1.handle, b_g1.before(b))
                for s in range(NS):
                    dve.wait_ge(b_miu.handle, b_miu.at(b, s + 1))
                    dve.scalar_tensor_tensor(out=tile[2 + s][:], in0=ps[2 + s][:], scalar=v(f"lam{s}"), in1=tile[1][:],
                                             op0=ALU.add, op1=ALU.mult).then_inc(b_mixed.handle, 1)
                dve.wait_ge(b_d.handle, b_d.at(b))
                dve.wait_ge(b_k.handle, b_k.at(b))
                if not first:
                    dve.wait_ge(b_kT.handle, b_kT.before(b))
                dve.scalar_tensor_tensor(out=tile[9][:], in0=tile[8][:], scalar=1.0, in1=ps[0][:],
                                         op0=ALU.min, op1=ALU.mult).then_inc(b_kd.handle, 1)
                dve.wait_ge(b_level.handle, b_level.at(b, 1))
                if not first:
                    dve.wait_ge(b_y.handle, b_y.before(b))
                for n in range(NH):
                    ins = dve.tensor_tensor(AT[n][:], blk(ps[n][:]),
                                            ID[:].rearrange("p (a c) -> p a c", a=1).to_broadcast([P, TB, P]), ALU.mult)
                ins.then_inc(b_put.handle, 1)
                dprod = tile[8]
                for lv in range(LEVELS):
                    half, nb = 1 << lv, T >> (lv + 1)
                    dve.wait_ge(b_level.handle, b_level.at(b, lv + 2))
                    dve.wait_ge(b_put.handle, b_put.at(b, lv + 1))
                    if lv:
                        dve.wait_ge(b_scaled.handle, b_scaled.at(b, 3 * lv))
                    else:
                        dve.wait_ge(b_kd.handle, b_kd.at(b))
                    dd = dprod[:].rearrange("p (m two) -> p m two", two=2)
                    for buf, hl, dl in ((tile[9], 0, 1), (tile[10], 1, 0)):
                        part = buf[:].rearrange("p (m two h) -> p m two h", two=2, h=half)[:, :, hl]
                        dve.tensor_tensor(part, part, dd[:, :, dl:dl + 1].to_broadcast([P, nb, half]), ALU.mult)\
                            .then_inc(b_scaled.handle, 1)
                    dve.tensor_tensor(D[lv][:], dd[:, :, 0], dd[:, :, 1], ALU.mult).then_inc(b_scaled.handle, 1)
                    dprod = D[lv]
                    for n in range(NH):
                        bank = 2 * ((lv + 1) % 3) + n
                        ins = dve.copy_predicated(AT[n][:], MASK[:, lv:lv + 1].to_broadcast([P, TB, P]), blk(ps[bank][:]))
                    ins.then_inc(b_put.handle, 1)
                dve.wait_ge(b_u.handle, b_u.at(b))
                dve.wait_ge(b_scaled.handle, b_scaled.at(b))
                for c in range(1, TB):
                    if c > 1:
                        dve.wait_ge(b_state.handle, b_state.at(b, c - 1))
                    for n in range(NH):
                        h = slice(HEAD * n, HEAD * (n + 1))
                        new, u = S4[h, c, h], ps[6][h, P * (c - 1) + HEAD * n:P * (c - 1) + HEAD * (n + 1)]
                        if c == 1:
                            ins = dve.tensor_copy(new, u)
                        else:
                            ins = dve.scalar_tensor_tensor(out=new, in0=S4[h, c - 1, h], scalar=D[LEVELS - 1][h, c - 1:c],
                                                           in1=u, op0=ALU.mult, op1=ALU.add)
                    ins.then_inc(b_state.handle, 1)
                dve.wait_ge(b_y.handle, b_y.at(b))
                if not first:
                    dve.wait_ge(b_ynT.handle, b_ynT.before(b))
                norm(b, "heads", chain_b, lambda j: ps[4][:, col(j, HEAD)], lambda j: tile[14][:, col(j, HEAD)], TB * NH)
                dve.wait_ge(b_o.handle, b_o.at(b))
                chain_b.step(dve.tensor_tensor(X[:, b], X[:, b], blk(ps[7][:]), ALU.add))
                fence(dve)
                norm(b, "ffn0", chain_b, lambda j: X[:, b, j], lambda j: tile[17][:, col(j)])
                dve.wait_ge(b_logits.handle, b_logits.at(b))
                logits = ps[5][:, 0:TB * NE].rearrange("p (j e) -> p j e", e=NE)
                chain_b.step(dve.tensor_reduce(R4[0][:], logits, AX.X, ALU.max))
                dve.tensor_tensor(R[0][:], logits, R4[0][:].to_broadcast([P, TB, NE]), ALU.subtract).then_inc(b_shift.handle, 1)
                dve.wait_ge(b_exp.handle, b_exp.at(b))
                chain_b.step(dve.tensor_reduce(R4[1][:], R[1][:], AX.X, ALU.add))
                chain_b.step(dve.reciprocal(R4[2][:], R4[1][:]))
                chain_b.step(dve.tensor_tensor(R[2][:], R[1][:], R4[2][:].to_broadcast([P, TB, NE]), ALU.mult))
                top_two(chain_b, R[2])
                chain_b.step(dve.tensor_tensor(R4[1][:], M8[:, :, 0:1], M8[:, :, 1:2], ALU.add))
                chain_b.step(dve.reciprocal(R4[2][:], R4[1][:]))
                chain_b.step(dve.tensor_tensor(W2[:], M8[:, :, 0:2], R4[2][:].to_broadcast([P, TB, 2]), ALU.mult))
                for k in range(2):
                    ins = dve.tensor_tensor(R[k][:], R[3 + k][:], W2[:, :, k:k + 1].to_broadcast([P, TB, NE]), ALU.mult)
                chain_b.step(ins)
                dve.tensor_tensor(CW[:, b], R[0][:], R[1][:], ALU.add).then_inc(b_cw.handle, 1)

            over_batches(dve, dve_b)

            def dve_moe(key, n, shared):
                gu, act, hid, down, total = moe_sems[key]

                def body(b, first):
                    for e in range(n + 1):
                        for c in range(HC if e < n else 0):
                            dve.wait_ge(act.handle, act.at(b, HC * e + c + 1))
                            dve.wait_ge(gu.handle, gu.at(b, 4 * e + 2 * c + 2))
                            if e >= 2:
                                dve.wait_ge(down.handle, down.at(b, e - 1))
                            elif not first:
                                dve.wait_ge(down.handle, down.before(b))
                            dve.tensor_tensor(tile[2 * (e % 2) + c][:], tile[4 + c][:], ps[2 * c + 1][:], ALU.mult)\
                                .then_inc(hid.handle, 1)
                        if e:
                            add(b, first, e - 1)

                def add(b, first, e):
                    dve.wait_ge(down.handle, down.at(b, e + 1))
                    if e:
                        dve.wait_ge(total.handle, total.at(b, e))
                    if shared and e == 0:
                        ins = dve.tensor_tensor(X[:, b], X[:, b], blk(ps[4][:]), ALU.add)
                    else:
                        for j in range(TB):
                            ins = dve.scalar_tensor_tensor(
                                out=X[:, b, j], in0=ps[4 + e % 2][:, col(j)], scalar=CW[:, b, j, e - shared:e - shared + 1],
                                in1=X[:, b, j], op0=ALU.mult, op1=ALU.add)
                    ins.then_inc(total.handle, 1)

                return body

            dve.wait_ge(b_cw.handle, b_cw.at(B - 1))
            over_batches(dve, dve_moe("c", NE + 1, 1))

            def dve_d(b, first):
                step = chain_d.step
                chain_d.start(b, first)
                summed = moe_sems["c"][4]
                if first:
                    dve.wait_ge(summed.handle, summed.at(B - 1))
                    fence(dve)
                norm(b, "attn1", chain_d, lambda j: X[:, b, j], lambda j: tile[0][:, col(j)])
                dve.wait_ge(norm_out["attn1"].handle, norm_out["attn1"].at(b))
                fence(dve)
                norm(b, "ln0", chain_d, lambda j: tile[0][:, col(j)], lambda j: tile[1][:, col(j)])
                dve.wait_ge(norm_out["ln0"].handle, norm_out["ln0"].at(b))
                step(dve.tensor_tensor(blk(tile[1][:]), blk(tile[1][:]), LNR[:, 0:1].to_broadcast([P, TB, C]), ALU.mult))
                step(dve.tensor_tensor(blk(tile[1][:]), blk(tile[1][:]), LNR[:, 1:2].to_broadcast([P, TB, C]), ALU.add))
                fence(dve)
                norm(b, "pre", chain_d, lambda j: tile[1][:, col(j)], lambda j: tile[2][:, col(j)])
                dve.wait_ge(d_xn.handle, d_xn.at(b))
                step(dve.tensor_tensor(tile[3][:], XP[0][:, 1:T + 1], XP[0][:, 0:T], ALU.subtract))
                for n, name in enumerate(("mix_k", "mix_v", "mix_r")):
                    dve.scalar_tensor_tensor(out=tile[4 + n][:], in0=tile[3][:], scalar=v(name), in1=XP[0][:, 0:T],
                                             op0=ALU.mult, op1=ALU.add).then_inc(d_mix.handle, 1)
                for c in range(UC):
                    kx, rt, kv, wk = (tile[i][:] for i in (7 + 2 * (c % 2), 8 + 2 * (c % 2), 11, 12))
                    rw = tile[13 + c][:]
                    first_c, decay_c = DEC[:, 1, c:c + 1], DEC[:, 0, c:c + 1]
                    dve.wait_ge(d_act.handle, d_act.at(b, 2 * c + 2))
                    dve.wait_ge(d_kvr.handle, d_kvr.at(b, 3 * c + 2))
                    step(dve.tensor_scalar(kx, kx, E_CLAMP, None, ALU.min))
                    dve.tensor_tensor(kv, kx, ps[2 + 3 * (c % 2)][:], ALU.mult).then_inc(d_kv.handle, 1)
                    dve.wait_ge(d_kv.handle, d_kv.at(b, c + 1))
                    for m, val in enumerate((kx, kv)):
                        ins = dve.tensor_tensor_scan(SKP[m][:, 1:T + 1], decay_c.to_broadcast([P, T]), val, 0.0,
                                                     ALU.mult, ALU.add)
                    step(ins)
                    step(dve.scalar_tensor_tensor(out=wk, in0=kx, scalar=first_c, in1=SKP[0][:, 0:T],
                                                  op0=ALU.mult, op1=ALU.add))
                    step(dve.tensor_scalar(wk, wk, K_EPS, None, ALU.add))
                    step(dve.reciprocal(wk, wk))
                    step(dve.scalar_tensor_tensor(out=kv, in0=kv, scalar=first_c, in1=SKP[1][:, 0:T],
                                                  op0=ALU.mult, op1=ALU.add))
                    step(dve.tensor_tensor(kv, kv, wk, ALU.mult))
                    step(dve.tensor_scalar(rt, rt, 0.5, 0.5, ALU.mult, ALU.add))
                    if not first:
                        dve.wait_ge(d_o.handle, d_o.before(b))
                    dve.tensor_tensor(rw, rt, kv, ALU.mult).then_inc(d_rw.handle, 1)
                    dve.wait_ge(d_rw.handle, d_rw.at(b, c + 1))
                dve.wait_ge(d_o.handle, d_o.at(b))
                dve.tensor_tensor(tile[1][:], tile[1][:], ps[7][:], ALU.add).then_inc(d_x1.handle, 1)
                dve.wait_ge(d_x1.handle, d_x1.at(b))
                fence(dve)
                norm(b, "post", chain_d, lambda j: tile[1][:, col(j)], lambda j: tile[2][:, col(j)])
                dve.wait_ge(d_xn2.handle, d_xn2.at(b))
                step(dve.tensor_tensor(tile[3][:], XP[1][:, 1:T + 1], XP[1][:, 0:T], ALU.subtract))
                for n, name in enumerate(("cmix_k", "cmix_r")):
                    dve.scalar_tensor_tensor(out=tile[4 + n][:], in0=tile[3][:], scalar=v(name), in1=XP[1][:, 0:T],
                                             op0=ALU.mult, op1=ALU.add).then_inc(d_mix2.handle, 1)
                dve.wait_ge(d_sig.handle, d_sig.at(b))
                step(dve.tensor_scalar(tile[17][:], tile[17][:], 0.5, 0.5, ALU.mult, ALU.add))
                dve.wait_ge(d_o2.handle, d_o2.at(b))
                step(dve.tensor_tensor(tile[17][:], tile[17][:], ps[5][:], ALU.add))
                step(dve.tensor_tensor(tile[17][:], tile[17][:], tile[1][:], ALU.add))
                step(dve.tensor_tensor(X[:, b], X[:, b], blk(tile[17][:]), ALU.add))
                fence(dve)
                norm(b, "ffn1", chain_d, lambda j: X[:, b, j], lambda j: tile[2][:, col(j)])
                dve.wait_ge(d_logits.handle, d_logits.at(b))
                logits = ps[7][:, 0:TB * NE].rearrange("p (j e) -> p j e", e=NE)
                step(dve.tensor_copy(R[0][:], logits))
                top_two(chain_d, R[0])
                dve.tensor_tensor(R[1][:], R[3][:], R[4][:], ALU.add).then_inc(d_sel.handle, 1)
                dve.tensor_tensor(W2[:], M8[:, :, 0:2], M8[:, :, 0:1].to_broadcast([P, TB, 2]), ALU.subtract)\
                    .then_inc(d_gap.handle, 1)
                dve.wait_ge(d_exp.handle, d_exp.at(b))
                step(dve.tensor_tensor(R4[0][:], W2[:, :, 0:1], W2[:, :, 1:2], ALU.add))
                step(dve.reciprocal(R4[1][:], R4[0][:]))
                step(dve.tensor_tensor(W2[:], W2[:], R4[1][:].to_broadcast([P, TB, 2]), ALU.mult))
                for k in range(2):
                    ins = dve.tensor_tensor(R[3 + k][:], R[3 + k][:], W2[:, :, k:k + 1].to_broadcast([P, TB, NE]), ALU.mult)
                step(ins)
                step(dve.tensor_tensor(R[2][:], R[3][:], R[4][:], ALU.add))
                dve.wait_ge(d_pos.handle, d_pos.at(b))
                pos = ps[1][:, 0:TB * NE].rearrange("p (j e) -> p j e", e=NE)
                step(dve.tensor_tensor(R[5][:], pos, CARRY[:].to_broadcast([P, TB, NE]), ALU.add))
                step(dve.tensor_scalar(R[5][:], R[5][:], float(CAP), None, ALU.is_lt))
                step(dve.tensor_tensor(CARRY[:, 0], CARRY[:, 0], ps[1][:, TB * NE:(TB + 1) * NE], ALU.add))
                dve.tensor_tensor(CW[:, b], R[2][:], R[5][:], ALU.mult).then_inc(d_cw.handle, 1)

            dve.wait_ge(dec.handle, 3)
            over_batches(dve, dve_d)
            dve.wait_ge(d_cw.handle, d_cw.at(B - 1))
            over_batches(dve, dve_moe("e", NE, 0))

        @block.scalar
        def _(act):
            act.wait_ge(w_in.handle, ALL_W)
            act.activation(DTMP[:], DF[:, 0], ACT.Exp).then_inc(dec.handle, 1)
            act.wait_ge(dec.handle, 1)
            act.activation(DEC[:, 0], DTMP[:], ACT.Exp, scale=-1.0).then_inc(dec.handle, 1)
            act.activation(DEC[:, 1], DF[:, 1], ACT.Exp).then_inc(dec.handle, 1)

            def act_a(b, first):
                act.wait_ge(a_xT.handle, a_xT.at(b))
                fence(act)
                act.activation(XN[:, b, 1:T + 1], ps[0][:], ACT.Copy).then_inc(a_xn.handle, 1)
                for q in range(2):
                    act.wait_ge(a_h.handle, a_h.at(b, q + 1))
                    if not first:
                        act.wait_ge(a_store.handle, a_store.before(b))
                    act.activation(HS[:, 2 * q:2 * q + 2].rearrange("p j k -> p (j k)"), ps[1 + q][:, 0:2 * NS * LR], ACT.Tanh)\
                        .then_inc(a_tanh.handle, 1)

            over_batches(act, act_a)

            def act_b(b, first):
                act.wait_ge(b_hT.handle, b_hT.at(b))
                if not first:
                    act.wait_ge(b_miu.handle, b_miu.before(b))
                act.activation(tile[0][:], ps[0][:], ACT.Copy).then_inc(b_hTs.handle, 1)
                act.activation(tile[7][0:LR], ps[1][0:LR], ACT.Copy).then_inc(b_hTs.handle, 1)
                act.wait_ge(b_td.handle, b_td.at(b))
                act.activation(tile[11][0:HEAD], ps[7][0:HEAD], ACT.Tanh).then_inc(b_tdt.handle, 1)
                act.wait_ge(b_v.handle, b_v.at(b))
                act.activation(tile[13][:], ps[1][:], ACT.Copy).then_inc(b_vs.handle, 1)
                act.wait_ge(b_w.handle, b_w.at(b))
                act.activation(tile[8][:], ps[2][:], ACT.Exp, bias=v("td_miu")).then_inc(b_d.handle, 1)
                act.wait_ge(b_r.handle, b_r.at(b))
                act.activation(tile[10][:], ps[3][:], ACT.Copy).then_inc(b_rs.handle, 1)
                act.activation(tile[12][:], ps[3][:], ACT.Identity, scale=v("u")).then_inc(b_ru.handle, 1)
                act.wait_ge(b_g1.handle, b_g1.at(b))
                act.activation(tile[18][:], ps[4][:], ACT.Tanh).then_inc(b_g1t.handle, 1)
                act.activation(tile[19][0:LR], ps[5][0:LR], ACT.Tanh).then_inc(b_g1t.handle, 1)
                act.wait_ge(b_g2.handle, b_g2.at(b))
                if not first:
                    act.wait_ge(b_z.handle, b_z.before(b))
                act.activation(tile[15][:], ps[6][:], ACT.Copy).then_inc(b_gs.handle, 1)
                act.wait_ge(b_kT.handle, b_kT.at(b))
                act.activation(tile[20][:], ps[7][:], ACT.Copy).then_inc(b_kTs.handle, 1)
                act.wait_ge(b_ynT.handle, b_ynT.at(b))
                if not first:
                    act.wait_ge(b_o.handle, b_o.before(b))
                act.activation(tile[16][:], ps[5][:], ACT.Identity, scale=v("gamma"), bias=v("beta")).then_inc(b_yg.handle, 1)
                act.wait_ge(b_xT.handle, b_xT.at(b))
                fence(act)
                act.activation(XN[:, b, 1:T + 1], ps[6][:], ACT.Copy)
                act.activation(tile[21][:], ps[6][:], ACT.Copy).then_inc(b_xf.handle, 1)
                act.wait_ge(b_shift.handle, b_shift.at(b))
                act.activation(R[1][:], R[0][:], ACT.Exp).then_inc(b_exp.handle, 1)

            over_batches(act, act_b)

            def act_moe(key, n, func):
                gu, acted, hid, down, total = moe_sems[key]

                def body(b, first):
                    for e in range(n):
                        for c in range(HC):
                            act.wait_ge(gu.handle, gu.at(b, 4 * e + 2 * c + 1))
                            if e:
                                act.wait_ge(hid.handle, hid.at(b, HC * (e - 1) + c + 1))
                            elif not first:
                                act.wait_ge(hid.handle, hid.before(b))
                            act.activation(tile[4 + c][:], ps[2 * c][:], func).then_inc(acted.handle, 1)

                return body

            over_batches(act, act_moe("c", NE + 1, ACT.Silu))

            def act_d(b, first):
                act.wait_ge(d_xT.handle, d_xT.at(b))
                act.activation(XP[0][:, 1:T + 1], ps[0][:], ACT.Identity, scale=v("pre_g"), bias=v("pre_b"))\
                    .then_inc(d_xn.handle, 1)
                for c in range(UC):
                    kx, rt = tile[7 + 2 * (c % 2)][:], tile[8 + 2 * (c % 2)][:]
                    act.wait_ge(d_kvr.handle, d_kvr.at(b, 3 * c + 1))
                    if c >= 2:
                        act.wait_ge(d_rw.handle, d_rw.at(b, c - 1))
                    elif not first:
                        act.wait_ge(d_rw.handle, d_rw.before(b))
                    act.activation(kx, ps[1 + 3 * (c % 2)][:], ACT.Exp).then_inc(d_act.handle, 1)
                    act.wait_ge(d_kvr.handle, d_kvr.at(b, 3 * c + 3))
                    act.activation(rt, ps[3 + 3 * (c % 2)][:], ACT.Tanh, scale=0.5).then_inc(d_act.handle, 1)
                act.wait_ge(d_x2T.handle, d_x2T.at(b))
                act.activation(XP[1][:, 1:T + 1], ps[0][:], ACT.Identity, scale=v("post_g"), bias=v("post_b"))\
                    .then_inc(d_xn2.handle, 1)
                for c in range(UC):
                    act.wait_ge(d_kk.handle, d_kk.at(b, c + 1))
                    if not first:
                        act.wait_ge(d_o2.handle, d_o2.before(b))
                    act.activation(tile[18 + c][:], ps[1 + c][:], ACT.Silu).then_inc(d_silu.handle, 1)
                act.wait_ge(d_o2.handle, d_o2.at(b))
                act.activation(tile[17][:], ps[6][:], ACT.Tanh, scale=0.5).then_inc(d_sig.handle, 1)
                act.wait_ge(d_x3T.handle, d_x3T.at(b))
                fence(act)
                act.activation(XN[:, b, 1:T + 1], ps[0][:], ACT.Copy)
                act.activation(tile[3][:], ps[0][:], ACT.Copy).then_inc(d_xf.handle, 1)
                act.wait_ge(d_gap.handle, d_gap.at(b))
                act.activation(W2[:], W2[:], ACT.Exp).then_inc(d_exp.handle, 1)

            over_batches(act, act_d)
            over_batches(act, act_moe("e", NE, ACT.Gelu))

        @block.tensor
        def _(pe):
            def product(dst, pairs):
                for i, (lhsT, rhs) in enumerate(pairs):
                    ins = pe.matmul(dst, lhsT, rhs, start=i == 0, stop=i == len(pairs) - 1)
                return ins

            def transposes(dst, src):
                for j in range(TB):
                    ins = pe.transpose(dst[:, col(j)], src[:, col(j)], ID[:])
                return ins

            pe.wait_ge(w_in.handle, ALL_W)
            pe.wait_ge(const.handle, N_CONST)

            def pe_a(b, first):
                pe.wait_ge(norm_out["attn0"].handle, norm_out["attn0"].at(b))
                if not first:
                    pe.wait_ge(a_xn.handle, a_xn.before(b))
                transposes(ps[0], tile[0]).then_inc(a_xT.handle, 1)
                pe.wait_ge(a_xx.handle, a_xx.at(b))
                for q in range(2):
                    if not first:
                        pe.wait_ge(a_tanh.handle, a_tanh.before(b, q + 1))
                    for j in range(2):
                        ins = product(ps[1 + q][:, col(j, NS * LR)], [(tile[2][:, col(2 * q + j)], w0("A", NS * LR))])
                    ins.then_inc(a_h.handle, 1)

            over_batches(pe, pe_a)

            def pe_b(b, first):
                pe.wait_ge(b_load.handle, b_load.at(b))
                if first:
                    pe.wait_ge(a_tanh.handle, a_tanh.at(B - 1))
                else:
                    pe.wait_ge(b_put.handle, b_put.before(b, 7))
                for j in range(TB):
                    pe.transpose(ps[0][:, col(j)], HS[:, j, 0:P], ID[:])
                    ins = pe.transpose(ps[1][0:LR, col(j)], HS[:, j, P:P + LR], ID[:])
                ins.then_inc(b_hT.handle, 1)
                pe.wait_ge(b_hTs.handle, b_hTs.at(b))
                if not first:
                    pe.wait_ge(b_xf.handle, b_xf.before(b))
                    pe.wait_ge(b_cw.handle, b_cw.before(b))
                for s in range(4):
                    product(ps[2 + s][:], [(W0[LR * s:LR * (s + 1), a0["Bp"]:a0["Bp"] + C], tile[0][LR * s:LR * (s + 1)])])\
                        .then_inc(b_miu.handle, 1)
                product(ps[6][:], [(BP4[:], tile[7][0:LR])]).then_inc(b_miu.handle, 1)
                pe.wait_ge(b_x5.handle, b_x5.at(b, 1))
                product(ps[7][0:HEAD], [(w0("tdA", HEAD), tile[2][:])]).then_inc(b_td.handle, 1)
                pe.wait_ge(b_x5.handle, b_x5.at(b, 2))
                product(ps[0][:], [(w0("WkT", C), tile[3][:])]).then_inc(b_k.handle, 1)
                pe.wait_ge(b_x5.handle, b_x5.at(b, 3))
                for j in range(TB):
                    ins = product(ps[1][:, col(j)], [(tile[4][:, col(j)], w0("WvT", C))])
                ins.then_inc(b_v.handle, 1)
                pe.wait_ge(b_tdt.handle, b_tdt.at(b))
                product(ps[2][:], [(TDB[:], tile[11][0:HEAD])]).then_inc(b_w.handle, 1)
                pe.wait_ge(b_x5.handle, b_x5.at(b, 4))
                product(ps[3][:], [(w0("WrT", C), tile[5][:])]).then_inc(b_r.handle, 1)
                pe.wait_ge(b_x5.handle, b_x5.at(b, 5))
                product(ps[4][:], [(w0("Wg1", P), tile[6][:])])
                product(ps[5][0:LR], [(w0("Wg1", LR, P), tile[6][:])]).then_inc(b_g1.handle, 1)
                pe.wait_ge(b_g1t.handle, b_g1t.at(b))
                product(ps[6][:], [(w0("Wg2a", C), tile[18][:]), (WG2B[:], tile[19][0:LR])]).then_inc(b_g2.handle, 1)

                pe.wait_ge(b_kd.handle, b_kd.at(b))
                pe.wait_ge(b_vs.handle, b_vs.at(b))
                pe.wait_ge(b_ru.handle, b_ru.at(b))
                for lv in range(-1, LEVELS):
                    if lv > 0:
                        pe.wait_ge(b_scaled.handle, b_scaled.at(b, 3 * lv))
                    if lv >= 2:
                        pe.wait_ge(b_put.handle, b_put.at(b, lv - 1))
                    if lv == 1:
                        pe.wait_ge(b_g1t.handle, b_g1t.at(b))
                    for n in range(NH):
                        h = slice(HEAD * n, HEAD * (n + 1))
                        r = tile[12] if lv < 0 else tile[10]
                        for c in range(TB):
                            ins = product(ps[2 * ((lv + 1) % 3) + n][:, col(c)], [(tile[9][h, col(c)], r[h, col(c)])])
                    ins.then_inc(b_level.handle, 1)
                pe.wait_ge(b_scaled.handle, b_scaled.at(b))
                transposes(ps[7], tile[9]).then_inc(b_kT.handle, 1)
                pe.wait_ge(b_kTs.handle, b_kTs.at(b))
                pe.wait_ge(b_gs.handle, b_gs.at(b))
                for c in range(TB - 1):
                    ins = product(ps[6][:, col(c)], [(tile[20][:, col(c)], tile[13][:, col(c)])])
                ins.then_inc(b_u.handle, 1)
                pe.wait_ge(b_put.handle, b_put.at(b))
                for c in range(TB):
                    if c:
                        pe.wait_ge(b_state.handle, b_state.at(b, c))
                        pe.matmul(ps[4][:, col(c)], tile[10][:, col(c)], S4[:, c], start=True, stop=False)
                    for n in range(NH):
                        at = P * c + HEAD * n
                        ins = pe.matmul(ps[4][:, at:at + HEAD], AT[n][:, c], tile[13][:, at:at + HEAD],
                                        start=c == 0, stop=c == 0 or n == NH - 1)
                ins.then_inc(b_y.handle, 1)
                pe.wait_ge(norm_out["heads"].handle, norm_out["heads"].at(b))
                transposes(ps[5], tile[14]).then_inc(b_ynT.handle, 1)
                pe.wait_ge(b_z.handle, b_z.at(b))
                for j in range(TB):
                    ins = product(ps[7][:, col(j)], [(tile[16][:, col(j)], w0("WoT", C))])
                ins.then_inc(b_o.handle, 1)
                pe.wait_ge(norm_out["ffn0"].handle, norm_out["ffn0"].at(b))
                transposes(ps[6], tile[17]).then_inc(b_xT.handle, 1)
                pe.wait_ge(b_xf.handle, b_xf.at(b))
                for j in range(TB):
                    ins = product(ps[5][:, col(j, NE)], [(tile[21][:, col(j)], WM0[:, m0["router"]:m0["router"] + NE])])
                ins.then_inc(b_logits.handle, 1)

            over_batches(pe, pe_b)

            def pe_moe(key, n, W, at, first_name, second_name):
                gu, acted, hid, down, total = moe_sems[key]

                def body(b, first):
                    for e in range(n + 1):
                        for c in range(HC if e < n else 0):
                            for m, name in enumerate((first_name, second_name)):
                                if e:
                                    before = acted if m == 0 else hid
                                    pe.wait_ge(before.handle, before.at(b, HC * (e - 1) + c + 1))
                                elif not first:
                                    pe.wait_ge(hid.handle, hid.before(b))
                                w = at[name] + HID * e + P * c
                                product(ps[2 * c + m][:], [(W[:, w:w + P], XF[:, b])]).then_inc(gu.handle, 1)
                        if e:
                            downs(b, first, e - 1)

                def downs(b, first, e):
                    pe.wait_ge(hid.handle, hid.at(b, HC * (e + 1)))
                    if e >= 2:
                        pe.wait_ge(total.handle, total.at(b, e - 1))
                    elif not first:
                        pe.wait_ge(total.handle, total.before(b))
                    for j in range(TB):
                        ins = product(ps[4 + e % 2][:, col(j)],
                                      [(tile[2 * (e % 2) + c][:, col(j)], W[:, at["d"] + C * (HC * e + c):at["d"] + C * (HC * e + c + 1)])
                                       for c in range(HC)])
                    ins.then_inc(down.handle, 1)

                return body

            pe.wait_ge(b_cw.handle, b_cw.at(B - 1))
            over_batches(pe, pe_moe("c", NE + 1, WM0, m0, "g", "u"))

            def pe_d(b, first):
                pe.wait_ge(norm_out["pre"].handle, norm_out["pre"].at(b))
                if not first:
                    pe.wait_ge(d_xf.handle, d_xf.before(b))
                transposes(ps[0], tile[2]).then_inc(d_xT.handle, 1)
                for c in range(UC):
                    for m, name in enumerate(("Wk", "Wv", "Wr")):
                        if c == 0:
                            pe.wait_ge(d_mix.handle, d_mix.at(b, m + 1))
                        if c >= 2:
                            if m == 1:
                                pe.wait_ge(d_kv.handle, d_kv.at(b, c - 1))
                            else:
                                pe.wait_ge(d_act.handle, d_act.at(b, 2 * (c - 2) + 1 + m // 2))
                        elif not first and m == 0:
                            pe.wait_ge(d_cw.handle, d_cw.before(b))
                        product(ps[1 + 3 * (c % 2) + m][:], [(w1(name, P, P * c), tile[4 + m][:])]).then_inc(d_kvr.handle, 1)
                pe.wait_ge(d_rw.handle, d_rw.at(b))
                for j in range(TB):
                    ins = product(ps[7][:, col(j)], [(tile[13 + c][:, col(j)], w1("Wo", C, C * c)) for c in range(UC)])
                ins.then_inc(d_o.handle, 1)
                pe.wait_ge(norm_out["post"].handle, norm_out["post"].at(b))
                transposes(ps[0], tile[2]).then_inc(d_x2T.handle, 1)
                pe.wait_ge(d_mix2.handle, d_mix2.at(b))
                for c in range(UC):
                    product(ps[1 + c][:], [(w1("cWk", P, P * c), tile[4][:])]).then_inc(d_kk.handle, 1)
                for j in range(TB):
                    product(ps[6][:, col(j)], [(tile[5][:, col(j)], w1("cWr", C))])
                pe.wait_ge(d_silu.handle, d_silu.at(b))
                for j in range(TB):
                    ins = product(ps[5][:, col(j)], [(tile[18 + c][:, col(j)], w1("cWv", C, C * c)) for c in range(UC)])
                ins.then_inc(d_o2.handle, 1)
                pe.wait_ge(norm_out["ffn1"].handle, norm_out["ffn1"].at(b))
                transposes(ps[0], tile[2]).then_inc(d_x3T.handle, 1)
                pe.wait_ge(d_xf.handle, d_xf.at(b))
                for j in range(TB):
                    ins = product(ps[7][:, col(j, NE)], [(tile[3][:, col(j)], WM1[:, m1["router"]:m1["router"] + NE])])
                ins.then_inc(d_logits.handle, 1)
                pe.wait_ge(d_sel.handle, d_sel.at(b))
                for j in range(TB):
                    product(ps[1][:, col(j, NE)], [(ONES[:], R[1][:, i]) for i in range(j)] + [(TRI[:], R[1][:, j])])
                product(ps[1][:, col(TB, NE)], [(ONES[:], R[1][:, i]) for i in range(TB)]).then_inc(d_pos.handle, 1)

            over_batches(pe, pe_d)
            pe.wait_ge(d_cw.handle, d_cw.at(B - 1))
            over_batches(pe, pe_moe("e", NE, WM1, m1, "in", "gate"))


def kernel(**inputs):
    import numpy as _np
    import concourse.bacc as _bacc
    from concourse import mybir as _mybir
    from concourse.bass_utils import run_bass_kernel_spmd as _run

    i = {k: _np.asarray(a) for k, a in inputs.items()}
    a0 = lambda n: i["L0_attn_" + n]
    f0 = lambda n: i["L0_ffn_" + n]
    a1 = lambda n: i["L1_attn_" + n]
    f1 = lambda n: i["L1_ffn_" + n]

    def rows(w):
        return w.reshape(-1, P, w.shape[1]).transpose(1, 0, 2).reshape(P, -1)

    def side(ws):
        return _np.concatenate(list(ws), axis=1)

    f32 = _np.float32
    steps = _np.arange(P)
    level = _np.stack([((steps[:, None] >> (lv + 1)) == (steps[None] >> (lv + 1)))
                       & ((steps[:, None] >> lv) % 2 == 0) & ((steps[None] >> lv) % 2 == 1) for lv in range(LEVELS)], 1)
    x = a0("x").reshape(B, TB, P, C).transpose(2, 0, 1, 3)
    arrays = {
        "x": x,
        "attn0": side([a0("A"), a0("Bp")[:4].reshape(4 * LR, C), a0("tdA"), a0("Wk").T, a0("Wv").T, a0("Wr").T,
                       a0("Wo").T, a0("Wg1"), a0("Wg2")[:P]]),
        "tdB": a0("tdB"),
        "bp4": a0("Bp")[4],
        "wg2b": a0("Wg2")[P:],
        "moe0": side([f0("sg").T, *(w.T for w in f0("eg")), f0("su").T, *(w.T for w in f0("eu")),
                      rows(f0("sd").T), *(rows(w.T) for w in f0("ed")), f0("router_w").T]),
        "attn1": side([a1("tm_Wk"), a1("tm_Wv"), a1("tm_Wr"), rows(a1("tm_Wo")), a1("cm_Wk"), rows(a1("cm_Wv")),
                       a1("cm_Wr")]),
        "lnrow": _np.broadcast_to(_np.stack([a1("ln0_g"), a1("ln0_b")]), (P, 2, C)),
        "dfvec": _np.stack([a1("tm_decay").reshape(UC, P).T, a1("tm_first").reshape(UC, P).T], 1),
        "vecs": _np.stack([a0("miu_x").reshape(C), *a0("lam").reshape(NS, C), a0("td_miu").reshape(C), a0("u").reshape(C),
                           a0("gamma"), a0("beta"), a1("pre_g"), a1("pre_b"), a1("post_g"), a1("post_b"),
                           a1("tm_mix_k"), a1("tm_mix_v"), a1("tm_mix_r"), a1("cm_mix_k"), a1("cm_mix_r")], 1),
        "moe1": side([*(w[:, :HID] for w in f1("W1")), *(w[:, HID:] for w in f1("W1")), *(rows(w) for w in f1("W2")),
                      f1("Wg").T]),
        "ident": _np.eye(P, dtype=f32),
        "levels": level.astype(_np.int32),
        "tri": _np.triu(_np.ones((P, P), f32), 1),
        "iota": _np.broadcast_to(_np.arange(NE, dtype=f32), (P, 1, NE)),
    }
    nc = _bacc.Bacc("TRN2", target_bir_lowering=False, num_devices=1)
    arrays = {f"in_{k}": _np.ascontiguousarray(a) for k, a in arrays.items()}
    args = [nc.dram_tensor(k, a.shape, _mybir.dt.from_np(a.dtype), kind="ExternalInput").ap() for k, a in arrays.items()]
    args.append(nc.dram_tensor("out_0", (B, P, TB, C), F32, kind="ExternalOutput").ap())
    build(nc, *args)
    r = _run(nc, [arrays], core_ids=[0])
    return r.results[0]["out_0"].transpose(0, 2, 1, 3).reshape(B, T, C)
```

```python
from contextlib import ExitStack

import concourse.bass as bass
from concourse import mybir

P = 128
B = 8
T = 512
TB = T // P
C = 128
HEAD = 64
NH = C // HEAD
NE = 8
HID = 256
HC = HID // P
HU = 512
UC = HU // P
NS = 5
LR = 32
CAP = int(B * T * 2 * 1.25 / NE)
EPS = 1e-5
K_CLAMP = 60.0
K_EPS = 1e-8
E_CLAMP = 1.1420073898156842e26

F32 = mybir.dt.float32
U32 = mybir.dt.uint32
I32 = mybir.dt.int32
ALU = mybir.AluOpType
ACT = mybir.ActivationFunctionType
AX = mybir.AxisListType

ATTN0 = [("A", NS * LR), ("Bp", C), ("tdA", HEAD), ("WkT", C), ("WvT", C), ("WrT", C), ("WoT", C),
         ("Wg1", 160), ("Wg2a", C)]
MOE0 = [("g", 9 * HID), ("u", 9 * HID), ("d", 9 * HC * C), ("router", NE)]
ATTN1 = [("Wk", HU), ("Wv", HU), ("Wr", HU), ("Wo", UC * C), ("cWk", HU), ("cWv", UC * C), ("cWr", C)]
MOE1 = [("in", NE * HID), ("gate", NE * HID), ("d", NE * HC * C), ("router", NE)]
VECS = ["miu_x", "lam0", "lam1", "lam2", "lam3", "lam4", "td_miu", "u", "gamma", "beta",
        "pre_g", "pre_b", "post_g", "post_b", "mix_k", "mix_v", "mix_r", "cmix_k", "cmix_r"]
NV = len(VECS)
NORMS = ("attn0", "heads", "ffn0", "attn1", "ln0", "pre", "post", "ffn1")
LEVELS = 7

SLOTS_B = (2, 2, 2, 1, 2, 1, 1, 1, 1, 1, 1, 1, 1, 1, 1, 3, 2, 3, 2)
SLOTS_D = (3, 3, 2, 1, 1, 1, 1, 2, 2, 2, 1, 2, 1, 0, 1, 1, 2)


def columns(parts):
    at, out = 0, {}
    for name, n in parts:
        out[name] = at
        at += n
    return out, at


class Sem:

    def __init__(self, handle, per):
        self.handle, self.per = handle, per

    def at(self, b, k=None):
        return b * self.per + (self.per if k is None else k)

    def before(self, b, k=None):
        return (b - 1) * self.per + (self.per if k is None else k)


class Chain:

    def __init__(self, eng, handle):
        self.eng, self.handle, self.per, self.b, self.k = eng, handle, 0, 0, 0

    def start(self, b, first):
        self.per = self.per if first else max(self.per, self.k)
        self.b, self.k = b, 0

    def step(self, ins):
        ins.then_inc(self.handle, 1)
        self.k += 1
        self.eng.wait_ge(self.handle, self.b * self.per + self.k)


def build(nc, x, attn0, tdB, bp4, wg2b, moe0, attn1, lnrow, dfvec, vecs, moe1, ident, levels, tri, iota, hsel, out):
    a0, na0 = columns(ATTN0)
    m0, nm0 = columns(MOE0)
    a1, na1 = columns(ATTN1)
    m1, nm1 = columns(MOE1)
    with ExitStack() as ctx:
        def sb(name, shape, dt=F32):
            return ctx.enter_context(nc.sbuf_tensor(name, shape, dt))

        def sem(name, per=1):
            return Sem(ctx.enter_context(nc.semaphore(name)), per)

        W0 = sb("W0", [P, na0])
        TDB = sb("TDB", [HEAD, C])
        BP4 = sb("BP4", [LR, C])
        WG2B = sb("WG2B", [LR, C])
        WM0 = sb("WM0", [P, nm0])
        W1 = sb("W1", [P, na1])
        WM1 = sb("WM1", [P, nm1])
        LNR = sb("LNR", [P, 2, C])
        DF = sb("DF", [P, 2, UC])
        V = sb("V", [P, NV])
        ID = sb("ID", [P, P])
        MASK = sb("MASK", [P, LEVELS, HEAD], I32)
        HSEL = sb("HSEL", [P, NH])
        TRI = sb("TRI", [P, P])
        IOTA = sb("IOTA", [P, 1, NE])
        ONES = sb("ONES", [P, P])
        CON = sb("CON", [P, 3, NE])
        DEC = sb("DEC", [P, 2, UC])
        DTMP = sb("DTMP", [P, UC])

        X = sb("X", [P, B, TB, C])
        XN = sb("XN", [P, B, T + 1])
        XF = XN[:, :, 1:T + 1]
        CW = sb("CW", [P, B, TB, NE])

        ST = sb("ST", [P, TB * NH, 6])
        MV = sb("MV", [P, TB * NH, 2])
        VE = sb("VE", [P, TB * NH])
        RS = sb("RS", [P, TB * NH])
        tile = [sb(f"tile{n}", [P, T]) for n in range(22)]
        acted = [sb(f"acted{c}", [P, T]) for c in range(HC)]
        hidden = [[sb(f"hidden{n}{c}", [P, T]) for c in range(HC)] for n in range(2)]
        DSC = sb("DSC", [P, TB * NH])
        XP = [sb(f"XP{n}", [P, T + 1]) for n in range(2)]
        SKP = [sb(f"SKP{n}", [P, T + 1]) for n in range(2)]
        AT = sb("AT", [P, NH, TB, P])
        D = [sb(f"D{n}", [P, T >> n]) for n in range(1, LEVELS + 1)]
        S4 = sb("S4", [P, TB, C])
        HS = sb("HS", [P, TB, NS * LR])
        R = [sb(f"R{n}", [P, TB, NE]) for n in range(6)]
        M8 = sb("M8", [P, TB, NE])
        I8 = sb("I8", [P, TB, NE], U32)
        IF = sb("IF", [P, TB, 2])
        R4 = [sb(f"R4{n}", [P, TB, 1]) for n in range(4)]
        W2 = sb("W2", [P, TB, 2])
        CARRY = sb("CARRY", [P, 1, NE])

        ps = [ctx.enter_context(nc.psum_tensor(f"bank{n}", [P, T], F32)) for n in range(8)]
        h_dram = nc.dram_tensor("h_scratch", [B * T * NS, LR], F32, kind="Internal").ap()

        def v(name):
            return V[:, VECS.index(name):VECS.index(name) + 1]

        def blk(ap):
            return ap.rearrange("p (a c) -> p a c", c=P)

        def col(j, n=P):
            return slice(n * j, n * (j + 1))

        def w0(name, n, at=0):
            return W0[:, a0[name] + at:a0[name] + at + n]

        def w1(name, n, at=0):
            return W1[:, a1[name] + at:a1[name] + at + n]

        x_in, w_in, later_in, const, dec, fences = (sem(n) for n in ("x_in", "w_in", "later_in", "const", "dec", "fences"))
        dve_chain, dve_chain_a, dve_chain_b = sem("dve_chain"), sem("dve_chain_a"), sem("dve_chain_b")
        norm_rstd = {n: sem(f"{n}_rstd") for n in NORMS}
        norm_moments = {n: sem(f"{n}_moments") for n in NORMS}
        norm_var_eps = {n: sem(f"{n}_var_eps") for n in NORMS}
        norm_out = {n: sem(f"{n}_out") for n in NORMS}
        a_xT, a_xn, a_xx, a_store = sem("a_xT"), sem("a_xn"), sem("a_xx"), sem("a_store", 16)
        a_h, a_tanh = sem("a_h", 2), sem("a_tanh", 2)
        b_load = sem("b_load", 16 * TB)
        b_hT, b_hTs, b_miu, b_mixed, b_x5 = sem("b_hT"), sem("b_hTs", 2), sem("b_miu", NS), sem("b_mixed", NS), sem("b_x5", NS)
        b_td, b_tdt, b_w, b_d, b_k, b_kd = (sem(n) for n in ("b_td", "b_tdt", "b_w", "b_d", "b_k", "b_kd"))
        b_v, b_vs, b_r, b_rs, b_ru = (sem(n) for n in ("b_v", "b_vs", "b_r", "b_rs", "b_ru"))
        b_ruk, b_dsc = sem("b_ruk"), sem("b_dsc")
        b_g1, b_g1t, b_g2, b_gs = sem("b_g1"), sem("b_g1t", 2), sem("b_g2"), sem("b_gs")
        b_level, b_scaled, b_put = sem("b_level", LEVELS), sem("b_scaled", 3 * LEVELS), sem("b_put", LEVELS + 1)
        b_kT, b_kTs, b_u, b_state, b_y = sem("b_kT"), sem("b_kTs"), sem("b_u"), sem("b_state", TB - 1), sem("b_y")
        b_ynT, b_yg, b_z, b_o, b_res = sem("b_ynT"), sem("b_yg"), sem("b_z"), sem("b_o"), sem("b_res")
        b_xT, b_xf, b_logits, b_shift, b_exp, b_cw = (sem(n) for n in ("b_xT", "b_xf", "b_logits", "b_shift", "b_exp", "b_cw"))
        moe_sems = {k: [sem(f"{k}_gu", 4 * n), sem(f"{k}_act", HC * n), sem(f"{k}_hid", HC * n),
                        sem(f"{k}_down", n), sem(f"{k}_sum", n)] for k, n in (("c", NE + 1), ("e", NE))}
        d_aff, d_xT, d_xn, d_mix = sem("d_aff", 2), sem("d_xT"), sem("d_xn"), sem("d_mix", 3)
        d_kvr, d_act, d_kv, d_rw, d_o, d_x1 = sem("d_kvr", 3 * UC), sem("d_act", 2 * UC), sem("d_kv", UC), sem("d_rw", UC), sem("d_o"), sem("d_x1")
        d_clip, d_sgm, d_sums, d_wk, d_den, d_quot = (sem(n, UC) for n in ("d_clip", "d_sgm", "d_sums", "d_wk", "d_den", "d_quot"))
        d_x2T, d_xn2, d_mix2, d_kk, d_silu = sem("d_x2T"), sem("d_xn2"), sem("d_mix2", 2), sem("d_kk", UC), sem("d_silu", UC)
        d_o2, d_sg, d_sig = sem("d_o2"), sem("d_sg"), sem("d_sig")
        d_x3T, d_xf, d_logits, d_gap, d_exp, d_sel, d_pos, d_cw = (
            sem(n) for n in ("d_x3T", "d_xf", "d_logits", "d_gap", "d_exp", "d_sel", "d_pos", "d_cw"))
        stored = sem("stored", 16)

        block = ctx.enter_context(nc.Block())

        def over_batches(eng, body):
            body(0, True)
            with eng.Fori(1, B) as b:
                body(b, False)

        def in_step(eng, block, experts, slots):
            at = [sum(slots[:n]) for n in range(len(slots) + 1)]
            block(0, True, lambda slot: None)
            block(1, False, lambda slot: experts(0, True, at[slot], at[slot + 1]))
            with eng.Fori(2, B) as b:
                block(b, False, lambda slot: experts(b - 1, False, at[slot], at[slot + 1]))
            if len(slots) > 1:
                experts(B - 1, False, 0, at[-1])

        def expert_item(k):
            return (k // 3, (k % 3) // 2, False) if k % 3 != 1 else (k // 3 - 1, None, True)

        MIU = (2, 3, 4, 0, 1)
        LEVEL_BANKS = ((0, 1), (2, 4))
        G, U, DN = 5, 6, 7

        def fence(eng):
            eng.sem_inc(fences.handle, 1)

        WEIGHTS = ((ID, ident), (V, vecs), (W0, attn0), (TDB, tdB), (BP4, bp4), (WG2B, wg2b), (MASK, levels),
                   (HSEL, hsel), (IOTA, iota))
        LATER = ((WM0, moe0), (W1, attn1), (LNR, lnrow), (DF, dfvec), (TRI, tri), (WM1, moe1))
        N_CONST = 8 + len(XP) + len(SKP)
        ALL_W = 16 * len(WEIGHTS)
        ALL_LATER = 16 * len(LATER)

        @block.sync
        def _(sp):
            sp.dma_start(X[:], x).then_inc(x_in.handle, 16)
            for dst, src in WEIGHTS:
                sp.dma_start(dst[:], src).then_inc(w_in.handle, 16)
            for dst, src in LATER:
                sp.dma_start(dst[:], src).then_inc(later_in.handle, 16)

            def store_h(b, first):
                sp.wait_ge(a_tanh.handle, a_tanh.at(b))
                sp.dma_start(h_dram.rearrange("(b j p s) k -> b p j (s k)", p=P, j=TB, s=NS)[b], HS[:])\
                    .then_inc(a_store.handle, 16)

            over_batches(sp, store_h)
            sp.wait_ge(a_store.handle, a_store.at(B - 1))

            def load_h(b, first):
                if not first:
                    sp.wait_ge(b_hT.handle, b_hT.before(b))
                src = h_dram.rearrange("(s b j p) k -> b j p s k", p=P, j=TB, s=NS)[b]
                for j in range(TB):
                    sp.dma_start(HS[:, j].rearrange("p (s k) -> p s k", s=NS), src[j]).then_inc(b_load.handle, 16)

            over_batches(sp, load_h)
            done = moe_sems["e"][4]

            def store_out(b, first):
                sp.wait_ge(done.handle, done.at(b))
                sp.dma_start(out[b], X[:, b]).then_inc(stored.handle, 16)

            over_batches(sp, store_out)
            sp.wait_ge(stored.handle, stored.at(B - 1))

        @block.gpsimd
        def _(pool):
            pool.memset(ONES[:], 1.0).then_inc(const.handle, 1)
            pool.memset(CON[:, 0], EPS).then_inc(const.handle, 1)
            pool.memset(CON[:, 1], EPS * NH).then_inc(const.handle, 1)
            pool.memset(CON[:, 2], -0.5).then_inc(const.handle, 1)
            pool.memset(XN[:, :, 0:1], 0.0).then_inc(const.handle, 1)
            for z in (*XP, *SKP):
                pool.memset(z[:, 0:1], 0.0).then_inc(const.handle, 1)
            pool.memset(S4[:], 0.0).then_inc(const.handle, 1)
            pool.memset(CARRY[:], 0.0).then_inc(const.handle, 1)
            pool.memset(R4[3][:], 0.0).then_inc(const.handle, 1)
            pool.wait_ge(const.handle, N_CONST)

            def rstd(b, name, n=TB, eps=0):
                pool.wait_ge(norm_moments[name].handle, norm_moments[name].at(b))
                pool.tensor_tensor(VE[:, 0:n], MV[:, 0:n, 1], CON[:, eps, 0:n], ALU.add).then_inc(norm_var_eps[name].handle, 1)
                pool.wait_ge(norm_var_eps[name].handle, norm_var_eps[name].at(b))
                pool.tensor_tensor(RS[:, 0:n], VE[:, 0:n], CON[:, 2, 0:n], ALU.pow).then_inc(norm_rstd[name].handle, 1)

            over_batches(pool, lambda b, first: rstd(b, "attn0"))

            def pool_b(b, first):
                for s in range(NS):
                    pool.wait_ge(b_mixed.handle, b_mixed.at(b, s + 1))
                    fence(pool)
                    pool.tensor_tensor(tile[2 + s][:], tile[2 + s][:], XN[:, b, 1:T + 1], ALU.add).then_inc(b_x5.handle, 1)
                pool.wait_ge(b_ru.handle, b_ru.at(b))
                pool.wait_ge(b_kd.handle, b_kd.at(b))
                pool.tensor_tensor(tile[12][:], tile[12][:], tile[9][:], ALU.mult).then_inc(b_ruk.handle, 1)
                rstd(b, "heads", TB * NH, 1)
                pool.wait_ge(b_yg.handle, b_yg.at(b))
                pool.wait_ge(b_gs.handle, b_gs.at(b))
                pool.tensor_tensor(tile[16][:], tile[16][:], tile[15][:], ALU.mult).then_inc(b_z.handle, 1)
                rstd(b, "ffn0")

            over_batches(pool, pool_b)

            def pool_d(b, first):
                rstd(b, "attn1")
                rstd(b, "ln0")
                pool.wait_ge(norm_out["ln0"].handle, norm_out["ln0"].at(b))
                pool.tensor_tensor(blk(tile[1][:]), blk(tile[1][:]), LNR[:, 0:1].to_broadcast([P, TB, C]), ALU.mult)\
                    .then_inc(d_aff.handle, 1)
                pool.wait_ge(d_aff.handle, d_aff.at(b, 1))
                pool.tensor_tensor(blk(tile[1][:]), blk(tile[1][:]), LNR[:, 1:2].to_broadcast([P, TB, C]), ALU.add)\
                    .then_inc(d_aff.handle, 1)
                rstd(b, "pre")

                def factors(c):
                    pool.wait_ge(d_act.handle, d_act.at(b, 2 * c + 2))
                    fence(pool)
                    pool.tensor_scalar(tile[7 + c % 2][:], tile[7 + c % 2][:], E_CLAMP, None, ALU.min)\
                        .then_inc(d_clip.handle, 1)
                    pool.tensor_scalar(tile[13 + c][:], tile[13 + c][:], 0.5, 0.5, ALU.mult, ALU.add).then_inc(d_sgm.handle, 1)

                def denominator(c):
                    pool.wait_ge(d_wk.handle, d_wk.at(b, c + 1))
                    fence(pool)
                    pool.tensor_scalar(tile[11 + c % 2][:], tile[11 + c % 2][:], K_EPS, None, ALU.add).then_inc(d_den.handle, 1)

                def times_sigmoid(c):
                    pool.wait_ge(d_sgm.handle, d_sgm.at(b, c + 1))
                    pool.wait_ge(d_quot.handle, d_quot.at(b, c + 1))
                    pool.tensor_tensor(tile[13 + c][:], tile[13 + c][:], tile[11 + c % 2][:], ALU.mult)\
                        .then_inc(d_rw.handle, 1)

                for c in range(UC + 2):
                    if c < UC:
                        factors(c)
                    if 1 <= c <= UC:
                        denominator(c - 1)
                    if c >= 2:
                        times_sigmoid(c - 2)
                rstd(b, "post")
                rstd(b, "ffn1")

            pool.wait_ge(later_in.handle, ALL_LATER)
            over_batches(pool, pool_d)

        @block.vector
        def _(dve):
            chain_a, chain_b, chain_d = (Chain(dve, s.handle) for s in (dve_chain_a, dve_chain_b, dve_chain))

            def norm(b, name, chain, src, dst, n=TB):
                for j in range(n):
                    ins = dve.bn_stats(ST[:, j], src(j))
                chain.step(ins)
                fence(dve)
                for j in range(n):
                    ins = dve.bn_aggr(MV[:, j], ST[:, j])
                ins.then_inc(norm_moments[name].handle, 1)
                dve.wait_ge(norm_rstd[name].handle, norm_rstd[name].at(b))
                for j in range(n):
                    ins = dve.tensor_scalar(dst(j), src(j), MV[:, j, 0:1], RS[:, j:j + 1], ALU.subtract, ALU.mult)
                ins.then_inc(norm_out[name].handle, 1)

            def top_two(chain, probs):
                fence(dve)
                for j in range(TB):
                    ins = dve.max(M8[:, j], probs[:, j])
                chain.step(ins)
                fence(dve)
                for j in range(TB):
                    ins = dve.max_index(I8[:, j], M8[:, j], probs[:, j])
                chain.step(ins)
                chain.step(dve.tensor_copy(IF[:], I8[:, :, 0:2]))
                for k in range(2):
                    ins = dve.tensor_tensor(R[3 + k][:], IOTA[:].to_broadcast([P, TB, NE]),
                                            IF[:, :, k:k + 1].to_broadcast([P, TB, NE]), ALU.is_equal)
                chain.step(ins)

            dve.wait_ge(x_in.handle, 16)
            dve.wait_ge(w_in.handle, ALL_W)
            dve.wait_ge(const.handle, N_CONST)

            def dve_a(b, first):
                chain_a.start(b, first)
                if not first:
                    dve.wait_ge(a_xT.handle, a_xT.before(b))
                    fence(dve)
                norm(b, "attn0", chain_a, lambda j: X[:, b, j], lambda j: tile[0][:, col(j)])
                dve.wait_ge(a_xn.handle, a_xn.at(b))
                if not first:
                    dve.wait_ge(a_h.handle, a_h.before(b))
                chain_a.step(dve.tensor_tensor(tile[1][:], XN[:, b, 0:T], XN[:, b, 1:T + 1], ALU.subtract))
                dve.scalar_tensor_tensor(out=tile[2][:], in0=tile[1][:], scalar=v("miu_x"), in1=XN[:, b, 1:T + 1],
                                         op0=ALU.mult, op1=ALU.add).then_inc(a_xx.handle, 1)

            over_batches(dve, dve_a)

            def dve_experts(key, n, shared):
                gu, act, hid, down, total = moe_sems[key]

                def items(b, first, k0, k1):
                    for k in range(k0, k1):
                        e, c, output = expert_item(k)
                        if output:
                            if e < 0:
                                continue
                            dve.wait_ge(down.handle, down.at(b, e + 1))
                            add(b, e, shared, total)
                        elif e < n:
                            dve.wait_ge(act.handle, act.at(b, HC * e + c + 1))
                            dve.wait_ge(gu.handle, gu.at(b, 4 * e + 2 * c + 2))
                            if e >= 2:
                                dve.wait_ge(down.handle, down.at(b, e - 1))
                            elif not first:
                                dve.wait_ge(down.handle, down.before(b))
                            dve.tensor_tensor(hidden[e % 2][c][:], acted[c][:], ps[U][:], ALU.mult).then_inc(hid.handle, 1)

                return items

            def add(b, e, shared, total):
                if e:
                    dve.wait_ge(total.handle, total.at(b, e))
                if shared and e == 0:
                    ins = dve.tensor_tensor(X[:, b], X[:, b], blk(ps[DN][:]), ALU.add)
                else:
                    for j in range(TB):
                        ins = dve.scalar_tensor_tensor(
                            out=X[:, b, j], in0=ps[DN][:, col(j)], scalar=CW[:, b, j, e - shared:e - shared + 1],
                            in1=X[:, b, j], op0=ALU.mult, op1=ALU.add)
                ins.then_inc(total.handle, 1)

            def dve_b(b, first, slot):
                chain_b.start(b, first)
                if first:
                    dve.wait_ge(a_h.handle, a_h.at(B - 1))
                chain_b.step(dve.tensor_tensor(tile[1][:], XN[:, b, 0:T], XN[:, b, 1:T + 1], ALU.subtract))
                slot(0)
                if not first:
                    dve.wait_ge(b_g1.handle, b_g1.before(b))
                for s in range(NS):
                    dve.wait_ge(b_miu.handle, b_miu.at(b, s + 1))
                    dve.scalar_tensor_tensor(out=tile[2 + s][:], in0=ps[MIU[s]][:], scalar=v(f"lam{s}"), in1=tile[1][:],
                                             op0=ALU.add, op1=ALU.mult).then_inc(b_mixed.handle, 1)
                slot(1)
                slot(2)
                dve.wait_ge(b_d.handle, b_d.at(b))
                dve.wait_ge(b_k.handle, b_k.at(b))
                if not first:
                    dve.wait_ge(b_kT.handle, b_kT.before(b))
                dve.scalar_tensor_tensor(out=tile[9][:], in0=tile[8][:], scalar=1.0, in1=ps[3][:],
                                         op0=ALU.min, op1=ALU.mult).then_inc(b_kd.handle, 1)
                slot(3)
                slot(4)
                slot(5)
                slot(6)
                dprod = tile[8]
                for lv in range(LEVELS):
                    half, nb = 1 << lv, T >> (lv + 1)
                    dve.wait_ge(b_level.handle, b_level.at(b, lv + 1))
                    if lv:
                        dve.wait_ge(b_put.handle, b_put.at(b, lv + 1))
                        dve.wait_ge(b_scaled.handle, b_scaled.at(b, 3 * lv))
                    else:
                        dve.wait_ge(b_ruk.handle, b_ruk.at(b))
                        dve.wait_ge(b_kd.handle, b_kd.at(b))
                    dd = dprod[:].rearrange("p (m two) -> p m two", two=2)
                    for buf, hl, dl in ((tile[9], 0, 1), (tile[10], 1, 0)):
                        part = buf[:].rearrange("p (m two h) -> p m two h", two=2, h=half)[:, :, hl]
                        dve.tensor_tensor(part, part, dd[:, :, dl:dl + 1].to_broadcast([P, nb, half]), ALU.mult)\
                            .then_inc(b_scaled.handle, 1)
                    dve.tensor_tensor(D[lv][:], dd[:, :, 0], dd[:, :, 1], ALU.mult).then_inc(b_scaled.handle, 1)
                    dprod = D[lv]
                    if lv == 0:
                        dve.wait_ge(b_dsc.handle, b_dsc.at(b))
                        chain_b.step(dve.tensor_copy(DSC[:], ps[3][:, 0:TB * NH]))
                        if not first:
                            dve.wait_ge(b_y.handle, b_y.before(b))
                        for c in range(TB):
                            for n in range(NH):
                                ins = dve.tensor_scalar(AT[:, n, c], ID[:], DSC[:, NH * c + n:NH * c + n + 1], None, ALU.mult)
                        ins.then_inc(b_put.handle, 1)
                        dve.wait_ge(b_put.handle, b_put.at(b, 1))
                        fence(dve)
                    mask = MASK[:, lv:lv + 1].rearrange("p a (m h) -> p a m h", h=half)\
                        .to_broadcast([P, TB, HEAD // half, half])
                    for n in range(NH):
                        right = AT[:, n].rearrange("p c (m two h) -> p c m two h", two=2, h=half)[:, :, :, 1]
                        fresh = ps[LEVEL_BANKS[lv % 2][n]][:, 0:TB * HEAD].rearrange("p (c m h) -> p c m h", c=TB, h=half)
                        ins = dve.copy_predicated(right, mask, fresh)
                    ins.then_inc(b_put.handle, 1)
                    if lv:
                        slot(6 + lv)
                slot(13)
                dve.wait_ge(b_u.handle, b_u.at(b))
                dve.wait_ge(b_scaled.handle, b_scaled.at(b))
                for c in range(1, TB):
                    if c > 1:
                        dve.wait_ge(b_state.handle, b_state.at(b, c - 1))
                    for n in range(NH):
                        h = slice(HEAD * n, HEAD * (n + 1))
                        new, u = S4[h, c, h], ps[4][h, P * (c - 1) + HEAD * n:P * (c - 1) + HEAD * (n + 1)]
                        if c == 1:
                            ins = dve.tensor_copy(new, u)
                        else:
                            ins = dve.scalar_tensor_tensor(out=new, in0=S4[h, c - 1, h], scalar=D[LEVELS - 1][h, c - 1:c],
                                                           in1=u, op0=ALU.mult, op1=ALU.add)
                    ins.then_inc(b_state.handle, 1)
                slot(14)
                dve.wait_ge(b_y.handle, b_y.at(b))
                if not first:
                    dve.wait_ge(b_ynT.handle, b_ynT.before(b))
                norm(b, "heads", chain_b, lambda j: ps[3][:, col(j, HEAD)], lambda j: tile[14][:, col(j, HEAD)], TB * NH)
                slot(15)
                slot(16)
                dve.wait_ge(b_o.handle, b_o.at(b))
                chain_b.step(dve.tensor_tensor(X[:, b], X[:, b], blk(ps[2][:]), ALU.add))
                fence(dve)
                norm(b, "ffn0", chain_b, lambda j: X[:, b, j], lambda j: tile[17][:, col(j)])
                slot(17)
                dve.wait_ge(b_logits.handle, b_logits.at(b))
                logits = ps[3][:, 0:TB * NE].rearrange("p (j e) -> p j e", e=NE)
                chain_b.step(dve.tensor_reduce(R4[0][:], logits, AX.X, ALU.max))
                dve.tensor_tensor(R[0][:], logits, R4[0][:].to_broadcast([P, TB, NE]), ALU.subtract).then_inc(b_shift.handle, 1)
                slot(18)
                dve.wait_ge(b_exp.handle, b_exp.at(b))
                chain_b.step(dve.tensor_reduce(R4[1][:], R[1][:], AX.X, ALU.add))
                chain_b.step(dve.reciprocal(R4[2][:], R4[1][:]))
                chain_b.step(dve.tensor_tensor(R[2][:], R[1][:], R4[2][:].to_broadcast([P, TB, NE]), ALU.mult))
                top_two(chain_b, R[2])
                chain_b.step(dve.tensor_tensor(R4[1][:], M8[:, :, 0:1], M8[:, :, 1:2], ALU.add))
                chain_b.step(dve.reciprocal(R4[2][:], R4[1][:]))
                chain_b.step(dve.tensor_tensor(W2[:], M8[:, :, 0:2], R4[2][:].to_broadcast([P, TB, 2]), ALU.mult))
                for k in range(2):
                    ins = dve.tensor_tensor(R[k][:], R[3 + k][:], W2[:, :, k:k + 1].to_broadcast([P, TB, NE]), ALU.mult)
                chain_b.step(ins)
                dve.tensor_tensor(CW[:, b], R[0][:], R[1][:], ALU.add).then_inc(b_cw.handle, 1)

            in_step(dve, dve_b, dve_experts("c", NE + 1, 1), SLOTS_B)

            def dve_d(b, first, slot):
                step = chain_d.step
                chain_d.start(b, first)
                summed = moe_sems["c"][4]
                if first:
                    dve.wait_ge(summed.handle, summed.at(B - 1))
                    fence(dve)
                norm(b, "attn1", chain_d, lambda j: X[:, b, j], lambda j: tile[0][:, col(j)])
                slot(0)
                dve.wait_ge(norm_out["attn1"].handle, norm_out["attn1"].at(b))
                fence(dve)
                norm(b, "ln0", chain_d, lambda j: tile[0][:, col(j)], lambda j: tile[1][:, col(j)])
                slot(1)
                dve.wait_ge(d_aff.handle, d_aff.at(b))
                fence(dve)
                norm(b, "pre", chain_d, lambda j: tile[1][:, col(j)], lambda j: tile[2][:, col(j)])
                slot(2)
                dve.wait_ge(d_xn.handle, d_xn.at(b))
                step(dve.tensor_tensor(tile[3][:], XP[0][:, 1:T + 1], XP[0][:, 0:T], ALU.subtract))
                for n, name in enumerate(("mix_k", "mix_v", "mix_r")):
                    dve.scalar_tensor_tensor(out=tile[4 + n][:], in0=tile[3][:], scalar=v(name), in1=XP[0][:, 0:T],
                                             op0=ALU.mult, op1=ALU.add).then_inc(d_mix.handle, 1)
                slot(3)

                def sums(c):
                    kx, kv, wk = (tile[i + c % 2][:] for i in (7, 9, 11))
                    first_c, decay_c = DEC[:, 1, c:c + 1], DEC[:, 0, c:c + 1]
                    dve.wait_ge(d_clip.handle, d_clip.at(b, c + 1))
                    dve.wait_ge(d_kvr.handle, d_kvr.at(b, 3 * c + 2))
                    if c >= 2:
                        dve.wait_ge(d_quot.handle, d_quot.at(b, c - 1))
                    dve.tensor_tensor(kv, kx, ps[2][:], ALU.mult).then_inc(d_kv.handle, 1)
                    dve.wait_ge(d_kv.handle, d_kv.at(b, c + 1))
                    for m, val in enumerate((kx, kv)):
                        ins = dve.tensor_tensor_scan(SKP[m][:, 1:T + 1], decay_c.to_broadcast([P, T]), val, 0.0,
                                                     ALU.mult, ALU.add)
                    step(ins)
                    if c >= 2:
                        dve.wait_ge(d_rw.handle, d_rw.at(b, c - 1))
                    elif not first:
                        dve.wait_ge(d_rw.handle, d_rw.before(b))
                    dve.scalar_tensor_tensor(out=wk, in0=kx, scalar=first_c, in1=SKP[0][:, 0:T],
                                             op0=ALU.mult, op1=ALU.add).then_inc(d_wk.handle, 1)
                    dve.scalar_tensor_tensor(out=kv, in0=kv, scalar=first_c, in1=SKP[1][:, 0:T],
                                             op0=ALU.mult, op1=ALU.add).then_inc(d_sums.handle, 1)

                def quotient(c):
                    kv, wk = tile[9 + c % 2][:], tile[11 + c % 2][:]
                    dve.wait_ge(d_den.handle, d_den.at(b, c + 1))
                    step(dve.reciprocal(wk, wk))
                    dve.wait_ge(d_sums.handle, d_sums.at(b, c + 1))
                    dve.tensor_tensor(wk, kv, wk, ALU.mult).then_inc(d_quot.handle, 1)

                slot(4)
                sums(0)
                slot(5)
                sums(1)
                slot(6)
                quotient(0)
                sums(2)
                slot(7)
                quotient(1)
                sums(3)
                slot(8)
                quotient(2)
                slot(9)
                quotient(3)
                slot(10)
                dve.wait_ge(d_o.handle, d_o.at(b))
                dve.tensor_tensor(tile[1][:], tile[1][:], ps[4][:], ALU.add).then_inc(d_x1.handle, 1)
                dve.wait_ge(d_x1.handle, d_x1.at(b))
                fence(dve)
                norm(b, "post", chain_d, lambda j: tile[1][:, col(j)], lambda j: tile[2][:, col(j)])
                slot(11)
                dve.wait_ge(d_xn2.handle, d_xn2.at(b))
                step(dve.tensor_tensor(tile[3][:], XP[1][:, 1:T + 1], XP[1][:, 0:T], ALU.subtract))
                for n, name in enumerate(("cmix_k", "cmix_r")):
                    dve.scalar_tensor_tensor(out=tile[4 + n][:], in0=tile[3][:], scalar=v(name), in1=XP[1][:, 0:T],
                                             op0=ALU.mult, op1=ALU.add).then_inc(d_mix2.handle, 1)
                slot(12)
                slot(13)
                dve.wait_ge(d_sig.handle, d_sig.at(b))
                step(dve.tensor_scalar(tile[17][:], tile[17][:], 0.5, 0.5, ALU.mult, ALU.add))
                dve.wait_ge(d_o2.handle, d_o2.at(b))
                step(dve.tensor_tensor(tile[17][:], tile[17][:], ps[0][:], ALU.add))
                step(dve.tensor_tensor(tile[17][:], tile[17][:], tile[1][:], ALU.add))
                step(dve.tensor_tensor(X[:, b], X[:, b], blk(tile[17][:]), ALU.add))
                fence(dve)
                norm(b, "ffn1", chain_d, lambda j: X[:, b, j], lambda j: tile[2][:, col(j)])
                slot(14)
                slot(15)
                dve.wait_ge(d_logits.handle, d_logits.at(b))
                logits = ps[2][:, 0:TB * NE].rearrange("p (j e) -> p j e", e=NE)
                step(dve.tensor_copy(R[0][:], logits))
                top_two(chain_d, R[0])
                dve.tensor_tensor(R[1][:], R[3][:], R[4][:], ALU.add).then_inc(d_sel.handle, 1)
                dve.tensor_tensor(W2[:], M8[:, :, 0:2], M8[:, :, 0:1].to_broadcast([P, TB, 2]), ALU.subtract)\
                    .then_inc(d_gap.handle, 1)
                slot(16)
                dve.wait_ge(d_exp.handle, d_exp.at(b))
                step(dve.tensor_tensor(R4[0][:], W2[:, :, 0:1], W2[:, :, 1:2], ALU.add))
                step(dve.reciprocal(R4[1][:], R4[0][:]))
                step(dve.tensor_tensor(W2[:], W2[:], R4[1][:].to_broadcast([P, TB, 2]), ALU.mult))
                for k in range(2):
                    ins = dve.tensor_tensor(R[3 + k][:], R[3 + k][:], W2[:, :, k:k + 1].to_broadcast([P, TB, NE]), ALU.mult)
                step(ins)
                step(dve.tensor_tensor(R[2][:], R[3][:], R[4][:], ALU.add))
                dve.wait_ge(d_pos.handle, d_pos.at(b))
                pos = ps[3][:, 0:TB * NE].rearrange("p (j e) -> p j e", e=NE)
                step(dve.tensor_tensor(R[5][:], pos, CARRY[:].to_broadcast([P, TB, NE]), ALU.add))
                step(dve.tensor_scalar(R[5][:], R[5][:], float(CAP), None, ALU.is_lt))
                step(dve.tensor_tensor(CARRY[:, 0], CARRY[:, 0], ps[3][:, TB * NE:(TB + 1) * NE], ALU.add))
                dve.tensor_tensor(CW[:, b], R[2][:], R[5][:], ALU.mult).then_inc(d_cw.handle, 1)

            dve.wait_ge(dec.handle, 3)
            in_step(dve, dve_d, dve_experts("e", NE, 0), SLOTS_D)

        @block.scalar
        def _(act):
            act.wait_ge(w_in.handle, ALL_W)
            def act_a(b, first):
                act.wait_ge(a_xT.handle, a_xT.at(b))
                fence(act)
                act.activation(XN[:, b, 1:T + 1], ps[0][:], ACT.Copy).then_inc(a_xn.handle, 1)
                for q in range(2):
                    act.wait_ge(a_h.handle, a_h.at(b, q + 1))
                    if not first:
                        act.wait_ge(a_store.handle, a_store.before(b))
                    act.activation(HS[:, 2 * q:2 * q + 2].rearrange("p j k -> p (j k)"), ps[1 + q][:, 0:2 * NS * LR], ACT.Tanh)\
                        .then_inc(a_tanh.handle, 1)

            over_batches(act, act_a)

            def act_experts(key, n, func):
                gu, act_done, hid, down, total = moe_sems[key]

                def items(b, first, k0, k1):
                    for k in range(k0, k1):
                        e, c, output = expert_item(k)
                        if output or e >= n:
                            continue
                        act.wait_ge(gu.handle, gu.at(b, 4 * e + 2 * c + 1))
                        if e:
                            act.wait_ge(hid.handle, hid.at(b, HC * (e - 1) + c + 1))
                        elif not first:
                            act.wait_ge(hid.handle, hid.before(b))
                        act.activation(acted[c][:], ps[G][:], func).then_inc(act_done.handle, 1)

                return items

            def act_b(b, first, slot):
                act.wait_ge(b_hT.handle, b_hT.at(b))
                if not first:
                    act.wait_ge(b_miu.handle, b_miu.before(b))
                act.activation(tile[0][:], ps[0][:], ACT.Copy).then_inc(b_hTs.handle, 1)
                act.activation(tile[7][0:LR], ps[1][0:LR], ACT.Copy).then_inc(b_hTs.handle, 1)
                slot(0)
                slot(1)
                act.wait_ge(b_td.handle, b_td.at(b))
                act.activation(tile[11][0:HEAD], ps[2][0:HEAD], ACT.Tanh).then_inc(b_tdt.handle, 1)
                act.wait_ge(b_v.handle, b_v.at(b))
                act.activation(tile[13][:], ps[4][:], ACT.Copy).then_inc(b_vs.handle, 1)
                slot(2)
                act.wait_ge(b_w.handle, b_w.at(b))
                act.activation(tile[8][:], ps[2][:], ACT.Exp, bias=v("td_miu")).then_inc(b_d.handle, 1)
                act.wait_ge(b_r.handle, b_r.at(b))
                act.activation(tile[10][:], ps[0][:], ACT.Copy).then_inc(b_rs.handle, 1)
                act.activation(tile[12][:], ps[0][:], ACT.Identity, scale=v("u")).then_inc(b_ru.handle, 1)
                slot(3)
                act.wait_ge(b_g1.handle, b_g1.at(b))
                act.activation(tile[18][:], ps[1][:], ACT.Tanh).then_inc(b_g1t.handle, 1)
                act.activation(tile[19][0:LR], ps[4][0:LR], ACT.Tanh).then_inc(b_g1t.handle, 1)
                slot(4)
                act.wait_ge(b_g2.handle, b_g2.at(b))
                if not first:
                    act.wait_ge(b_z.handle, b_z.before(b))
                act.activation(tile[15][:], ps[2][:], ACT.Copy).then_inc(b_gs.handle, 1)
                for s in range(5, 13):
                    slot(s)
                act.wait_ge(b_kT.handle, b_kT.at(b))
                act.activation(tile[20][:], ps[3][:], ACT.Copy).then_inc(b_kTs.handle, 1)
                slot(13)
                slot(14)
                slot(15)
                act.wait_ge(b_ynT.handle, b_ynT.at(b))
                if not first:
                    act.wait_ge(b_o.handle, b_o.before(b))
                act.activation(tile[16][:], ps[0][:], ACT.Identity, scale=v("gamma"), bias=v("beta")).then_inc(b_yg.handle, 1)
                slot(16)
                slot(17)
                act.wait_ge(b_xT.handle, b_xT.at(b))
                fence(act)
                act.activation(XN[:, b, 1:T + 1], ps[1][:], ACT.Copy)
                act.activation(tile[21][:], ps[1][:], ACT.Copy).then_inc(b_xf.handle, 1)
                slot(18)
                act.wait_ge(b_shift.handle, b_shift.at(b))
                act.activation(R[1][:], R[0][:], ACT.Exp).then_inc(b_exp.handle, 1)

            in_step(act, act_b, act_experts("c", NE + 1, ACT.Silu), SLOTS_B)
            act.wait_ge(later_in.handle, ALL_LATER)
            act.activation(DTMP[:], DF[:, 0], ACT.Exp).then_inc(dec.handle, 1)
            act.wait_ge(dec.handle, 1)
            act.activation(DEC[:, 0], DTMP[:], ACT.Exp, scale=-1.0).then_inc(dec.handle, 1)
            act.activation(DEC[:, 1], DF[:, 1], ACT.Exp).then_inc(dec.handle, 1)

            def act_d(b, first, slot):
                slot(0)
                slot(1)
                slot(2)
                act.wait_ge(d_xT.handle, d_xT.at(b))
                act.activation(XP[0][:, 1:T + 1], ps[0][:], ACT.Identity, scale=v("pre_g"), bias=v("pre_b"))\
                    .then_inc(d_xn.handle, 1)
                slot(3)

                def factors(c):
                    act.wait_ge(d_kvr.handle, d_kvr.at(b, 3 * c + 1))
                    if c >= 2:
                        act.wait_ge(d_wk.handle, d_wk.at(b, c - 1))
                    act.activation(tile[7 + c % 2][:], ps[1][:], ACT.Exp).then_inc(d_act.handle, 1)
                    act.wait_ge(d_kvr.handle, d_kvr.at(b, 3 * c + 3))
                    if not first and c == 0:
                        act.wait_ge(d_o.handle, d_o.before(b))
                    act.activation(tile[13 + c][:], ps[3][:], ACT.Tanh, scale=0.5).then_inc(d_act.handle, 1)

                factors(0)
                slot(4)
                factors(1)
                slot(5)
                slot(6)
                factors(2)
                slot(7)
                factors(3)
                slot(8)
                slot(9)
                slot(10)
                slot(11)
                act.wait_ge(d_x2T.handle, d_x2T.at(b))
                act.activation(XP[1][:, 1:T + 1], ps[0][:], ACT.Identity, scale=v("post_g"), bias=v("post_b"))\
                    .then_inc(d_xn2.handle, 1)
                slot(12)
                for c in range(UC):
                    act.wait_ge(d_kk.handle, d_kk.at(b, c + 1))
                    if not first and c == 0:
                        act.wait_ge(d_o2.handle, d_o2.before(b))
                    act.activation(tile[18 + c][:], ps[1 + c % 3][:], ACT.Silu).then_inc(d_silu.handle, 1)
                act.wait_ge(d_sg.handle, d_sg.at(b))
                act.activation(tile[17][:], ps[4][:], ACT.Tanh, scale=0.5).then_inc(d_sig.handle, 1)
                slot(13)
                slot(14)
                act.wait_ge(d_x3T.handle, d_x3T.at(b))
                fence(act)
                act.activation(XN[:, b, 1:T + 1], ps[1][:], ACT.Copy)
                act.activation(tile[3][:], ps[1][:], ACT.Copy).then_inc(d_xf.handle, 1)
                slot(15)
                slot(16)
                act.wait_ge(d_gap.handle, d_gap.at(b))
                act.activation(W2[:], W2[:], ACT.Exp).then_inc(d_exp.handle, 1)

            in_step(act, act_d, act_experts("e", NE, ACT.Gelu), SLOTS_D)

        @block.tensor
        def _(pe):
            def product(dst, pairs):
                for i, (lhsT, rhs) in enumerate(pairs):
                    ins = pe.matmul(dst, lhsT, rhs, start=i == 0, stop=i == len(pairs) - 1)
                return ins

            def transposes(dst, src):
                for j in range(TB):
                    ins = pe.transpose(dst[:, col(j)], src[:, col(j)], ID[:])
                return ins

            pe.wait_ge(w_in.handle, ALL_W)
            pe.wait_ge(const.handle, N_CONST)

            def pe_a(b, first):
                pe.wait_ge(norm_out["attn0"].handle, norm_out["attn0"].at(b))
                if not first:
                    pe.wait_ge(a_xn.handle, a_xn.before(b))
                transposes(ps[0], tile[0]).then_inc(a_xT.handle, 1)
                pe.wait_ge(a_xx.handle, a_xx.at(b))
                for q in range(2):
                    if not first:
                        pe.wait_ge(a_tanh.handle, a_tanh.before(b, q + 1))
                    for j in range(2):
                        ins = product(ps[1 + q][:, col(j, NS * LR)], [(tile[2][:, col(2 * q + j)], w0("A", NS * LR))])
                    ins.then_inc(a_h.handle, 1)

            over_batches(pe, pe_a)

            def pe_experts(key, n, W, at, first_name, second_name):
                gu, act_done, hid, down, total = moe_sems[key]

                def items(b, first, k0, k1):
                    for k in range(k0, k1):
                        e, c, output = expert_item(k)
                        if output:
                            if e >= 0:
                                outputs(b, first, e)
                        elif e < n:
                            for m, name in enumerate((first_name, second_name)):
                                before, done = (act_done, HC * e + c) if m == 0 else (hid, HC * e + c)
                                if done:
                                    pe.wait_ge(before.handle, before.at(b, done))
                                elif not first:
                                    pe.wait_ge(before.handle, before.before(b))
                                w = at[name] + HID * e + P * c
                                product(ps[G + m][:], [(W[:, w:w + P], XF[:, b])]).then_inc(gu.handle, 1)

                def outputs(b, first, e):
                    pe.wait_ge(hid.handle, hid.at(b, HC * (e + 1)))
                    if e:
                        pe.wait_ge(total.handle, total.at(b, e))
                    elif not first:
                        pe.wait_ge(total.handle, total.before(b))
                    for j in range(TB):
                        ins = product(ps[DN][:, col(j)],
                                      [(hidden[e % 2][c][:, col(j)], W[:, at["d"] + C * (HC * e + c):at["d"] + C * (HC * e + c + 1)])
                                       for c in range(HC)])
                    ins.then_inc(down.handle, 1)

                return items

            def pe_b(b, first, slot):
                pe.wait_ge(b_load.handle, b_load.at(b))
                if first:
                    pe.wait_ge(a_tanh.handle, a_tanh.at(B - 1))
                for j in range(TB):
                    pe.transpose(ps[0][:, col(j)], HS[:, j, 0:P], ID[:])
                    ins = pe.transpose(ps[1][0:LR, col(j)], HS[:, j, P:P + LR], ID[:])
                ins.then_inc(b_hT.handle, 1)
                slot(0)
                pe.wait_ge(b_hTs.handle, b_hTs.at(b))
                if not first:
                    pe.wait_ge(b_shift.handle, b_shift.before(b))
                for s in range(4):
                    product(ps[MIU[s]][:], [(W0[LR * s:LR * (s + 1), a0["Bp"]:a0["Bp"] + C], tile[0][LR * s:LR * (s + 1)])])\
                        .then_inc(b_miu.handle, 1)
                product(ps[MIU[4]][:], [(BP4[:], tile[7][0:LR])]).then_inc(b_miu.handle, 1)
                slot(1)
                pe.wait_ge(b_x5.handle, b_x5.at(b, 1))
                product(ps[2][0:HEAD], [(w0("tdA", HEAD), tile[2][:])]).then_inc(b_td.handle, 1)
                pe.wait_ge(b_x5.handle, b_x5.at(b, 2))
                product(ps[3][:], [(w0("WkT", C), tile[3][:])]).then_inc(b_k.handle, 1)
                pe.wait_ge(b_x5.handle, b_x5.at(b, 3))
                for j in range(TB):
                    ins = product(ps[4][:, col(j)], [(tile[4][:, col(j)], w0("WvT", C))])
                ins.then_inc(b_v.handle, 1)
                slot(2)
                pe.wait_ge(b_tdt.handle, b_tdt.at(b))
                product(ps[2][:], [(TDB[:], tile[11][0:HEAD])]).then_inc(b_w.handle, 1)
                pe.wait_ge(b_x5.handle, b_x5.at(b, 4))
                product(ps[0][:], [(w0("WrT", C), tile[5][:])]).then_inc(b_r.handle, 1)
                slot(3)
                pe.wait_ge(b_x5.handle, b_x5.at(b, 5))
                product(ps[1][:], [(w0("Wg1", P), tile[6][:])])
                pe.wait_ge(b_vs.handle, b_vs.at(b))
                product(ps[4][0:LR], [(w0("Wg1", LR, P), tile[6][:])]).then_inc(b_g1.handle, 1)
                slot(4)
                pe.wait_ge(b_g1t.handle, b_g1t.at(b))
                pe.wait_ge(b_d.handle, b_d.at(b))
                product(ps[2][:], [(w0("Wg2a", C), tile[18][:]), (WG2B[:], tile[19][0:LR])]).then_inc(b_g2.handle, 1)
                slot(5)

                pe.wait_ge(b_kd.handle, b_kd.at(b))
                pe.wait_ge(b_ru.handle, b_ru.at(b))
                for lv in range(LEVELS):
                    half = 1 << lv
                    if lv:
                        pe.wait_ge(b_scaled.handle, b_scaled.at(b, 3 * lv))
                    if lv == 1:
                        pe.wait_ge(b_gs.handle, b_gs.at(b))
                    if lv >= 2:
                        pe.wait_ge(b_put.handle, b_put.at(b, lv))
                    for c in range(TB):
                        for n in range(NH):
                            h = slice(HEAD * n, HEAD * (n + 1))
                            right = tile[10][h, col(c)].rearrange("p (m two h) -> p m two h", two=2, h=half)[:, :, 1]
                            ins = product(ps[LEVEL_BANKS[lv % 2][n]][:, col(c, HEAD)], [(tile[9][h, col(c)], right)])
                    ins.then_inc(b_level.handle, 1)
                    if lv == 0:
                        slot(6)
                        pe.wait_ge(b_ruk.handle, b_ruk.at(b))
                        for c in range(TB):
                            ins = product(ps[3][:, col(c, NH)], [(tile[12][:, col(c)], HSEL[:])])
                        ins.then_inc(b_dsc.handle, 1)
                    else:
                        slot(6 + lv)
                pe.wait_ge(b_scaled.handle, b_scaled.at(b))
                transposes(ps[3], tile[9]).then_inc(b_kT.handle, 1)
                slot(13)
                pe.wait_ge(b_kTs.handle, b_kTs.at(b))
                pe.wait_ge(b_put.handle, b_put.at(b, LEVELS))
                for c in range(TB - 1):
                    ins = product(ps[4][:, col(c)], [(tile[20][:, col(c)], tile[13][:, col(c)])])
                ins.then_inc(b_u.handle, 1)
                slot(14)
                pe.wait_ge(b_put.handle, b_put.at(b))
                for c in range(TB):
                    if c:
                        pe.wait_ge(b_state.handle, b_state.at(b, c))
                        pe.matmul(ps[3][:, col(c)], tile[10][:, col(c)], S4[:, c], start=True, stop=False)
                    for n in range(NH):
                        at = P * c + HEAD * n
                        ins = pe.matmul(ps[3][:, at:at + HEAD], AT[:, n, c], tile[13][:, at:at + HEAD],
                                        start=c == 0, stop=c == 0 or n == NH - 1)
                ins.then_inc(b_y.handle, 1)
                slot(15)
                pe.wait_ge(norm_out["heads"].handle, norm_out["heads"].at(b))
                transposes(ps[0], tile[14]).then_inc(b_ynT.handle, 1)
                slot(16)
                pe.wait_ge(b_z.handle, b_z.at(b))
                for j in range(TB):
                    ins = product(ps[2][:, col(j)], [(tile[16][:, col(j)], w0("WoT", C))])
                ins.then_inc(b_o.handle, 1)
                slot(17)
                pe.wait_ge(norm_out["ffn0"].handle, norm_out["ffn0"].at(b))
                transposes(ps[1], tile[17]).then_inc(b_xT.handle, 1)
                pe.wait_ge(b_xf.handle, b_xf.at(b))
                if first:
                    pe.wait_ge(later_in.handle, ALL_LATER)
                for j in range(TB):
                    ins = product(ps[3][:, col(j, NE)], [(tile[21][:, col(j)], WM0[:, m0["router"]:m0["router"] + NE])])
                ins.then_inc(b_logits.handle, 1)
                slot(18)

            in_step(pe, pe_b, pe_experts("c", NE + 1, WM0, m0, "g", "u"), SLOTS_B)

            def pe_d(b, first, slot):
                slot(0)
                slot(1)
                slot(2)
                pe.wait_ge(norm_out["pre"].handle, norm_out["pre"].at(b))
                transposes(ps[0], tile[2]).then_inc(d_xT.handle, 1)
                slot(3)

                def factors(c):
                    for m, name in enumerate(("Wk", "Wv", "Wr")):
                        if c == 0:
                            pe.wait_ge(d_mix.handle, d_mix.at(b, m + 1))
                        if c:
                            if m == 1:
                                pe.wait_ge(d_kv.handle, d_kv.at(b, c))
                            else:
                                pe.wait_ge(d_act.handle, d_act.at(b, 2 * (c - 1) + 1 + m // 2))
                        elif not first and m == 0:
                            pe.wait_ge(d_cw.handle, d_cw.before(b))
                        product(ps[1 + m][:], [(w1(name, P, P * c), tile[4 + m][:])]).then_inc(d_kvr.handle, 1)

                factors(0)
                slot(4)
                factors(1)
                slot(5)
                slot(6)
                factors(2)
                slot(7)
                factors(3)
                slot(8)
                slot(9)
                slot(10)
                pe.wait_ge(d_rw.handle, d_rw.at(b))
                for j in range(TB):
                    ins = product(ps[4][:, col(j)], [(tile[13 + c][:, col(j)], w1("Wo", C, C * c)) for c in range(UC)])
                ins.then_inc(d_o.handle, 1)
                slot(11)
                pe.wait_ge(norm_out["post"].handle, norm_out["post"].at(b))
                transposes(ps[0], tile[2]).then_inc(d_x2T.handle, 1)
                slot(12)
                pe.wait_ge(d_mix2.handle, d_mix2.at(b))
                for c in range(UC):
                    if c == 3:
                        pe.wait_ge(d_silu.handle, d_silu.at(b, 1))
                    product(ps[1 + c % 3][:], [(w1("cWk", P, P * c), tile[4][:])]).then_inc(d_kk.handle, 1)
                for j in range(TB):
                    ins = product(ps[4][:, col(j)], [(tile[5][:, col(j)], w1("cWr", C))])
                ins.then_inc(d_sg.handle, 1)
                slot(13)
                pe.wait_ge(d_silu.handle, d_silu.at(b))
                for j in range(TB):
                    ins = product(ps[0][:, col(j)], [(tile[18 + c][:, col(j)], w1("cWv", C, C * c)) for c in range(UC)])
                ins.then_inc(d_o2.handle, 1)
                slot(14)
                pe.wait_ge(norm_out["ffn1"].handle, norm_out["ffn1"].at(b))
                transposes(ps[1], tile[2]).then_inc(d_x3T.handle, 1)
                slot(15)
                pe.wait_ge(d_xf.handle, d_xf.at(b))
                for j in range(TB):
                    ins = product(ps[2][:, col(j, NE)], [(tile[3][:, col(j)], WM1[:, m1["router"]:m1["router"] + NE])])
                ins.then_inc(d_logits.handle, 1)
                slot(16)
                pe.wait_ge(d_sel.handle, d_sel.at(b))
                for j in range(TB):
                    product(ps[3][:, col(j, NE)], [(ONES[:], R[1][:, i]) for i in range(j)] + [(TRI[:], R[1][:, j])])
                product(ps[3][:, col(TB, NE)], [(ONES[:], R[1][:, i]) for i in range(TB)]).then_inc(d_pos.handle, 1)

            in_step(pe, pe_d, pe_experts("e", NE, WM1, m1, "in", "gate"), SLOTS_D)


def kernel(**inputs):
    import numpy as _np
    import concourse.bacc as _bacc
    from concourse import mybir as _mybir
    from concourse.bass_utils import run_bass_kernel_spmd as _run

    i = {k: _np.asarray(a) for k, a in inputs.items()}
    a0 = lambda n: i["L0_attn_" + n]
    f0 = lambda n: i["L0_ffn_" + n]
    a1 = lambda n: i["L1_attn_" + n]
    f1 = lambda n: i["L1_ffn_" + n]

    def rows(w):
        return w.reshape(-1, P, w.shape[1]).transpose(1, 0, 2).reshape(P, -1)

    def side(ws):
        return _np.concatenate(list(ws), axis=1)

    f32 = _np.float32
    steps = _np.arange(P)
    level = _np.stack([((steps[:, None] >> (lv + 1)) == (steps[None] >> (lv + 1)))
                       & ((steps[:, None] >> lv) % 2 == 0) & ((steps[None] >> lv) % 2 == 1) for lv in range(LEVELS)], 1)
    x = a0("x").reshape(B, TB, P, C).transpose(2, 0, 1, 3)
    arrays = {
        "x": x,
        "attn0": side([a0("A"), a0("Bp")[:4].reshape(4 * LR, C), a0("tdA"), a0("Wk").T, a0("Wv").T, a0("Wr").T,
                       a0("Wo").T, a0("Wg1"), a0("Wg2")[:P]]),
        "tdB": a0("tdB"),
        "bp4": a0("Bp")[4],
        "wg2b": a0("Wg2")[P:],
        "moe0": side([f0("sg").T, *(w.T for w in f0("eg")), f0("su").T, *(w.T for w in f0("eu")),
                      rows(f0("sd").T), *(rows(w.T) for w in f0("ed")), f0("router_w").T]),
        "attn1": side([a1("tm_Wk"), a1("tm_Wv"), a1("tm_Wr"), rows(a1("tm_Wo")), a1("cm_Wk"), rows(a1("cm_Wv")),
                       a1("cm_Wr")]),
        "lnrow": _np.broadcast_to(_np.stack([a1("ln0_g"), a1("ln0_b")]), (P, 2, C)),
        "dfvec": _np.stack([a1("tm_decay").reshape(UC, P).T, a1("tm_first").reshape(UC, P).T], 1),
        "vecs": _np.stack([a0("miu_x").reshape(C), *a0("lam").reshape(NS, C), a0("td_miu").reshape(C), a0("u").reshape(C),
                           a0("gamma"), a0("beta"), a1("pre_g"), a1("pre_b"), a1("post_g"), a1("post_b"),
                           a1("tm_mix_k"), a1("tm_mix_v"), a1("tm_mix_r"), a1("cm_mix_k"), a1("cm_mix_r")], 1),
        "moe1": side([*(w[:, :HID] for w in f1("W1")), *(w[:, HID:] for w in f1("W1")), *(rows(w) for w in f1("W2")),
                      f1("Wg").T]),
        "ident": _np.eye(P, dtype=f32),
        "levels": _np.stack([level[:, lv][:, (steps >> lv) % 2 == 1] for lv in range(LEVELS)], 1).astype(_np.int32),
        "tri": _np.triu(_np.ones((P, P), f32), 1),
        "iota": _np.broadcast_to(_np.arange(NE, dtype=f32), (P, 1, NE)),
        "hsel": (_np.arange(P)[:, None] // HEAD == _np.arange(NH)[None]).astype(f32),
    }
    nc = _bacc.Bacc("TRN2", target_bir_lowering=False, num_devices=1)
    arrays = {f"in_{k}": _np.ascontiguousarray(a) for k, a in arrays.items()}
    args = [nc.dram_tensor(k, a.shape, _mybir.dt.from_np(a.dtype), kind="ExternalInput").ap() for k, a in arrays.items()]
    args.append(nc.dram_tensor("out_0", (B, P, TB, C), F32, kind="ExternalOutput").ap())
    build(nc, *args)
    r = _run(nc, [arrays], core_ids=[0])
    return r.results[0]["out_0"].transpose(0, 2, 1, 3).reshape(B, T, C)
```

```python
from contextlib import ExitStack

import concourse.bass as bass
from concourse import mybir

P = 128
B = 8
T = 512
TB = T // P
C = 128
HEAD = 64
NH = C // HEAD
NE = 8
HID = 256
HC = HID // P
HU = 512
UC = HU // P
NS = 5
LR = 32
CAP = int(B * T * 2 * 1.25 / NE)
EPS = 1e-5
K_CLAMP = 60.0
K_EPS = 1e-8
E_CLAMP = 1.1420073898156842e26

F32 = mybir.dt.float32
F32R = mybir.dt.float32r
U32 = mybir.dt.uint32
I32 = mybir.dt.int32
ALU = mybir.AluOpType
ACT = mybir.ActivationFunctionType
AX = mybir.AxisListType

ATTN0 = [("A", NS * LR), ("Bp", C), ("tdA", HEAD), ("WkT", C), ("WvT", C), ("WrT", C), ("WoT", C),
         ("Wg1", 160), ("Wg2a", C)]
MOE0 = [("g", 9 * HID), ("u", 9 * HID), ("d", 9 * HC * C), ("router", NE)]
ATTN1 = [("Wk", HU), ("Wv", HU), ("Wr", HU), ("Wo", UC * C), ("cWk", HU), ("cWv", UC * C), ("cWr", C)]
MOE1 = [("in", NE * HID), ("gate", NE * HID), ("d", NE * HC * C), ("router", NE)]
VECS = ["miu_x", "lam0", "lam1", "lam2", "lam3", "lam4", "td_miu", "u", "gamma", "beta",
        "pre_g", "pre_b", "post_g", "post_b", "mix_k", "mix_v", "mix_r", "cmix_k", "cmix_r"]
NV = len(VECS)
NORMS = ("attn0", "heads", "ffn0", "attn1", "pre", "post", "ffn1")
LEVELS = 7

SLOTS_B = (2, 1, 1, 2, 3, 0, 1, 1, 1, 1, 1, 1, 2, 0, 0, 1, 3, 3, 1, 2, 1, 1)
SLOTS_D = (2, 2, 2, 1, 0, 2, 0, 1, 0, 1, 1, 2, 0, 1, 2, 0, 1, 1, 2, 0, 1, 0, 1, 1, 2)
SLOTS_D0 = (2, 2, 3, 2, 1, 1, 1, 1, 1, 1, 1, 1, 1, 1, 1, 1, 0, 1, 1, 1, 2, 0, 1, 1, 1)


def columns(parts):
    at, out = 0, {}
    for name, n in parts:
        out[name] = at
        at += n
    return out, at


class Sem:

    def __init__(self, handle, per):
        self.handle, self.per = handle, per

    def at(self, b, k=None):
        return b * self.per + (self.per if k is None else k)

    def before(self, b, k=None):
        return (b - 1) * self.per + (self.per if k is None else k)


class Chain:

    def __init__(self, eng, handle):
        self.eng, self.handle, self.per, self.b, self.k = eng, handle, 0, 0, 0

    def start(self, b, first):
        self.per = self.per if first else max(self.per, self.k)
        self.b, self.k = b, 0

    def step(self, ins):
        ins.then_inc(self.handle, 1)
        self.k += 1
        self.eng.wait_ge(self.handle, self.b * self.per + self.k)


def build(nc, x, attn0, tdB, bp4, wg2b, moe0, attn1, lnrow, dfvec, vecs, moe1, ident, levels, tri, iota, hsel, out):
    a0, na0 = columns(ATTN0)
    m0, nm0 = columns(MOE0)
    a1, na1 = columns(ATTN1)
    m1, nm1 = columns(MOE1)
    with ExitStack() as ctx:
        def sb(name, shape, dt=F32):
            return ctx.enter_context(nc.sbuf_tensor(name, shape, dt))

        def sem(name, per=1):
            return Sem(ctx.enter_context(nc.semaphore(name)), per)

        W0 = sb("W0", [P, na0])
        TDB = sb("TDB", [HEAD, C])
        BP4 = sb("BP4", [LR, C])
        WG2B = sb("WG2B", [LR, C])
        WHIGH = sb("WHIGH", [P, 2 * (NE + 1) * HID], F32R)
        WLOW = sb("WLOW", [P, 2 * (NE + 1) * HID], F32R)
        WD0 = sb("WD0", [P, nm0 - m0["d"]])
        W1 = sb("W1", [P, na1])
        WD1 = sb("WD1", [P, nm1 - m1["d"]])
        LNR = sb("LNR", [P, 2, C])
        DF = sb("DF", [P, 2, UC])
        V = sb("V", [P, NV])
        ID = sb("ID", [P, P])
        MASK = sb("MASK", [P, LEVELS, HEAD], I32)
        HSEL = sb("HSEL", [P, NH])
        TRI = sb("TRI", [P, P])
        IOTA = sb("IOTA", [P, 1, NE])
        ONES = sb("ONES", [P, P])
        CON = sb("CON", [P, 3, NE])
        DEC = sb("DEC", [P, 2, UC])
        DTMP = sb("DTMP", [P, UC])

        X = sb("X", [P, B, TB, C])
        XN = sb("XN", [P, B, T + 1])
        XHIGH = sb("XHIGH", [P, T], F32R)
        XLOW = sb("XLOW", [P, T], F32R)
        CW = sb("CW", [P, B, TB, NE])

        STAT = [(sb(f"ST{n}", [P, TB * NH, 6]), sb(f"MV{n}", [P, TB * NH, 2]), sb(f"VE{n}", [P, TB * NH]),
                 sb(f"RS{n}", [P, TB * NH])) for n in range(2)]
        tile = [sb(f"tile{n}", [P, T]) for n in range(22)]
        X1 = sb("X1", [P, T])
        CN = sb("CN", [P, T])
        CX = [sb(f"CX{n}", [P, T]) for n in range(3)]
        acted = [sb(f"acted{c}", [P, T]) for c in range(HC)]
        hidden = [[sb(f"hidden{n}{c}", [P, T]) for c in range(HC)] for n in range(2)]
        SCALED = [sb(f"SCALED{n}", [P, T]) for n in range(2)]
        STAGE = (*acted, *hidden[0], *hidden[1])
        DSC = sb("DSC", [P, TB * NH])
        XP = [sb(f"XP{n}", [P, T + 1]) for n in range(2)]
        SKP = [sb(f"SKP{n}", [P, T + 1]) for n in range(2)]
        AT = sb("AT", [P, NH, TB, P])
        D = [sb(f"D{n}", [P, T >> n]) for n in range(1, LEVELS + 1)]
        S4 = sb("S4", [P, TB, C])
        HS = sb("HS", [P, TB, NS * LR])
        R = [sb(f"R{n}", [P, TB, NE]) for n in range(6)]
        CHOSEN = sb("CHOSEN", [P, TB + 1, NE])
        M8 = sb("M8", [P, TB, NE])
        I8 = sb("I8", [P, TB, NE], U32)
        IF = sb("IF", [P, TB, 2])
        R4 = [sb(f"R4{n}", [P, TB, 1]) for n in range(4)]
        W2 = sb("W2", [P, TB, 2])
        CARRY = sb("CARRY", [P, 1, NE])

        ps = [ctx.enter_context(nc.psum_tensor(f"bank{n}", [P, T], F32)) for n in range(8)]
        h_dram = nc.dram_tensor("h_scratch", [B * T * NS, LR], F32, kind="Internal").ap()

        def v(name):
            return V[:, VECS.index(name):VECS.index(name) + 1]

        def blk(ap):
            return ap.rearrange("p (a c) -> p a c", c=P)

        def col(j, n=P):
            return slice(n * j, n * (j + 1))

        def plain(ap):
            return ap.bitcast(F32)

        def w0(name, n, at=0):
            return W0[:, a0[name] + at:a0[name] + at + n]

        def w1(name, n, at=0):
            return W1[:, a1[name] + at:a1[name] + at + n]

        w_high, w_low, b_xhigh, d_xhigh = sem("w_high"), sem("w_low"), sem("b_xhigh"), sem("d_xhigh")
        staged = sem("staged0"), sem("staged1")
        b_xlow, d_xlow = sem("b_xlow"), sem("d_xlow")
        x0_in, x1_in, x3_in, a_w_in, w_in, later_in, const, dec, fences = (
            sem(n) for n in ("x0_in", "x1_in", "x3_in", "a_w_in", "w_in", "later_in", "const", "dec", "fences"))
        chain_a, chain_b, chain_d1, chain_d2 = (sem(n) for n in ("chain_a", "chain_b", "chain_d1", "chain_d2"))
        norm_stats = {n: sem(f"{n}_stats") for n in NORMS}
        norm_rstd = {n: sem(f"{n}_rstd") for n in NORMS}
        norm_moments = {n: sem(f"{n}_moments") for n in NORMS}
        norm_var_eps = {n: sem(f"{n}_var_eps", 3 if n == "attn1" else 1) for n in NORMS}
        norm_out = {n: sem(f"{n}_out") for n in NORMS}
        a_xT, a_xn, a_xx, a_store = sem("a_xT"), sem("a_xn"), sem("a_xx"), sem("a_store", 16)
        a_h, a_tanh = sem("a_h", 2), sem("a_tanh", 2)
        b_load = sem("b_load", 16 * TB)
        b_hT, b_hTs, b_miu, b_mixed, b_x5 = sem("b_hT"), sem("b_hTs", 2), sem("b_miu", NS), sem("b_mixed", NS), sem("b_x5", NS)
        b_td, b_tdt, b_w, b_d, b_k, b_kd = (sem(n) for n in ("b_td", "b_tdt", "b_w", "b_d", "b_k", "b_kd"))
        b_v, b_vs, b_r, b_rs, b_ru = (sem(n) for n in ("b_v", "b_vs", "b_r", "b_rs", "b_ru"))
        b_ruk, b_dsc = sem("b_ruk"), sem("b_dsc")
        b_g1, b_g1t, b_g2, b_gs = sem("b_g1"), sem("b_g1t", 2), sem("b_g2"), sem("b_gs")
        b_level, b_scaled, b_put = sem("b_level", LEVELS), sem("b_scaled", 3 * LEVELS), sem("b_put", LEVELS + 1)
        b_kT, b_kTs, b_u, b_state, b_y = sem("b_kT"), sem("b_kTs"), sem("b_u"), sem("b_state", TB - 1), sem("b_y")
        b_ynT, b_yg, b_z, b_o, b_res = sem("b_ynT"), sem("b_yg"), sem("b_z"), sem("b_o"), sem("b_res")
        b_xT, b_xf, b_logits, b_shift, b_exp, b_cw = (sem(n) for n in ("b_xT", "b_xf", "b_logits", "b_shift", "b_exp", "b_cw"))
        moe_sems = {k: [sem(f"{k}_gu", 4 * n), sem(f"{k}_act", HC * n), sem(f"{k}_hid", HC * n),
                        sem(f"{k}_down", n), sem(f"{k}_sum", n)] for k, n in (("c", NE + 1), ("e", NE))}
        e_scaled = sem("e_scaled", NE)
        d_aff, d_xT, d_xn, d_mix = sem("d_aff", 2), sem("d_xT"), sem("d_xn"), sem("d_mix", 3)
        d_kr, d_v, d_act, d_kv, d_rw, d_o, d_x1 = sem("d_kr", 2 * UC), sem("d_v", UC), sem("d_act", 2 * UC), sem("d_kv", UC), sem("d_rw", UC), sem("d_o"), sem("d_x1")
        d_clip, d_sgm, d_sums, d_wk, d_den = (sem(n, UC) for n in ("d_clip", "d_sgm", "d_sums", "d_wk", "d_den"))
        d_gated = sem("d_gated", UC)
        d_inv = sem("d_inv", 2 * UC)
        d_x2T, d_xn2, d_mix2, d_kk, d_silu = sem("d_x2T"), sem("d_xn2"), sem("d_mix2", 2), sem("d_kk", UC), sem("d_silu", UC)
        d_o2, d_sg, d_sig = sem("d_o2"), sem("d_sg"), sem("d_sig")
        d_x3T, d_xf, d_logits, d_gap, d_exp, d_sel, d_pos, d_cw = (
            sem(n) for n in ("d_x3T", "d_xf", "d_logits", "d_gap", "d_exp", "d_sel", "d_pos", "d_cw"))
        stored = sem("stored", 16)

        block = ctx.enter_context(nc.Block())

        def over_batches(eng, body):
            body(0, True)
            with eng.Fori(1, B) as b:
                body(b, False)

        def given(seq, piece, *args):
            if seq is not None:
                piece(*args)

        def items_at(experts, b, first, slots):
            at = [sum(slots[:n]) for n in range(len(slots) + 1)]
            return lambda slot: experts(b, first, at[slot], at[slot + 1])

        def b_steps(eng, block, experts, free=lambda slot: None):
            block(0, True, free)
            block(1, False, items_at(experts, 0, True, SLOTS_B))
            with eng.Fori(2, B) as b:
                block(b, False, items_at(experts, b - 1, False, SLOTS_B))

        def d_steps(eng, block, first_moe, experts, free=lambda slot: None):
            block(0, None, True, items_at(first_moe, B - 1, False, SLOTS_D0))
            block(1, 0, False, free)
            block(2, 1, False, items_at(experts, 0, True, SLOTS_D))
            with eng.Fori(3, B) as b:
                block(b, b - 1, False, items_at(experts, b - 2, False, SLOTS_D))
            block(None, B - 1, False, items_at(experts, B - 2, False, SLOTS_D))
            experts(B - 1, False, 0, sum(SLOTS_D))

        def expert_item(k):
            return (k // 3, (k % 3) // 2, False) if k % 3 != 1 else (k // 3 - 1, None, True)

        MIU = (2, 3, 4, 0, 1)
        LEVEL_BANKS = ((0, 1), (2, 4))
        EK = (tile[7], tile[8], tile[0], tile[2])
        KR = (1, 3)
        CM = (0, 3)
        G, U, DN = 5, {"c": (6, 6), "e": (6, 4)}, 7

        def fence(eng):
            eng.sem_inc(fences.handle, 1)

        FIRST = ((ID, ident), (V, vecs), (W0, attn0))
        WEIGHTS = ((TDB, tdB), (BP4, bp4), (WG2B, wg2b), (MASK, levels),
                   (HSEL, hsel), (IOTA, iota))
        LATER = ((WD0, moe0[:, m0["d"]:]), (W1, attn1), (LNR, lnrow), (DF, dfvec), (TRI, tri), (WD1, moe1[:, m1["d"]:]))
        SPLIT0, SPLIT1 = m0["d"] // T, m1["d"] // T
        X_PARTS = ((1, 3, x1_in), (3, B, x3_in))
        N_CONST = 9 + len(XP) + len(SKP)
        ALL_FIRST = 16 * len(FIRST)
        ALL_W = 16 * len(WEIGHTS)
        ALL_LATER = 16 * len(LATER)

        @block.sync
        def _(sp):
            sp.dma_start(X[:, 0], x[:, 0]).then_inc(x0_in.handle, 16)
            for dst, src in FIRST:
                sp.dma_start(dst[:], src).then_inc(a_w_in.handle, 16)
            for first_b, end_b, part_in in X_PARTS:
                sp.dma_start(X[:, first_b:end_b], x[:, first_b:end_b]).then_inc(part_in.handle, 16)
            for dst, src in WEIGHTS:
                sp.dma_start(dst[:], src).then_inc(w_in.handle, 16)

            def store_h(b, first):
                sp.wait_ge(a_tanh.handle, a_tanh.at(b))
                sp.dma_start(h_dram.rearrange("(b j p s) k -> b p j (s k)", p=P, j=TB, s=NS)[b], HS[:])\
                    .then_inc(a_store.handle, 16)

            over_batches(sp, store_h)
            sp.wait_ge(a_store.handle, a_store.at(B - 1))

            def load_part(moe, src, c, before):
                if c >= len(STAGE):
                    sp.wait_ge(w_low.handle, before + c + 1 - len(STAGE))
                sp.dma_start(STAGE[c % len(STAGE)][:], src[:, col(c, T)]).then_inc(staged[moe].handle, 16)

            def load_h(b, first):
                if not first:
                    sp.wait_ge(b_hT.handle, b_hT.before(b))
                src = h_dram.rearrange("(s b j p) k -> b j p s k", p=P, j=TB, s=NS)[b]
                for j in range(TB):
                    sp.dma_start(HS[:, j].rearrange("p (s k) -> p s k", s=NS), src[j]).then_inc(b_load.handle, 16)

            load_h(0, True)
            for c in range(SPLIT0):
                if c == len(STAGE):
                    for dst, src in LATER:
                        sp.dma_start(dst[:], src).then_inc(later_in.handle, 16)
                load_part(0, moe0, c, 0)
            with sp.Fori(1, B) as b:
                load_h(b, False)
            used = moe_sems["c"][4]
            sp.wait_ge(used.handle, used.at(B - 1))
            for c in range(SPLIT1):
                load_part(1, moe1, c, SPLIT0)
            done = moe_sems["e"][4]

            def store_out(b, first):
                sp.wait_ge(done.handle, done.at(b))
                sp.dma_start(out[b], X[:, b]).then_inc(stored.handle, 16)

            over_batches(sp, store_out)
            sp.wait_ge(stored.handle, stored.at(B - 1))

        @block.gpsimd
        def _(pool):
            pool.memset(ONES[:], 1.0).then_inc(const.handle, 1)
            pool.memset(CON[:, 0], EPS).then_inc(const.handle, 1)
            pool.memset(CON[:, 1], EPS * NH).then_inc(const.handle, 1)
            pool.memset(CON[:, 2], -0.5).then_inc(const.handle, 1)
            pool.memset(XN[:, :, 0:1], 0.0).then_inc(const.handle, 1)
            for z in (*XP, *SKP):
                pool.memset(z[:, 0:1], 0.0).then_inc(const.handle, 1)
            pool.memset(S4[:], 0.0).then_inc(const.handle, 1)
            pool.memset(CARRY[:], 0.0).then_inc(const.handle, 1)
            pool.memset(CHOSEN[:], 0.0).then_inc(const.handle, 1)
            pool.memset(R4[3][:], 0.0).then_inc(const.handle, 1)
            pool.wait_ge(const.handle, N_CONST)

            def rstd(b, name, n=TB, eps=0, stat=0):
                ST, MV, VE, RS = STAT[stat]
                pool.wait_ge(norm_moments[name].handle, norm_moments[name].at(b))
                pool.tensor_tensor(VE[:, 0:n], MV[:, 0:n, 1], CON[:, eps, 0:n], ALU.add).then_inc(norm_var_eps[name].handle, 1)
                pool.wait_ge(norm_var_eps[name].handle, norm_var_eps[name].at(b))
                pool.tensor_tensor(RS[:, 0:n], VE[:, 0:n], CON[:, 2, 0:n], ALU.pow).then_inc(norm_rstd[name].handle, 1)

            over_batches(pool, lambda b, first: rstd(b, "attn0"))

            def pool_b(b, first):
                for s in range(NS):
                    pool.wait_ge(b_mixed.handle, b_mixed.at(b, s + 1))
                    fence(pool)
                    pool.tensor_tensor(tile[2 + s][:], tile[2 + s][:], XN[:, b, 1:T + 1], ALU.add).then_inc(b_x5.handle, 1)
                pool.wait_ge(b_ru.handle, b_ru.at(b))
                pool.wait_ge(b_kd.handle, b_kd.at(b))
                pool.tensor_tensor(tile[12][:], tile[12][:], tile[9][:], ALU.mult).then_inc(b_ruk.handle, 1)
                rstd(b, "heads", TB * NH, 1)
                pool.wait_ge(b_yg.handle, b_yg.at(b))
                pool.wait_ge(b_gs.handle, b_gs.at(b))
                pool.tensor_tensor(tile[16][:], tile[16][:], tile[15][:], ALU.mult).then_inc(b_z.handle, 1)
                rstd(b, "ffn0")
                pool.wait_ge(b_xhigh.handle, b_xhigh.at(b))
                pool.tensor_tensor(XLOW[:], tile[21][:], plain(XHIGH[:]), ALU.subtract).then_inc(b_xlow.handle, 1)

            over_batches(pool, pool_b)

            def pool_d(b, a, first, slot):
                def affine():
                    pool.wait_ge(norm_out["attn1"].handle, norm_out["attn1"].at(b))
                    pool.tensor_tensor(blk(tile[1][:]), blk(tile[1][:]), LNR[:, 0:1].to_broadcast([P, TB, C]), ALU.mult)\
                        .then_inc(d_aff.handle, 1)
                    pool.wait_ge(d_aff.handle, d_aff.at(b, 1))
                    pool.tensor_tensor(blk(tile[1][:]), blk(tile[1][:]), LNR[:, 1:2].to_broadcast([P, TB, C]), ALU.add)\
                        .then_inc(d_aff.handle, 1)

                def clip(c):
                    pool.wait_ge(d_act.handle, d_act.at(b, c + 1))
                    fence(pool)
                    pool.tensor_scalar(EK[c][:], EK[c][:], E_CLAMP, None, ALU.min).then_inc(d_clip.handle, 1)

                def sigmoid(c):
                    pool.wait_ge(d_act.handle, d_act.at(b, UC + c + 1))
                    fence(pool)
                    pool.tensor_scalar(tile[13 + c][:], tile[13 + c][:], 0.5, 0.5, ALU.mult, ALU.add).then_inc(d_sgm.handle, 1)

                def denominator(c):
                    pool.wait_ge(d_wk.handle, d_wk.at(b, c + 1))
                    fence(pool)
                    pool.tensor_scalar(tile[11 + c % 2][:], tile[11 + c % 2][:], K_EPS, None, ALU.add).then_inc(d_den.handle, 1)

                def gate_sum(c):
                    pool.wait_ge(d_sgm.handle, d_sgm.at(b, c + 1))
                    pool.wait_ge(d_sums.handle, d_sums.at(b, c + 1))
                    pool.tensor_tensor(tile[13 + c][:], tile[13 + c][:], tile[9 + c % 2][:], ALU.mult)\
                        .then_inc(d_gated.handle, 1)

                def quotient(c):
                    pool.wait_ge(d_gated.handle, d_gated.at(b, c + 1))
                    pool.wait_ge(d_inv.handle, d_inv.at(b, 2 * c + 2))
                    pool.tensor_tensor(tile[13 + c][:], tile[13 + c][:], tile[11 + c % 2][:], ALU.mult)\
                        .then_inc(d_rw.handle, 1)

                def double_rstd():
                    ST, MV, VE, RS = STAT[0]
                    var, done = MV[:, 0:TB, 1], norm_var_eps["attn1"]
                    pool.wait_ge(norm_moments["attn1"].handle, norm_moments["attn1"].at(b))
                    pool.tensor_tensor(VE[:, 0:TB], var, CON[:, 0, 0:TB], ALU.add).then_inc(done.handle, 1)
                    pool.wait_ge(done.handle, done.at(b, 1))
                    pool.tensor_tensor(VE[:, 0:TB], VE[:, 0:TB], CON[:, 0, 0:TB], ALU.mult).then_inc(done.handle, 1)
                    pool.wait_ge(done.handle, done.at(b, 2))
                    pool.tensor_tensor(VE[:, 0:TB], VE[:, 0:TB], var, ALU.add).then_inc(done.handle, 1)
                    pool.wait_ge(done.handle, done.at(b, 3))
                    pool.tensor_tensor(RS[:, 0:TB], VE[:, 0:TB], CON[:, 2, 0:TB], ALU.pow).then_inc(norm_rstd["attn1"].handle, 1)

                def time_rstd(name):
                    rstd(b, name)

                def channel_rstd(name):
                    rstd(a, name, stat=1)

                def input_low():
                    pool.wait_ge(d_xhigh.handle, d_xhigh.at(a))
                    pool.tensor_tensor(XLOW[:], CX[0][:], plain(XHIGH[:]), ALU.subtract).then_inc(d_xlow.handle, 1)

                def slots(n, end):
                    for k in range(n, end):
                        slot(k)

                given(b, double_rstd)
                slot(0)
                given(a, channel_rstd, "post")
                slots(1, 5)
                given(b, affine)
                slot(5)
                given(b, time_rstd, "pre")
                slots(6, 9)
                given(b, clip, 0)
                slot(9)
                given(b, clip, 1)
                given(b, clip, 2)
                given(b, clip, 3)
                slot(10)
                given(b, denominator, 0)
                given(b, sigmoid, 0)
                given(b, sigmoid, 1)
                slots(11, 13)
                given(b, denominator, 1)
                given(a, channel_rstd, "ffn1")
                given(b, gate_sum, 0)
                slot(13)
                given(b, quotient, 0)
                slot(14)
                given(b, gate_sum, 1)
                given(b, sigmoid, 2)
                slot(15)
                given(b, denominator, 2)
                slot(16)
                given(b, quotient, 1)
                given(b, gate_sum, 2)
                given(b, sigmoid, 3)
                slots(17, 19)
                given(b, denominator, 3)
                given(b, gate_sum, 3)
                slots(19, 22)
                given(b, quotient, 2)
                slot(22)
                given(b, quotient, 3)
                given(a, input_low)
                slots(23, 25)

            def add_outputs(b, first, k0, k1):
                scaled, total = e_scaled, moe_sems["e"][4]
                for k in range(k0, k1):
                    e, c, output = expert_item(k)
                    if output and e >= 0:
                        pool.wait_ge(scaled.handle, scaled.at(b, e + 1))
                        if e:
                            pool.wait_ge(total.handle, total.at(b, e))
                        fence(pool)
                        pool.tensor_tensor(X[:, b], X[:, b], blk(SCALED[e % 2][:]), ALU.add).then_inc(total.handle, 1)

            pool.wait_ge(later_in.handle, ALL_LATER)
            d_steps(pool, pool_d, lambda *args: None, add_outputs)

        @block.vector
        def _(dve):
            steps_a, steps_b, steps_d1, steps_d2 = (Chain(dve, s.handle) for s in (chain_a, chain_b, chain_d1, chain_d2))

            def stats(b, name, src, n=TB, stat=0):
                ST, MV, VE, RS = STAT[stat]
                for j in range(n):
                    ins = dve.bn_stats(ST[:, j], src(j))
                ins.then_inc(norm_stats[name].handle, 1)
                dve.wait_ge(norm_stats[name].handle, norm_stats[name].at(b))
                fence(dve)
                for j in range(n):
                    ins = dve.bn_aggr(MV[:, j], ST[:, j])
                ins.then_inc(norm_moments[name].handle, 1)

            def apply(b, name, src, dst, n=TB, stat=0):
                ST, MV, VE, RS = STAT[stat]
                dve.wait_ge(norm_rstd[name].handle, norm_rstd[name].at(b))
                for j in range(n):
                    ins = dve.tensor_scalar(dst(j), src(j), MV[:, j, 0:1], RS[:, j:j + 1], ALU.subtract, ALU.mult)
                ins.then_inc(norm_out[name].handle, 1)

            def top_two(chain, probs):
                fence(dve)
                for j in range(TB):
                    ins = dve.max(M8[:, j], probs[:, j])
                chain.step(ins)
                fence(dve)
                for j in range(TB):
                    ins = dve.max_index(I8[:, j], M8[:, j], probs[:, j])
                chain.step(ins)
                chain.step(dve.tensor_copy(IF[:], I8[:, :, 0:2]))
                for k in range(2):
                    ins = dve.tensor_tensor(R[3 + k][:], IOTA[:].to_broadcast([P, TB, NE]),
                                            IF[:, :, k:k + 1].to_broadcast([P, TB, NE]), ALU.is_equal)
                chain.step(ins)

            def x_block(b):
                return lambda j: X[:, b, j]

            def tile_block(n):
                return lambda j: n[:, col(j)]

            def dve_a(b, first, last):
                steps_a.start(b, first)
                if not first:
                    dve.wait_ge(a_xT.handle, a_xT.before(b))
                    fence(dve)
                apply(b, "attn0", x_block(b), tile_block(tile[0]))
                if not last:
                    stats(b + 1, "attn0", x_block(b + 1))
                dve.wait_ge(a_xn.handle, a_xn.at(b))
                if not first:
                    dve.wait_ge(a_h.handle, a_h.before(b))
                steps_a.step(dve.tensor_tensor(tile[1][:], XN[:, b, 0:T], XN[:, b, 1:T + 1], ALU.subtract))
                dve.scalar_tensor_tensor(out=tile[2][:], in0=tile[1][:], scalar=v("miu_x"), in1=XN[:, b, 1:T + 1],
                                         op0=ALU.mult, op1=ALU.add).then_inc(a_xx.handle, 1)

            dve.wait_ge(x0_in.handle, 16)
            stats(0, "attn0", x_block(0))
            dve.wait_ge(a_w_in.handle, ALL_FIRST)
            dve.wait_ge(const.handle, N_CONST)
            dve.wait_ge(x1_in.handle, 16)
            dve_a(0, True, False)
            dve_a(1, False, False)
            dve.wait_ge(x3_in.handle, 16)
            with dve.Fori(2, B - 1) as b:
                dve_a(b, False, False)
            dve_a(B - 1, False, True)
            dve.wait_ge(w_in.handle, ALL_W)

            def dve_experts(key, n, shared):
                gu, act, hid, down, total = moe_sems[key]

                def items(b, first, k0, k1):
                    for k in range(k0, k1):
                        e, c, output = expert_item(k)
                        if output:
                            if e < 0 or key == "e":
                                continue
                            dve.wait_ge(down.handle, down.at(b, e + 1))
                            add(b, e, shared, total)
                        elif e < n:
                            dve.wait_ge(act.handle, act.at(b, HC * e + c + 1))
                            dve.wait_ge(gu.handle, gu.at(b, 4 * e + 2 * c + 2))
                            if e >= 2:
                                dve.wait_ge(down.handle, down.at(b, e - 1))
                            elif not first:
                                dve.wait_ge(down.handle, down.before(b))
                            dve.tensor_tensor(hidden[e % 2][c][:], acted[c][:], ps[U[key][c]][:], ALU.mult).then_inc(hid.handle, 1)

                return items

            def add(b, e, shared, total):
                if e:
                    dve.wait_ge(total.handle, total.at(b, e))
                if shared and e == 0:
                    ins = dve.tensor_tensor(X[:, b], X[:, b], blk(ps[DN][:]), ALU.add)
                else:
                    for j in range(TB):
                        ins = dve.scalar_tensor_tensor(
                            out=X[:, b, j], in0=ps[DN][:, col(j)], scalar=CW[:, b, j, e - shared:e - shared + 1],
                            in1=X[:, b, j], op0=ALU.mult, op1=ALU.add)
                ins.then_inc(total.handle, 1)

            def dve_b(b, first, slot):
                steps_b.start(b, first)
                if first:
                    dve.wait_ge(a_h.handle, a_h.at(B - 1))
                steps_b.step(dve.tensor_tensor(tile[1][:], XN[:, b, 0:T], XN[:, b, 1:T + 1], ALU.subtract))
                slot(0)
                if not first:
                    dve.wait_ge(b_g1.handle, b_g1.before(b))
                for s in range(NS):
                    dve.wait_ge(b_miu.handle, b_miu.at(b, s + 1))
                    dve.scalar_tensor_tensor(out=tile[2 + s][:], in0=ps[MIU[s]][:], scalar=v(f"lam{s}"), in1=tile[1][:],
                                             op0=ALU.add, op1=ALU.mult).then_inc(b_mixed.handle, 1)
                slot(1)
                slot(2)
                dve.wait_ge(b_d.handle, b_d.at(b))
                dve.wait_ge(b_k.handle, b_k.at(b))
                if not first:
                    dve.wait_ge(b_kT.handle, b_kT.before(b))
                dve.scalar_tensor_tensor(out=tile[9][:], in0=tile[8][:], scalar=1.0, in1=ps[3][:],
                                         op0=ALU.min, op1=ALU.mult).then_inc(b_kd.handle, 1)
                slot(3)
                slot(4)
                slot(5)
                slot(6)
                dprod = tile[8]
                for lv in range(LEVELS):
                    half, nb = 1 << lv, T >> (lv + 1)
                    dve.wait_ge(b_level.handle, b_level.at(b, lv + 1))
                    if lv:
                        dve.wait_ge(b_put.handle, b_put.at(b, lv + 1))
                        dve.wait_ge(b_scaled.handle, b_scaled.at(b, 3 * lv))
                    else:
                        dve.wait_ge(b_ruk.handle, b_ruk.at(b))
                        dve.wait_ge(b_kd.handle, b_kd.at(b))
                    dd = dprod[:].rearrange("p (m two) -> p m two", two=2)
                    for buf, hl, dl in ((tile[9], 0, 1), (tile[10], 1, 0)):
                        part = buf[:].rearrange("p (m two h) -> p m two h", two=2, h=half)[:, :, hl]
                        dve.tensor_tensor(part, part, dd[:, :, dl:dl + 1].to_broadcast([P, nb, half]), ALU.mult)\
                            .then_inc(b_scaled.handle, 1)
                    dve.tensor_tensor(D[lv][:], dd[:, :, 0], dd[:, :, 1], ALU.mult).then_inc(b_scaled.handle, 1)
                    dprod = D[lv]
                    if lv == 0:
                        dve.wait_ge(b_dsc.handle, b_dsc.at(b))
                        steps_b.step(dve.tensor_copy(DSC[:], ps[3][:, 0:TB * NH]))
                        if not first:
                            dve.wait_ge(b_y.handle, b_y.before(b))
                        for c in range(TB):
                            for n in range(NH):
                                ins = dve.tensor_scalar(AT[:, n, c], ID[:], DSC[:, NH * c + n:NH * c + n + 1], None, ALU.mult)
                        ins.then_inc(b_put.handle, 1)
                        dve.wait_ge(b_put.handle, b_put.at(b, 1))
                        fence(dve)
                    mask = MASK[:, lv:lv + 1].rearrange("p a (m h) -> p a m h", h=half)\
                        .to_broadcast([P, TB, HEAD // half, half])
                    for n in range(NH):
                        right = AT[:, n].rearrange("p c (m two h) -> p c m two h", two=2, h=half)[:, :, :, 1]
                        fresh = ps[LEVEL_BANKS[lv % 2][n]][:, 0:TB * HEAD].rearrange("p (c m h) -> p c m h", c=TB, h=half)
                        ins = dve.copy_predicated(right, mask, fresh)
                    ins.then_inc(b_put.handle, 1)
                    if lv:
                        slot(6 + lv)
                slot(13)
                dve.wait_ge(b_u.handle, b_u.at(b))
                dve.wait_ge(b_scaled.handle, b_scaled.at(b))
                for c in range(1, TB):
                    if c > 1:
                        dve.wait_ge(b_state.handle, b_state.at(b, c - 1))
                    for n in range(NH):
                        h = slice(HEAD * n, HEAD * (n + 1))
                        new, u = S4[h, c, h], ps[4][h, P * (c - 1) + HEAD * n:P * (c - 1) + HEAD * (n + 1)]
                        if c == 1:
                            ins = dve.tensor_copy(new, u)
                        else:
                            ins = dve.scalar_tensor_tensor(out=new, in0=S4[h, c - 1, h], scalar=D[LEVELS - 1][h, c - 1:c],
                                                           in1=u, op0=ALU.mult, op1=ALU.add)
                    ins.then_inc(b_state.handle, 1)
                slot(14)
                dve.wait_ge(b_y.handle, b_y.at(b))
                if not first:
                    dve.wait_ge(b_ynT.handle, b_ynT.before(b))
                heads = lambda j: ps[3][:, col(j, HEAD)]
                stats(b, "heads", heads, TB * NH)
                slot(15)
                apply(b, "heads", heads, lambda j: tile[14][:, col(j, HEAD)], TB * NH)
                slot(16)
                slot(17)
                dve.wait_ge(b_o.handle, b_o.at(b))
                steps_b.step(dve.tensor_tensor(X[:, b], X[:, b], blk(ps[2][:]), ALU.add))
                fence(dve)
                stats(b, "ffn0", x_block(b))
                slot(18)
                apply(b, "ffn0", x_block(b), tile_block(tile[17]))
                slot(19)
                dve.wait_ge(b_logits.handle, b_logits.at(b))
                logits = ps[3][:, 0:TB * NE].rearrange("p (j e) -> p j e", e=NE)
                steps_b.step(dve.tensor_reduce(R4[0][:], logits, AX.X, ALU.max))
                dve.tensor_tensor(R[0][:], logits, R4[0][:].to_broadcast([P, TB, NE]), ALU.subtract).then_inc(b_shift.handle, 1)
                slot(20)
                dve.wait_ge(b_exp.handle, b_exp.at(b))
                steps_b.step(dve.tensor_reduce(R4[1][:], R[1][:], AX.X, ALU.add))
                steps_b.step(dve.reciprocal(R4[2][:], R4[1][:]))
                steps_b.step(dve.tensor_tensor(R[2][:], R[1][:], R4[2][:].to_broadcast([P, TB, NE]), ALU.mult))
                top_two(steps_b, R[2])
                slot(21)
                steps_b.step(dve.tensor_tensor(R4[1][:], M8[:, :, 0:1], M8[:, :, 1:2], ALU.add))
                steps_b.step(dve.reciprocal(R4[2][:], R4[1][:]))
                steps_b.step(dve.tensor_tensor(W2[:], M8[:, :, 0:2], R4[2][:].to_broadcast([P, TB, 2]), ALU.mult))
                for k in range(2):
                    ins = dve.tensor_tensor(R[k][:], R[3 + k][:], W2[:, :, k:k + 1].to_broadcast([P, TB, NE]), ALU.mult)
                steps_b.step(ins)
                dve.tensor_tensor(CW[:, b], R[0][:], R[1][:], ALU.add).then_inc(b_cw.handle, 1)

            def split_low(slot, slots, parts, before):
                c = slot - (len(slots) - parts)
                if c >= 0:
                    dve.wait_ge(w_high.handle, before + c + 1)
                    dve.tensor_tensor(WLOW[:, col(c, T)], STAGE[c % len(STAGE)][:], plain(WHIGH[:, col(c, T)]), ALU.subtract)\
                        .then_inc(w_low.handle, 1)

            first_moe = dve_experts("c", NE + 1, 1)
            b_steps(dve, dve_b, first_moe, lambda slot: split_low(slot, SLOTS_B, SPLIT0, 0))

            def dve_d(b, a, first, slot):
                def attn1_stats():
                    if first:
                        fence(dve)
                    stats(b, "attn1", x_block(b))

                def ln0():
                    apply(b, "attn1", x_block(b), tile_block(tile[1]))

                def pre_stats():
                    dve.wait_ge(d_aff.handle, d_aff.at(b))
                    fence(dve)
                    stats(b, "pre", tile_block(tile[1]))

                def pre():
                    apply(b, "pre", tile_block(tile[1]), tile_block(tile[2]))

                def mixes():
                    dve.wait_ge(d_xn.handle, d_xn.at(b))
                    steps_d1.step(dve.tensor_tensor(tile[3][:], XP[0][:, 1:T + 1], XP[0][:, 0:T], ALU.subtract))
                    for n, name in enumerate(("mix_k", "mix_v", "mix_r")):
                        dve.scalar_tensor_tensor(out=tile[4 + n][:], in0=tile[3][:], scalar=v(name), in1=XP[0][:, 0:T],
                                                 op0=ALU.mult, op1=ALU.add).then_inc(d_mix.handle, 1)

                def sums(c):
                    kx, kv = EK[c][:], tile[9 + c % 2][:]
                    dve.wait_ge(d_clip.handle, d_clip.at(b, c + 1))
                    dve.wait_ge(d_v.handle, d_v.at(b, c + 1))
                    if c >= 2:
                        dve.wait_ge(d_gated.handle, d_gated.at(b, c - 1))
                    elif not first:
                        dve.wait_ge(d_gated.handle, d_gated.before(b))
                    dve.tensor_tensor(kv, kx, ps[2][:], ALU.mult).then_inc(d_kv.handle, 1)
                    dve.wait_ge(d_kv.handle, d_kv.at(b, c + 1))
                    for m, val in enumerate((kx, kv)):
                        ins = dve.tensor_tensor_scan(SKP[m][:, 1:T + 1], DEC[:, 0, c:c + 1].to_broadcast([P, T]), val, 0.0,
                                                     ALU.mult, ALU.add)
                    steps_d1.step(ins)

                def present(c):
                    kx, kv, wk = EK[c][:], tile[9 + c % 2][:], tile[11 + c % 2][:]
                    if c >= 2:
                        dve.wait_ge(d_rw.handle, d_rw.at(b, c - 1))
                    elif not first:
                        dve.wait_ge(d_rw.handle, d_rw.before(b))
                    dve.scalar_tensor_tensor(out=wk, in0=kx, scalar=DEC[:, 1, c:c + 1], in1=SKP[0][:, 0:T],
                                             op0=ALU.mult, op1=ALU.add).then_inc(d_wk.handle, 1)
                    dve.scalar_tensor_tensor(out=kv, in0=kv, scalar=DEC[:, 1, c:c + 1], in1=SKP[1][:, 0:T],
                                             op0=ALU.mult, op1=ALU.add).then_inc(d_sums.handle, 1)

                def inverse(c, half):
                    wk = tile[11 + c % 2][:, col(half, T // 2)]
                    dve.wait_ge(d_den.handle, d_den.at(b, c + 1))
                    dve.reciprocal(wk, wk).then_inc(d_inv.handle, 1)

                def x1():
                    dve.wait_ge(d_o.handle, d_o.at(a))
                    dve.tensor_tensor(X1[:], tile[1][:], ps[2][:], ALU.add).then_inc(d_x1.handle, 1)
                    dve.wait_ge(d_x1.handle, d_x1.at(a))
                    fence(dve)
                    stats(a, "post", tile_block(X1), stat=1)

                def post():
                    apply(a, "post", tile_block(X1), tile_block(CN), stat=1)

                def channel_mixes():
                    dve.wait_ge(d_xn2.handle, d_xn2.at(a))
                    steps_d2.step(dve.tensor_tensor(CX[0][:], XP[1][:, 1:T + 1], XP[1][:, 0:T], ALU.subtract))
                    for n, name in enumerate(("cmix_k", "cmix_r")):
                        dve.scalar_tensor_tensor(out=CX[1 + n][:], in0=CX[0][:], scalar=v(name), in1=XP[1][:, 0:T],
                                                 op0=ALU.mult, op1=ALU.add).then_inc(d_mix2.handle, 1)

                def x2():
                    dve.wait_ge(d_sig.handle, d_sig.at(a))
                    dve.wait_ge(d_o2.handle, d_o2.at(a))
                    steps_d2.step(dve.scalar_tensor_tensor(out=tile[17][:], in0=tile[17][:], scalar=0.5, in1=ps[0][:],
                                                           op0=ALU.mult, op1=ALU.add))
                    steps_d2.step(dve.scalar_tensor_tensor(out=tile[17][:], in0=X1[:], scalar=0.5, in1=tile[17][:],
                                                           op0=ALU.add, op1=ALU.add))
                    steps_d2.step(dve.tensor_tensor(X[:, a], X[:, a], blk(tile[17][:]), ALU.add))

                def ffn1_stats():
                    fence(dve)
                    stats(a, "ffn1", x_block(a), stat=1)

                def ffn1():
                    apply(a, "ffn1", x_block(a), tile_block(CN), stat=1)

                def top():
                    dve.wait_ge(d_logits.handle, d_logits.at(a))
                    logits = ps[0][:, 0:TB * NE].rearrange("p (j e) -> p j e", e=NE)
                    steps_d2.step(dve.tensor_copy(R[0][:], logits))
                    top_two(steps_d2, R[0])
                    dve.tensor_tensor(CHOSEN[:, 0:TB], R[3][:], R[4][:], ALU.add).then_inc(d_sel.handle, 1)
                    dve.tensor_tensor(W2[:], M8[:, :, 0:2], M8[:, :, 0:1].to_broadcast([P, TB, 2]), ALU.subtract)\
                        .then_inc(d_gap.handle, 1)

                def gates():
                    dve.wait_ge(d_exp.handle, d_exp.at(a))
                    steps_d2.step(dve.tensor_tensor(R4[0][:], W2[:, :, 0:1], W2[:, :, 1:2], ALU.add))
                    steps_d2.step(dve.reciprocal(R4[1][:], R4[0][:]))
                    steps_d2.step(dve.tensor_tensor(W2[:], W2[:], R4[1][:].to_broadcast([P, TB, 2]), ALU.mult))
                    for k in range(2):
                        ins = dve.tensor_tensor(R[3 + k][:], R[3 + k][:], W2[:, :, k:k + 1].to_broadcast([P, TB, NE]), ALU.mult)
                    steps_d2.step(ins)
                    steps_d2.step(dve.tensor_tensor(R[2][:], R[3][:], R[4][:], ALU.add))
                    dve.wait_ge(d_pos.handle, d_pos.at(a))
                    pos = ps[0][:, 0:TB * NE].rearrange("p (j e) -> p j e", e=NE)
                    steps_d2.step(dve.tensor_tensor(R[5][:], pos, CARRY[:].to_broadcast([P, TB, NE]), ALU.add))
                    steps_d2.step(dve.tensor_scalar(R[5][:], R[5][:], float(CAP), None, ALU.is_lt))
                    steps_d2.step(dve.tensor_tensor(CARRY[:, 0], CARRY[:, 0], ps[0][:, TB * NE:(TB + 1) * NE], ALU.add))
                    dve.tensor_tensor(CW[:, a], R[2][:], R[5][:], ALU.mult).then_inc(d_cw.handle, 1)

                def slots(n, end):
                    for k in range(n, end):
                        slot(k)

                if b is not None:
                    steps_d1.start(b, first)
                if a is not None:
                    steps_d2.start(a, isinstance(a, int) and a == 0)
                given(b, attn1_stats)
                slot(0)
                given(a, x1)
                slots(1, 3)
                given(a, post)
                slot(3)
                given(b, ln0)
                slot(4)
                given(a, channel_mixes)
                slot(5)
                given(b, pre_stats)
                slot(6)
                given(b, pre)
                slots(7, 9)
                given(b, mixes)
                slot(9)
                given(b, sums, 0)
                slot(10)
                given(a, x2)
                slot(11)
                given(b, present, 0)
                given(b, sums, 1)
                given(a, ffn1_stats)
                slot(12)
                given(b, present, 1)
                slot(13)
                given(b, inverse, 0, 0)
                given(b, inverse, 0, 1)
                slot(14)
                given(a, ffn1)
                slot(15)
                given(b, sums, 2)
                slot(16)
                given(b, present, 2)
                given(b, inverse, 1, 0)
                slot(17)
                given(a, top)
                given(b, inverse, 1, 1)
                slot(18)
                given(b, sums, 3)
                slot(19)
                given(b, present, 3)
                given(b, inverse, 2, 0)
                slot(20)
                given(b, inverse, 2, 1)
                slots(21, 23)
                given(b, inverse, 3, 0)
                slot(23)
                given(b, inverse, 3, 1)
                given(a, gates)
                slot(24)

            dve.wait_ge(dec.handle, 3)
            d_steps(dve, dve_d, first_moe, dve_experts("e", NE, 0),
                    lambda slot: split_low(slot, SLOTS_D, SPLIT1, SPLIT0))

        @block.scalar
        def _(act):
            act.wait_ge(a_w_in.handle, ALL_FIRST)

            def act_a(b, first):
                act.wait_ge(a_xT.handle, a_xT.at(b))
                fence(act)
                act.activation(XN[:, b, 1:T + 1], ps[0][:], ACT.Copy).then_inc(a_xn.handle, 1)
                for q in range(2):
                    act.wait_ge(a_h.handle, a_h.at(b, q + 1))
                    if not first:
                        act.wait_ge(a_store.handle, a_store.before(b))
                    act.activation(HS[:, 2 * q:2 * q + 2].rearrange("p j k -> p (j k)"), ps[1 + q][:, 0:2 * NS * LR], ACT.Tanh)\
                        .then_inc(a_tanh.handle, 1)

            over_batches(act, act_a)
            act.wait_ge(w_in.handle, ALL_W)

            def act_experts(key, n, func):
                gu, act_done, hid, down, total = moe_sems[key]

                def items(b, first, k0, k1):
                    for k in range(k0, k1):
                        e, c, output = expert_item(k)
                        if output and key == "e" and e >= 0:
                            scale_output(b, e, down)
                        if output or e >= n:
                            continue
                        act.wait_ge(gu.handle, gu.at(b, 4 * e + 2 * c + 1))
                        if e:
                            act.wait_ge(hid.handle, hid.at(b, HC * (e - 1) + c + 1))
                        elif not first:
                            act.wait_ge(hid.handle, hid.before(b))
                        act.activation(acted[c][:], ps[G][:], func).then_inc(act_done.handle, 1)

                return items

            def scale_output(b, e, down):
                act.wait_ge(down.handle, down.at(b, e + 1))
                added = moe_sems["e"][4]
                if e >= 2:
                    act.wait_ge(added.handle, added.at(b, e - 1))
                elif not isinstance(b, int) or b > 0:
                    act.wait_ge(added.handle, added.before(b))
                fence(act)
                for j in range(TB):
                    ins = act.activation(SCALED[e % 2][:, col(j)], ps[DN][:, col(j)], ACT.Copy, scale=CW[:, b, j, e:e + 1])
                ins.then_inc(e_scaled.handle, 1)

            def act_b(b, first, slot):
                act.wait_ge(b_hT.handle, b_hT.at(b))
                if not first:
                    act.wait_ge(b_miu.handle, b_miu.before(b))
                act.activation(tile[0][:], ps[0][:], ACT.Copy).then_inc(b_hTs.handle, 1)
                act.activation(tile[7][0:LR], ps[1][0:LR], ACT.Copy).then_inc(b_hTs.handle, 1)
                slot(0)
                slot(1)
                act.wait_ge(b_td.handle, b_td.at(b))
                act.activation(tile[11][0:HEAD], ps[2][0:HEAD], ACT.Tanh).then_inc(b_tdt.handle, 1)
                act.wait_ge(b_v.handle, b_v.at(b))
                act.activation(tile[13][:], ps[4][:], ACT.Copy).then_inc(b_vs.handle, 1)
                slot(2)
                act.wait_ge(b_w.handle, b_w.at(b))
                act.activation(tile[8][:], ps[2][:], ACT.Exp, bias=v("td_miu")).then_inc(b_d.handle, 1)
                act.wait_ge(b_r.handle, b_r.at(b))
                act.activation(tile[10][:], ps[0][:], ACT.Copy).then_inc(b_rs.handle, 1)
                act.activation(tile[12][:], ps[0][:], ACT.Identity, scale=v("u")).then_inc(b_ru.handle, 1)
                slot(3)
                act.wait_ge(b_g1.handle, b_g1.at(b))
                act.activation(tile[18][:], ps[1][:], ACT.Tanh).then_inc(b_g1t.handle, 1)
                act.activation(tile[19][0:LR], ps[4][0:LR], ACT.Tanh).then_inc(b_g1t.handle, 1)
                slot(4)
                act.wait_ge(b_g2.handle, b_g2.at(b))
                if not first:
                    act.wait_ge(b_z.handle, b_z.before(b))
                act.activation(tile[15][:], ps[2][:], ACT.Copy).then_inc(b_gs.handle, 1)
                for s in range(5, 13):
                    slot(s)
                act.wait_ge(b_kT.handle, b_kT.at(b))
                act.activation(tile[20][:], ps[3][:], ACT.Copy).then_inc(b_kTs.handle, 1)
                slot(13)
                slot(14)
                slot(15)
                slot(16)
                act.wait_ge(b_ynT.handle, b_ynT.at(b))
                if not first:
                    act.wait_ge(b_o.handle, b_o.before(b))
                act.activation(tile[16][:], ps[0][:], ACT.Identity, scale=v("gamma"), bias=v("beta")).then_inc(b_yg.handle, 1)
                slot(17)
                slot(18)
                slot(19)
                act.wait_ge(b_xT.handle, b_xT.at(b))
                act.activation(tile[21][:], ps[1][:], ACT.Copy).then_inc(b_xf.handle, 1)
                slot(20)
                act.wait_ge(b_shift.handle, b_shift.at(b))
                act.activation(R[1][:], R[0][:], ACT.Exp).then_inc(b_exp.handle, 1)
                slot(21)
                round_input(b, first, tile[21], moe_sems["c"][0], b_xhigh)

            def split_high(slot, slots, parts, moe):
                c = slot - (len(slots) - parts)
                if c >= 0:
                    act.wait_ge(staged[moe].handle, 16 * (len(STAGE) if c < len(STAGE) else parts))
                    act.activation(WHIGH[:, col(c, T)], STAGE[c % len(STAGE)][:], ACT.Copy).then_inc(w_high.handle, 1)

            def round_input(b, first, source, used, done):
                if not first:
                    act.wait_ge(used.handle, used.before(b))
                act.activation(XHIGH[:], source[:], ACT.Copy).then_inc(done.handle, 1)

            first_moe = act_experts("c", NE + 1, ACT.Silu)
            b_steps(act, act_b, first_moe, lambda slot: split_high(slot, SLOTS_B, SPLIT0, 0))
            act.wait_ge(later_in.handle, ALL_LATER)
            act.activation(DTMP[:], DF[:, 0], ACT.Exp).then_inc(dec.handle, 1)
            act.wait_ge(dec.handle, 1)
            act.activation(DEC[:, 0], DTMP[:], ACT.Exp, scale=-1.0).then_inc(dec.handle, 1)
            act.activation(DEC[:, 1], DF[:, 1], ACT.Exp).then_inc(dec.handle, 1)

            def act_d(b, a, first, slot):
                def slots(n, end):
                    for k in range(n, end):
                        slot(k)

                def exp_k(c):
                    act.wait_ge(d_kr.handle, d_kr.at(b, c + 1))
                    act.activation(EK[c][:], ps[KR[c % 2]][:], ACT.Exp).then_inc(d_act.handle, 1)

                def tanh_r(c):
                    act.wait_ge(d_kr.handle, d_kr.at(b, UC + c + 1))
                    act.activation(tile[13 + c][:], ps[KR[c % 2]][:], ACT.Tanh, scale=0.5).then_inc(d_act.handle, 1)

                def post_affine():
                    act.wait_ge(d_x2T.handle, d_x2T.at(a))
                    act.activation(XP[1][:, 1:T + 1], ps[0][:], ACT.Identity, scale=v("post_g"), bias=v("post_b"))\
                        .then_inc(d_xn2.handle, 1)

                def pre_affine():
                    act.wait_ge(d_xT.handle, d_xT.at(b))
                    act.activation(XP[0][:, 1:T + 1], ps[1][:], ACT.Identity, scale=v("pre_g"), bias=v("pre_b"))\
                        .then_inc(d_xn.handle, 1)

                def channel_hidden():
                    for c in range(UC):
                        act.wait_ge(d_kk.handle, d_kk.at(a, c + 1))
                        act.activation(tile[18 + c][:], ps[CM[c % 2]][:], ACT.Silu).then_inc(d_silu.handle, 1)
                    act.wait_ge(d_sg.handle, d_sg.at(a))
                    act.activation(tile[17][:], ps[0][:], ACT.Tanh, scale=0.5).then_inc(d_sig.handle, 1)

                def ffn1_input():
                    act.wait_ge(d_x3T.handle, d_x3T.at(a))
                    act.activation(CX[0][:], ps[0][:], ACT.Copy).then_inc(d_xf.handle, 1)

                def gate_exp():
                    act.wait_ge(d_gap.handle, d_gap.at(a))
                    act.activation(W2[:], W2[:], ACT.Exp).then_inc(d_exp.handle, 1)

                slots(0, 4)
                given(a, post_affine)
                slots(4, 6)
                given(a, channel_hidden)
                slots(6, 8)
                given(b, pre_affine)
                slots(8, 10)
                given(b, exp_k, 0)
                given(b, exp_k, 1)
                given(b, exp_k, 2)
                given(b, exp_k, 3)
                slots(10, 12)
                given(b, tanh_r, 0)
                slot(12)
                given(b, tanh_r, 1)
                slots(13, 15)
                given(b, tanh_r, 2)
                given(a, ffn1_input)
                given(b, tanh_r, 3)
                slots(15, 20)
                given(a, gate_exp)
                slots(20, 25)
                if a is not None:
                    round_input(a, isinstance(a, int) and a == 0, CX[0], moe_sems["e"][0], d_xhigh)

            d_steps(act, act_d, first_moe, act_experts("e", NE, ACT.Gelu),
                    lambda slot: split_high(slot, SLOTS_D, SPLIT1, 1))

        @block.tensor
        def _(pe):
            def product(dst, pairs):
                for i, (lhsT, rhs) in enumerate(pairs):
                    ins = pe.matmul(dst, lhsT, rhs, start=i == 0, stop=i == len(pairs) - 1)
                return ins

            def transposes(dst, src):
                for j in range(TB):
                    ins = pe.transpose(dst[:, col(j)], src[:, col(j)], ID[:])
                return ins

            pe.wait_ge(a_w_in.handle, ALL_FIRST)
            pe.wait_ge(const.handle, N_CONST)

            def pe_a(b, first):
                pe.wait_ge(norm_out["attn0"].handle, norm_out["attn0"].at(b))
                if not first:
                    pe.wait_ge(a_xn.handle, a_xn.before(b))
                transposes(ps[0], tile[0]).then_inc(a_xT.handle, 1)
                pe.wait_ge(a_xx.handle, a_xx.at(b))
                for q in range(2):
                    if not first:
                        pe.wait_ge(a_tanh.handle, a_tanh.before(b, q + 1))
                    for j in range(2):
                        ins = product(ps[1 + q][:, col(j, NS * LR)], [(tile[2][:, col(2 * q + j)], w0("A", NS * LR))])
                    ins.then_inc(a_h.handle, 1)

            over_batches(pe, pe_a)
            pe.wait_ge(w_in.handle, ALL_W)

            def pe_experts(key, n, WD, at, first_name, second_name, split, xlow):
                gu, act_done, hid, down, total = moe_sems[key]

                def items(b, first, k0, k1):
                    for k in range(k0, k1):
                        e, c, output = expert_item(k)
                        if output:
                            if e >= 0:
                                outputs(b, first, e)
                        elif e < n:
                            for m, name in enumerate((first_name, second_name)):
                                bank = (G, U[key][c])[m]
                                before, done = (act_done, HC * e + c) if m == 0 else (hid, HC * e + c + 1 - len({*U[key]}))
                                if done > 0:
                                    pe.wait_ge(before.handle, before.at(b, done))
                                elif not first:
                                    pe.wait_ge(before.handle, before.before(b))
                                if first and k == m == 0:
                                    pe.wait_ge(w_low.handle, split)
                                if k == m == 0:
                                    pe.wait_ge(xlow.handle, xlow.at(b))
                                w = slice(at[name] + HID * e + P * c, at[name] + HID * e + P * (c + 1))
                                product(ps[bank][:], [(WLOW[:, w], XHIGH[:]), (WHIGH[:, w], XLOW[:]),
                                                      (WHIGH[:, w], XHIGH[:])]).then_inc(gu.handle, 1)

                def outputs(b, first, e):
                    pe.wait_ge(hid.handle, hid.at(b, HC * (e + 1)))
                    read = e_scaled if key == "e" else total
                    if e:
                        pe.wait_ge(read.handle, read.at(b, e))
                    elif not first:
                        pe.wait_ge(read.handle, read.before(b))
                    for j in range(TB):
                        ins = product(ps[DN][:, col(j)],
                                      [(hidden[e % 2][c][:, col(j)], WD[:, C * (HC * e + c):C * (HC * e + c + 1)])
                                       for c in range(HC)])
                    ins.then_inc(down.handle, 1)

                return items

            def pe_b(b, first, slot):
                pe.wait_ge(b_load.handle, b_load.at(b))
                if first:
                    pe.wait_ge(a_tanh.handle, a_tanh.at(B - 1))
                for j in range(TB):
                    pe.transpose(ps[0][:, col(j)], HS[:, j, 0:P], ID[:])
                    ins = pe.transpose(ps[1][0:LR, col(j)], HS[:, j, P:P + LR], ID[:])
                ins.then_inc(b_hT.handle, 1)
                slot(0)
                pe.wait_ge(b_hTs.handle, b_hTs.at(b))
                if not first:
                    pe.wait_ge(b_shift.handle, b_shift.before(b))
                for s in range(4):
                    product(ps[MIU[s]][:], [(W0[LR * s:LR * (s + 1), a0["Bp"]:a0["Bp"] + C], tile[0][LR * s:LR * (s + 1)])])\
                        .then_inc(b_miu.handle, 1)
                product(ps[MIU[4]][:], [(BP4[:], tile[7][0:LR])]).then_inc(b_miu.handle, 1)
                slot(1)
                pe.wait_ge(b_x5.handle, b_x5.at(b, 1))
                product(ps[2][0:HEAD], [(w0("tdA", HEAD), tile[2][:])]).then_inc(b_td.handle, 1)
                pe.wait_ge(b_x5.handle, b_x5.at(b, 2))
                product(ps[3][:], [(w0("WkT", C), tile[3][:])]).then_inc(b_k.handle, 1)
                pe.wait_ge(b_x5.handle, b_x5.at(b, 3))
                for j in range(TB):
                    ins = product(ps[4][:, col(j)], [(tile[4][:, col(j)], w0("WvT", C))])
                ins.then_inc(b_v.handle, 1)
                slot(2)
                pe.wait_ge(b_tdt.handle, b_tdt.at(b))
                product(ps[2][:], [(TDB[:], tile[11][0:HEAD])]).then_inc(b_w.handle, 1)
                pe.wait_ge(b_x5.handle, b_x5.at(b, 4))
                product(ps[0][:], [(w0("WrT", C), tile[5][:])]).then_inc(b_r.handle, 1)
                slot(3)
                pe.wait_ge(b_x5.handle, b_x5.at(b, 5))
                product(ps[1][:], [(w0("Wg1", P), tile[6][:])])
                pe.wait_ge(b_vs.handle, b_vs.at(b))
                product(ps[4][0:LR], [(w0("Wg1", LR, P), tile[6][:])]).then_inc(b_g1.handle, 1)
                slot(4)
                pe.wait_ge(b_g1t.handle, b_g1t.at(b))
                pe.wait_ge(b_d.handle, b_d.at(b))
                product(ps[2][:], [(w0("Wg2a", C), tile[18][:]), (WG2B[:], tile[19][0:LR])]).then_inc(b_g2.handle, 1)
                slot(5)

                pe.wait_ge(b_kd.handle, b_kd.at(b))
                pe.wait_ge(b_ru.handle, b_ru.at(b))
                for lv in range(LEVELS):
                    half = 1 << lv
                    if lv:
                        pe.wait_ge(b_scaled.handle, b_scaled.at(b, 3 * lv))
                    if lv == 1:
                        pe.wait_ge(b_gs.handle, b_gs.at(b))
                    if lv >= 2:
                        pe.wait_ge(b_put.handle, b_put.at(b, lv))
                    for c in range(TB):
                        for n in range(NH):
                            h = slice(HEAD * n, HEAD * (n + 1))
                            right = tile[10][h, col(c)].rearrange("p (m two h) -> p m two h", two=2, h=half)[:, :, 1]
                            ins = product(ps[LEVEL_BANKS[lv % 2][n]][:, col(c, HEAD)], [(tile[9][h, col(c)], right)])
                    ins.then_inc(b_level.handle, 1)
                    if lv == 0:
                        slot(6)
                        pe.wait_ge(b_ruk.handle, b_ruk.at(b))
                        for c in range(TB):
                            ins = product(ps[3][:, col(c, NH)], [(tile[12][:, col(c)], HSEL[:])])
                        ins.then_inc(b_dsc.handle, 1)
                    else:
                        slot(6 + lv)
                pe.wait_ge(b_scaled.handle, b_scaled.at(b))
                transposes(ps[3], tile[9]).then_inc(b_kT.handle, 1)
                slot(13)
                pe.wait_ge(b_kTs.handle, b_kTs.at(b))
                pe.wait_ge(b_put.handle, b_put.at(b, LEVELS))
                for c in range(TB - 1):
                    ins = product(ps[4][:, col(c)], [(tile[20][:, col(c)], tile[13][:, col(c)])])
                ins.then_inc(b_u.handle, 1)
                slot(14)
                pe.wait_ge(b_put.handle, b_put.at(b))
                for c in range(TB):
                    if c:
                        pe.wait_ge(b_state.handle, b_state.at(b, c))
                        pe.matmul(ps[3][:, col(c)], tile[10][:, col(c)], S4[:, c], start=True, stop=False)
                    for n in range(NH):
                        at = P * c + HEAD * n
                        ins = pe.matmul(ps[3][:, at:at + HEAD], AT[:, n, c], tile[13][:, at:at + HEAD],
                                        start=c == 0, stop=c == 0 or n == NH - 1)
                ins.then_inc(b_y.handle, 1)
                slot(15)
                slot(16)
                pe.wait_ge(norm_out["heads"].handle, norm_out["heads"].at(b))
                transposes(ps[0], tile[14]).then_inc(b_ynT.handle, 1)
                slot(17)
                pe.wait_ge(b_z.handle, b_z.at(b))
                for j in range(TB):
                    ins = product(ps[2][:, col(j)], [(tile[16][:, col(j)], w0("WoT", C))])
                ins.then_inc(b_o.handle, 1)
                slot(18)
                slot(19)
                pe.wait_ge(norm_out["ffn0"].handle, norm_out["ffn0"].at(b))
                transposes(ps[1], tile[17]).then_inc(b_xT.handle, 1)
                pe.wait_ge(b_xf.handle, b_xf.at(b))
                if first:
                    pe.wait_ge(later_in.handle, ALL_LATER)
                for j in range(TB):
                    ins = product(ps[3][:, col(j, NE)], [(tile[21][:, col(j)], WD0[:, m0["router"] - m0["d"]:])])
                ins.then_inc(b_logits.handle, 1)
                slot(20)
                slot(21)

            first_moe = pe_experts("c", NE + 1, WD0, m0, "g", "u", SPLIT0, b_xlow)
            b_steps(pe, pe_b, first_moe)

            def pe_d(b, a, first, slot):
                def slots(n, end):
                    for k in range(n, end):
                        slot(k)

                def k_r(n):
                    m, c = divmod(n, UC)
                    if c == 0:
                        pe.wait_ge(d_mix.handle, d_mix.at(b, 1 + 2 * m))
                    if n >= 2:
                        pe.wait_ge(d_act.handle, d_act.at(b, n - 1))
                    if n == 1 and a is not None:
                        pe.wait_ge(d_silu.handle, d_silu.at(a))
                    product(ps[KR[n % 2]][:], [(w1(("Wk", "Wr")[m], P, P * c), tile[4 + 2 * m][:])]).then_inc(d_kr.handle, 1)

                def v_of(c):
                    if c == 0:
                        pe.wait_ge(d_mix.handle, d_mix.at(b, 2))
                    else:
                        pe.wait_ge(d_kv.handle, d_kv.at(b, c))
                    product(ps[2][:], [(w1("Wv", P, P * c), tile[5][:])]).then_inc(d_v.handle, 1)

                def post_transposes():
                    pe.wait_ge(norm_out["post"].handle, norm_out["post"].at(a))
                    transposes(ps[0], CN).then_inc(d_x2T.handle, 1)

                def pre_transposes():
                    pe.wait_ge(norm_out["pre"].handle, norm_out["pre"].at(b))
                    transposes(ps[1], tile[2]).then_inc(d_xT.handle, 1)

                def channel_hidden():
                    pe.wait_ge(d_mix2.handle, d_mix2.at(a))
                    for c in range(UC):
                        if c >= 2:
                            pe.wait_ge(d_silu.handle, d_silu.at(a, c - 1))
                        product(ps[CM[c % 2]][:], [(w1("cWk", P, P * c), CX[1][:])]).then_inc(d_kk.handle, 1)
                    pe.wait_ge(d_silu.handle, d_silu.at(a, UC - 1))
                    for j in range(TB):
                        ins = product(ps[0][:, col(j)], [(CX[2][:, col(j)], w1("cWr", C))])
                    ins.then_inc(d_sg.handle, 1)

                def channel_output():
                    pe.wait_ge(d_silu.handle, d_silu.at(a))
                    pe.wait_ge(d_sig.handle, d_sig.at(a))
                    for j in range(TB):
                        ins = product(ps[0][:, col(j)], [(tile[18 + c][:, col(j)], w1("cWv", C, C * c)) for c in range(UC)])
                    ins.then_inc(d_o2.handle, 1)

                def ffn1_transposes():
                    pe.wait_ge(norm_out["ffn1"].handle, norm_out["ffn1"].at(a))
                    transposes(ps[0], CN).then_inc(d_x3T.handle, 1)

                def logits():
                    pe.wait_ge(d_xf.handle, d_xf.at(a))
                    for j in range(TB):
                        ins = product(ps[0][:, col(j, NE)], [(CX[0][:, col(j)], WD1[:, m1["router"] - m1["d"]:])])
                    ins.then_inc(d_logits.handle, 1)

                def positions():
                    pe.wait_ge(d_sel.handle, d_sel.at(a))
                    chosen = CHOSEN[:].rearrange("p j e -> p (j e)")
                    pe.matmul(ps[0][:, 0:(TB + 1) * NE], TRI[:], chosen, start=True, stop=False)
                    for shift in range(1, TB + 1):
                        ins = pe.matmul(ps[0][:, shift * NE:(TB + 1) * NE], ONES[:], chosen[:, 0:(TB + 1 - shift) * NE],
                                        start=False, stop=shift == TB)
                    ins.then_inc(d_pos.handle, 1)

                def time_output():
                    pe.wait_ge(d_rw.handle, d_rw.at(b))
                    for j in range(TB):
                        ins = product(ps[2][:, col(j)], [(tile[13 + c][:, col(j)], w1("Wo", C, C * c)) for c in range(UC)])
                    ins.then_inc(d_o.handle, 1)

                slots(0, 4)
                given(a, post_transposes)
                slots(4, 7)
                given(a, channel_hidden)
                slots(7, 9)
                given(b, pre_transposes)
                slot(9)
                given(b, k_r, 0)
                given(b, k_r, 1)
                given(b, k_r, 2)
                given(b, v_of, 0)
                given(b, k_r, 3)
                slot(10)
                given(a, channel_output)
                slot(11)
                given(b, v_of, 1)
                given(b, k_r, 4)
                given(b, k_r, 5)
                slots(12, 14)
                given(b, v_of, 2)
                slot(14)
                given(b, k_r, 6)
                given(b, k_r, 7)
                slot(15)
                given(a, ffn1_transposes)
                slot(16)
                given(b, v_of, 3)
                slot(17)
                given(a, logits)
                slots(18, 20)
                given(a, positions)
                slots(20, 25)
                given(b, time_output)

            d_steps(pe, pe_d, first_moe, pe_experts("e", NE, WD1, m1, "in", "gate", SPLIT0 + SPLIT1, d_xlow))


def kernel(**inputs):
    import numpy as _np
    import concourse.bacc as _bacc
    from concourse import mybir as _mybir
    from concourse.bass_utils import run_bass_kernel_spmd as _run

    i = {k: _np.asarray(a) for k, a in inputs.items()}
    a0 = lambda n: i["L0_attn_" + n]
    f0 = lambda n: i["L0_ffn_" + n]
    a1 = lambda n: i["L1_attn_" + n]
    f1 = lambda n: i["L1_ffn_" + n]

    def rows(w):
        return w.reshape(-1, P, w.shape[1]).transpose(1, 0, 2).reshape(P, -1)

    def side(ws):
        return _np.concatenate(list(ws), axis=1)

    f32 = _np.float32
    steps = _np.arange(P)
    level = _np.stack([((steps[:, None] >> (lv + 1)) == (steps[None] >> (lv + 1)))
                       & ((steps[:, None] >> lv) % 2 == 0) & ((steps[None] >> lv) % 2 == 1) for lv in range(LEVELS)], 1)
    x = a0("x").reshape(B, TB, P, C).transpose(2, 0, 1, 3)
    arrays = {
        "x": x,
        "attn0": side([a0("A"), a0("Bp")[:4].reshape(4 * LR, C), a0("tdA"), a0("Wk").T, a0("Wv").T, a0("Wr").T,
                       a0("Wo").T, a0("Wg1"), a0("Wg2")[:P]]),
        "tdB": a0("tdB"),
        "bp4": a0("Bp")[4],
        "wg2b": a0("Wg2")[P:],
        "moe0": side([f0("sg").T, *(w.T for w in f0("eg")), f0("su").T, *(w.T for w in f0("eu")),
                      rows(f0("sd").T), *(rows(w.T) for w in f0("ed")), f0("router_w").T]),
        "attn1": side([a1("tm_Wk"), a1("tm_Wv"), a1("tm_Wr"), rows(a1("tm_Wo")), a1("cm_Wk"), rows(a1("cm_Wv")),
                       a1("cm_Wr")]),
        "lnrow": _np.broadcast_to(_np.stack([a1("ln0_g"), a1("ln0_b")]), (P, 2, C)),
        "dfvec": _np.stack([a1("tm_decay").reshape(UC, P).T, a1("tm_first").reshape(UC, P).T], 1),
        "vecs": _np.stack([a0("miu_x").reshape(C), *a0("lam").reshape(NS, C), a0("td_miu").reshape(C), a0("u").reshape(C),
                           a0("gamma"), a0("beta"), a1("pre_g"), a1("pre_b"), a1("post_g"), a1("post_b"),
                           a1("tm_mix_k"), a1("tm_mix_v"), a1("tm_mix_r"), a1("cm_mix_k"), a1("cm_mix_r")], 1),
        "moe1": side([*(w[:, :HID] for w in f1("W1")), *(w[:, HID:] for w in f1("W1")), *(rows(w) for w in f1("W2")),
                      f1("Wg").T]),
        "ident": _np.eye(P, dtype=f32),
        "levels": _np.stack([level[:, lv][:, (steps >> lv) % 2 == 1] for lv in range(LEVELS)], 1).astype(_np.int32),
        "tri": _np.triu(_np.ones((P, P), f32), 1),
        "iota": _np.broadcast_to(_np.arange(NE, dtype=f32), (P, 1, NE)),
        "hsel": (_np.arange(P)[:, None] // HEAD == _np.arange(NH)[None]).astype(f32),
    }
    nc = _bacc.Bacc("TRN2", target_bir_lowering=False, num_devices=1)
    arrays = {f"in_{k}": _np.ascontiguousarray(a) for k, a in arrays.items()}
    args = [nc.dram_tensor(k, a.shape, _mybir.dt.from_np(a.dtype), kind="ExternalInput").ap() for k, a in arrays.items()]
    args.append(nc.dram_tensor("out_0", (B, P, TB, C), F32, kind="ExternalOutput").ap())
    build(nc, *args)
    r = _run(nc, [arrays], core_ids=[0])
    return r.results[0]["out_0"].transpose(0, 2, 1, 3).reshape(B, T, C)
```
